# Optimizing a Trainium2 kernel written in Bass

```python
import numpy as np
import jax
import jax.numpy as jnp

def _softmax(x, axis=-1):
    return jax.nn.softmax(x, axis=axis)

def _gelu(x):
    return jax.nn.gelu(x, approximate=True)

def _silu(x):
    return jax.nn.silu(x)

def _sigmoid(x):
    return jax.nn.sigmoid(x)

def _layernorm(x, axis=-1, eps=1e-05):
    m = jnp.mean(x, axis=axis, keepdims=True)
    v = jnp.var(x, axis=axis, keepdims=True)
    return (x - m) / jnp.sqrt(v + eps)

def _scatter_add(tgt, idx, src, axis=0):
    return tgt.at[idx].add(src)

def _segment_sum(src, seg, n):
    return jax.ops.segment_sum(src, seg, n)
kernel_name = 'mk_vit_tower_postln_d4_tok_img1024_r4_96e94b'

def setup_inputs(seed: int=0):
    np.random.seed(seed)
    _w = jnp.asarray

    def _rec_inputs():
        import jax
        import jax.numpy as jnp
        _rk = jax.random.key(seed)
        x = -0.000169711 + 1.00022 * jax.random.normal(jax.random.fold_in(_rk, 1), (64, 3, 96, 96), jnp.float32)
        return x
    x = _rec_inputs()

    def _L0_tok_setup():
        import jax, jax.numpy as jnp
        import numpy as np
        C = 256
        H8 = 8
        DH = C // H8
        PS = 14
        CS = 3
        IMG = 168
        B = 4

        def _ln(x, g, b):
            mu = jnp.mean(x, axis=-1, keepdims=True)
            xc = x - mu
            var = jnp.mean(xc * xc, axis=-1, keepdims=True)
            return xc * jax.lax.rsqrt(var + 1e-05) * g + b

        def _forward(pixel_values, conv_w, class_emb, la_ln_q_g, la_ln_q_b, la_wq, la_ln_kv_g, la_ln_kv_b, la_wkv, la_proj_w, la_proj_b, ga_ln_q_g, ga_ln_q_b, ga_wq, ga_ln_kv_g, ga_ln_kv_b, ga_wkv, ga_proj_w, ga_proj_b, mod_w, mod_b):
            b = pixel_values.shape[0]
            pe = jax.lax.conv_general_dilated(pixel_values, conv_w, (PS, PS), 'VALID', dimension_numbers=('NCHW', 'OIHW', 'NCHW'))
            HP = pe.shape[2]
            h = HP // CS
            hw, N = (h * h, CS * CS)
            scale = C ** (-0.5)
            grid = pe.reshape(b, C, h, CS, h, CS)
            red = grid.mean(axis=(3, 5)).reshape(b, C, hw).transpose(0, 2, 1)
            win = grid.transpose(0, 2, 4, 3, 5, 1).reshape(b, hw, N, C)
            q = _ln(red, la_ln_q_g, la_ln_q_b) @ la_wq
            q = q.reshape(b, hw, H8, DH).transpose(0, 2, 1, 3)
            kv = _ln(win, la_ln_kv_g, la_ln_kv_b) @ la_wkv
            kv = kv.reshape(b, hw, N, 2, H8, DH).transpose(3, 0, 4, 1, 2, 5)
            k_, v_ = (kv[0], kv[1])
            attn = jax.nn.softmax(jnp.einsum('bhnd,bhnkd->bhnk', q * scale, k_), axis=-1)
            agg = jnp.einsum('bhnk,bhnkd->bhnd', attn, v_)
            agg = agg.transpose(0, 2, 1, 3).reshape(b, hw, C)
            local_out = red + agg @ la_proj_w + la_proj_b
            cls = jnp.broadcast_to(class_emb, (b, 1, C))
            gq = (_ln(cls, ga_ln_q_g, ga_ln_q_b) @ ga_wq).reshape(b, H8, DH)
            gkv = _ln(local_out, ga_ln_kv_g, ga_ln_kv_b) @ ga_wkv
            gkv = gkv.reshape(b, hw, 2, H8, DH).transpose(2, 0, 3, 1, 4)
            gk, gv = (gkv[0], gkv[1])
            gattn = jax.nn.softmax(jnp.einsum('bhd,bhnd->bhn', gq * scale, gk), axis=-1)
            gagg = jnp.einsum('bhn,bhnd->bhd', gattn, gv).reshape(b, 1, C)
            cls_out = cls + gagg @ ga_proj_w + ga_proj_b
            patch_out = local_out @ mod_w + mod_b
            return jnp.concatenate([patch_out, cls_out], axis=1)
        key = jax.random.key(seed)
        ks = jax.random.split(key, 16)
        nrm = lambda k, shape: jax.random.normal(k, shape, jnp.float32) * 0.02
        return {'pixel_values': jax.random.normal(ks[0], (B, 3, IMG, IMG), jnp.float32), 'pixel_masks': jnp.ones((B, 1, IMG, IMG), jnp.float32), 'conv_w': nrm(ks[1], (C, 3, PS, PS)), 'class_emb': nrm(ks[2], (C,)), 'la_ln_q_g': jnp.ones((C,)), 'la_ln_q_b': jnp.zeros((C,)), 'la_wq': nrm(ks[3], (C, C)), 'la_ln_kv_g': jnp.ones((C,)), 'la_ln_kv_b': jnp.zeros((C,)), 'la_wkv': nrm(ks[4], (C, 2 * C)), 'la_proj_w': nrm(ks[5], (C, C)), 'la_proj_b': jnp.zeros((C,)), 'ga_ln_q_g': jnp.ones((C,)), 'ga_ln_q_b': jnp.zeros((C,)), 'ga_wq': nrm(ks[6], (C, C)), 'ga_ln_kv_g': jnp.ones((C,)), 'ga_ln_kv_b': jnp.zeros((C,)), 'ga_wkv': nrm(ks[7], (C, 2 * C)), 'ga_proj_w': nrm(ks[8], (C, C)), 'ga_proj_b': jnp.zeros((C,)), 'mod_w': nrm(ks[9], (C, C)), 'mod_b': jnp.zeros((C,))}
    _L0_tok_all = _L0_tok_setup()
    _L0_tok_in = {k: v for k, v in _L0_tok_all.items() if k in ('pixel_masks', 'conv_w', 'class_emb', 'la_ln_q_g', 'la_ln_q_b', 'la_wq', 'la_ln_kv_g', 'la_ln_kv_b', 'la_wkv', 'la_proj_w', 'la_proj_b', 'ga_ln_q_g', 'ga_ln_q_b', 'ga_wq', 'ga_ln_kv_g', 'ga_ln_kv_b', 'ga_wkv', 'ga_proj_w', 'ga_proj_b', 'mod_w', 'mod_b')}
    del _L0_tok_all

    def _L0_attn_setup():
        import jax, jax.numpy as jnp
        import numpy as np
        D_MODEL = 256
        D_STATE = 16
        EXPAND = 2
        D_INNER = D_MODEL * EXPAND
        DT_RANK = (D_MODEL + 15) // 16
        BATCH = 2
        SEQ = 256

        def _s6_forward(x, W_in, W_conv, W_x, W_dt, b_dt, A_log, D_param, W_out):
            B, L, _ = x.shape
            u, res = jnp.split(x @ W_in, 2, axis=-1)
            up = jnp.pad(u, ((0, 0), (2, 0), (0, 0)))
            u = up[:, :L] * W_conv[:, 0] + up[:, 1:L + 1] * W_conv[:, 1] + up[:, 2:L + 2] * W_conv[:, 2]
            u = jax.nn.silu(u)
            x_dbl = u @ W_x
            dt, Bm, Cm = jnp.split(x_dbl, [DT_RANK, DT_RANK + D_STATE], axis=-1)
            delta = jax.nn.softplus(dt @ W_dt + b_dt)
            A = -jnp.exp(A_log)
            deltaA = jnp.exp(jnp.einsum('bld,dn->bldn', delta, A))
            deltaB_u = jnp.einsum('bld,bln->bldn', delta * u, Bm)

            def step(h, inp):
                dA, dbu, c = inp
                h = dA * h + dbu
                y = jnp.einsum('bdn,bn->bd', h, c)
                return (h, y)
            h0 = jnp.zeros((B, D_INNER, D_STATE), dtype=u.dtype)
            _, ys = jax.lax.scan(step, h0, (jnp.moveaxis(deltaA, 1, 0), jnp.moveaxis(deltaB_u, 1, 0), jnp.moveaxis(Cm, 1, 0)))
            y = jnp.moveaxis(ys, 0, 1)
            y = y + u * D_param
            y = y * jax.nn.silu(res)
            return y @ W_out
        key = jax.random.key(seed)
        ks = jax.random.split(key, 8)

        def nrm(k, shape, scale):
            return jax.random.normal(k, shape, dtype=jnp.float32) * scale
        x = jax.random.normal(ks[0], (BATCH, SEQ, D_MODEL), dtype=jnp.float32)
        W_in = nrm(ks[1], (D_MODEL, 2 * D_INNER), D_MODEL ** (-0.5))
        W_conv = nrm(ks[2], (D_INNER, 3), 3 ** (-0.5))
        W_x = nrm(ks[3], (D_INNER, DT_RANK + 2 * D_STATE), D_INNER ** (-0.5))
        W_dt = nrm(ks[4], (DT_RANK, D_INNER), DT_RANK ** (-0.5))
        b_dt = nrm(ks[5], (D_INNER,), 0.1)
        A_log = jnp.log(jnp.tile(jnp.arange(1, D_STATE + 1, dtype=jnp.float32), (D_INNER, 1)))
        D_param = jnp.ones((D_INNER,), dtype=jnp.float32)
        W_out = nrm(ks[6], (D_INNER, D_MODEL), D_INNER ** (-0.5))
        return {'x': x, 'W_in': W_in, 'W_conv': W_conv, 'W_x': W_x, 'W_dt': W_dt, 'b_dt': b_dt, 'A_log': A_log, 'D_param': D_param, 'W_out': W_out}
    _L0_attn_all = _L0_attn_setup()
    _L0_attn_in = {k: v for k, v in _L0_attn_all.items() if k in ('W_in', 'W_conv', 'W_x', 'W_dt', 'b_dt', 'A_log', 'D_param', 'W_out')}
    del _L0_attn_all

    def _L0_ffn_setup():
        import jax, jax.numpy as jnp
        import numpy as np
        DIM = 256
        NUM_EXPERTS = 8
        TOP_K = 2
        HIDDEN = int(DIM * 1.5)
        key = jax.random.key(seed)
        k_x, k_r, k_w1, k_w2, k_w3 = jax.random.split(key, 5)
        B, T = (2, 1024)
        s_in = 1.0 / np.sqrt(DIM)
        s_h = 1.0 / np.sqrt(HIDDEN)
        return {'x': jax.random.normal(k_x, (B, T, DIM), dtype=jnp.float32), 'Wr': jax.random.uniform(k_r, (DIM, NUM_EXPERTS), minval=-s_in, maxval=s_in, dtype=jnp.float32), 'W1': jax.random.uniform(k_w1, (NUM_EXPERTS, DIM, HIDDEN), minval=-s_in, maxval=s_in, dtype=jnp.float32), 'W2': jax.random.uniform(k_w2, (NUM_EXPERTS, HIDDEN, DIM), minval=-s_h, maxval=s_h, dtype=jnp.float32), 'W3': jax.random.uniform(k_w3, (NUM_EXPERTS, DIM, HIDDEN), minval=-s_in, maxval=s_in, dtype=jnp.float32)}
    _L0_ffn_all = _L0_ffn_setup()
    _L0_ffn_in = {k: v for k, v in _L0_ffn_all.items() if k in ('Wr', 'W1', 'W2', 'W3')}
    del _L0_ffn_all

    def _L1_attn_setup():
        import jax, jax.numpy as jnp
        import numpy as np
        B, S, D = (2, 512, 256)
        H = 16
        HD = D // H
        THETA = 1000.0
        SCALE = 0.02

        def _rope(t, cos, sin):
            even = t[..., ::2]
            odd = t[..., 1::2]
            return jnp.concatenate([even * cos - odd * sin, odd * cos + even * sin], axis=-1)
        key = jax.random.key(seed)
        k0, k1, k2, k3, k4 = jax.random.split(key, 5)
        x = jax.random.normal(k0, (B, S, D), dtype=jnp.float32)
        wq = SCALE * jax.random.normal(k1, (D, D), dtype=jnp.float32)
        wk = SCALE * jax.random.normal(k2, (D, HD), dtype=jnp.float32)
        wv = SCALE * jax.random.normal(k3, (D, HD), dtype=jnp.float32)
        wo = SCALE * jax.random.normal(k4, (D, D), dtype=jnp.float32)
        return {'x': x, 'wq': wq, 'wk': wk, 'wv': wv, 'wo': wo}
    _L1_attn_all = _L1_attn_setup()
    _L1_attn_in = {k: v for k, v in _L1_attn_all.items() if k in ('wq', 'wk', 'wv', 'wo')}
    del _L1_attn_all

    def _L1_ffn_setup():
        import jax, jax.numpy as jnp
        import numpy as np
        IN_F = 256
        OUT_F = 256
        B, S = (8, 1024)

        def _pack_ternary(tern):
            enc = (tern + 1.0).astype(jnp.int32).reshape(-1)
            return (enc[0::4] | enc[1::4] << 2 | enc[2::4] << 4 | enc[3::4] << 6).astype(jnp.int32)
        key = jax.random.key(seed)
        kx, kw = jax.random.split(key)
        x = jax.random.normal(kx, (B, S, IN_F), dtype=jnp.float32)
        w = jax.random.normal(kw, (OUT_F, IN_F), dtype=jnp.float32) * 0.02
        scale = jnp.maximum(jnp.mean(jnp.abs(w)), 1e-05)
        wn = w / scale
        tern = jnp.sign(wn) * (jnp.abs(wn) > 0.5).astype(jnp.float32)
        packed = _pack_ternary(tern)
        bias = jnp.zeros((OUT_F,), dtype=jnp.float32)
        return {'x': x, 'packed_weight': packed, 'weight_scale': scale.reshape(1), 'bias': bias}
    _L1_ffn_all = _L1_ffn_setup()
    _L1_ffn_in = {k: v for k, v in _L1_ffn_all.items() if k in ('packed_weight', 'weight_scale', 'bias')}
    del _L1_ffn_all

    def _L2_attn_setup():
        import jax, jax.numpy as jnp
        import numpy as np
        HEADS = 16
        HEAD_DIM = 64
        EMB = 256
        B, S = (4, 512)
        SCALE = 1.0 / 8.0
        MASK_PENALTY = -50.0
        key = jax.random.key(seed)
        ks = jax.random.split(key, 5)
        x = jax.random.normal(ks[0], (B, S, EMB), dtype=jnp.float32)
        Wq = jax.random.normal(ks[1], (EMB, HEADS * HEAD_DIM), dtype=jnp.float32) * 0.02
        Wk = jax.random.normal(ks[2], (EMB, HEADS * HEAD_DIM), dtype=jnp.float32) * 0.02
        Wv = jax.random.normal(ks[3], (EMB, HEADS * HEAD_DIM), dtype=jnp.float32) * 0.02
        Wr = jax.random.normal(ks[4], (HEADS * HEAD_DIM, EMB), dtype=jnp.float32) * 0.02
        return {'x': x, 'Wq': Wq, 'Wk': Wk, 'Wv': Wv, 'Wr': Wr}
    _L2_attn_all = _L2_attn_setup()
    _L2_attn_in = {k: v for k, v in _L2_attn_all.items() if k in ('Wq', 'Wk', 'Wv', 'Wr')}
    del _L2_attn_all

    def _L2_ffn_setup():
        import jax, jax.numpy as jnp
        import numpy as np
        B, S, DIM = (4, 1024, 256)
        BASE_COUPLING = 0.1
        NUM_CYCLES = 3

        def _gelu(x):
            return jax.nn.gelu(x, approximate=False)

        def _coupling_net(h, w1, b1, w2, b2, w3, b3, w4, b4):
            h = _gelu(h @ w1 + b1)
            h = _gelu(h @ w2 + b2)
            h = _gelu(h @ w3 + b3)
            return jax.nn.sigmoid(h @ w4 + b4)

        def _global_net(h, w1, b1, w2, b2, w3, b3):
            h = _gelu(h @ w1 + b1)
            h = _gelu(h @ w2 + b2)
            return jax.nn.sigmoid(h @ w3 + b3)

        def _twist(x):
            o_r, o_i, p_r, p_i = jnp.split(x, 4, axis=-1)
            return jnp.concatenate([p_r, -p_i, -o_r, o_i], axis=-1)
        key = jax.random.key(seed)
        ks = jax.random.split(key, 9)
        d = DIM

        def w(k, fan_in, fan_out):
            return jax.random.normal(k, (fan_in, fan_out), dtype=jnp.float32) / np.sqrt(fan_in).astype(np.float32)
        inp = {'x': jax.random.normal(ks[0], (B, S, d), dtype=jnp.float32)}
        cn_dims = [(d, d), (d, d // 2), (d // 2, d // 4), (d // 4, 1)]
        for i, (a, b) in enumerate(cn_dims):
            inp[f'cn_w{i + 1}'] = w(ks[1 + i], a, b)
            inp[f'cn_b{i + 1}'] = jnp.zeros((b,), dtype=jnp.float32)
        gc_dims = [(d, d // 2), (d // 2, d // 4), (d // 4, 1)]
        for i, (a, b) in enumerate(gc_dims):
            inp[f'gc_w{i + 1}'] = w(ks[5 + i], a, b)
            inp[f'gc_b{i + 1}'] = jnp.zeros((b,), dtype=jnp.float32)
        inp['adaptive_range'] = jnp.full((1,), 0.2, dtype=jnp.float32)
        return inp
    _L2_ffn_all = _L2_ffn_setup()
    _L2_ffn_in = {k: v for k, v in _L2_ffn_all.items() if k in ('cn_w1', 'cn_b1', 'cn_w2', 'cn_b2', 'cn_w3', 'cn_b3', 'cn_w4', 'cn_b4', 'gc_w1', 'gc_b1', 'gc_w2', 'gc_b2', 'gc_w3', 'gc_b3', 'adaptive_range')}
    del _L2_ffn_all

    def _L3_attn_setup():
        import jax, jax.numpy as jnp
        import numpy as np
        HEADS = 4
        EPS = 1e-05
        GATE_LOGIT_NORMALIZER = 16.0
        B, N, D = (4, 512, 256)
        DK, DV, R = (256, 512, 16)

        def _gla_scan(q, k, v, gk):
            dk, dv = (q.shape[1], v.shape[1])

            def step(S, inp):
                q_t, k_t, v_t, g_t = inp
                S = S * jnp.exp(g_t)[:, None] + k_t[:, None] * v_t[None, :]
                return (S, q_t @ S)
            S0 = jnp.zeros((dk, dv), q.dtype)
            _, o = jax.lax.scan(step, S0, (q, k, v, gk))
            return o
        key = jax.random.key(seed)
        ks = jax.random.split(key, 10)
        s = 0.02
        return {'x': jax.random.normal(ks[0], (B, N, D), jnp.float32), 'Wq': jax.random.normal(ks[1], (D, DK), jnp.float32) * s, 'Wk': jax.random.normal(ks[2], (D, DK), jnp.float32) * s, 'Wv': jax.random.normal(ks[3], (D, DV), jnp.float32) * s, 'Wg': jax.random.normal(ks[4], (D, DV), jnp.float32) * s, 'Wgk1': jax.random.normal(ks[5], (D, R), jnp.float32) * s, 'Wgk2': jax.random.normal(ks[6], (R, DK), jnp.float32) * s, 'bgk2': jnp.zeros((DK,), jnp.float32), 'Wo': jax.random.normal(ks[7], (DV, D), jnp.float32) * s, 'g_norm_weight': jnp.ones((DV // HEADS,), jnp.float32)}
    _L3_attn_all = _L3_attn_setup()
    _L3_attn_in = {k: v for k, v in _L3_attn_all.items() if k in ('Wq', 'Wk', 'Wv', 'Wg', 'Wgk1', 'Wgk2', 'bgk2', 'Wo', 'g_norm_weight')}
    del _L3_attn_all

    def _L3_ffn_setup():
        import jax, jax.numpy as jnp
        import numpy as np
        D_IN, D_HID = (256, 1024)

        def _ternary(key, shape):
            return jax.random.randint(key, shape, -1, 2).astype(jnp.float32)

        def _tlin(x, w, s):
            return jnp.einsum('bsi,oi->bso', x, w) * s
        key = jax.random.key(seed)
        ks = jax.random.split(key, 12)
        inv = lambda fan: 1.0 / np.sqrt(fan).astype(np.float32)
        return {'x': jax.random.normal(ks[0], (4, 512, D_IN), dtype=jnp.float32), 'w1_w': _ternary(ks[1], (D_HID, D_IN)), 'w1_s': jax.random.uniform(ks[2], (D_HID,), dtype=jnp.float32) * inv(D_IN), 'w2_w': _ternary(ks[3], (D_HID, D_IN)), 'w2_s': jax.random.uniform(ks[4], (D_HID,), dtype=jnp.float32) * inv(D_IN), 'h1_w': _ternary(ks[5], (D_HID, D_HID)), 'h1_s': jax.random.uniform(ks[6], (D_HID,), dtype=jnp.float32) * inv(D_HID), 'h2_w': _ternary(ks[7], (D_HID, D_HID)), 'h2_s': jax.random.uniform(ks[8], (D_HID,), dtype=jnp.float32) * inv(D_HID), 'w3_w': _ternary(ks[9], (D_IN, D_HID)), 'w3_s': jax.random.uniform(ks[10], (D_IN,), dtype=jnp.float32) * inv(D_HID)}
    _L3_ffn_all = _L3_ffn_setup()
    _L3_ffn_in = {k: v for k, v in _L3_ffn_all.items() if k in ('w1_w', 'w1_s', 'w2_w', 'w2_s', 'h1_w', 'h1_s', 'h2_w', 'h2_s', 'w3_w', 'w3_s')}
    del _L3_ffn_all
    return {'x': x, 'L0_tok_pixel_masks': _L0_tok_in['pixel_masks'], 'L0_tok_conv_w': _L0_tok_in['conv_w'], 'L0_tok_class_emb': _L0_tok_in['class_emb'], 'L0_tok_la_ln_q_g': _L0_tok_in['la_ln_q_g'], 'L0_tok_la_ln_q_b': _L0_tok_in['la_ln_q_b'], 'L0_tok_la_wq': _L0_tok_in['la_wq'], 'L0_tok_la_ln_kv_g': _L0_tok_in['la_ln_kv_g'], 'L0_tok_la_ln_kv_b': _L0_tok_in['la_ln_kv_b'], 'L0_tok_la_wkv': _L0_tok_in['la_wkv'], 'L0_tok_la_proj_w': _L0_tok_in['la_proj_w'], 'L0_tok_la_proj_b': _L0_tok_in['la_proj_b'], 'L0_tok_ga_ln_q_g': _L0_tok_in['ga_ln_q_g'], 'L0_tok_ga_ln_q_b': _L0_tok_in['ga_ln_q_b'], 'L0_tok_ga_wq': _L0_tok_in['ga_wq'], 'L0_tok_ga_ln_kv_g': _L0_tok_in['ga_ln_kv_g'], 'L0_tok_ga_ln_kv_b': _L0_tok_in['ga_ln_kv_b'], 'L0_tok_ga_wkv': _L0_tok_in['ga_wkv'], 'L0_tok_ga_proj_w': _L0_tok_in['ga_proj_w'], 'L0_tok_ga_proj_b': _L0_tok_in['ga_proj_b'], 'L0_tok_mod_w': _L0_tok_in['mod_w'], 'L0_tok_mod_b': _L0_tok_in['mod_b'], 'L0_attn_W_in': _L0_attn_in['W_in'], 'L0_attn_W_conv': _L0_attn_in['W_conv'], 'L0_attn_W_x': _L0_attn_in['W_x'], 'L0_attn_W_dt': _L0_attn_in['W_dt'], 'L0_attn_b_dt': _L0_attn_in['b_dt'], 'L0_attn_A_log': _L0_attn_in['A_log'], 'L0_attn_D_param': _L0_attn_in['D_param'], 'L0_attn_W_out': _L0_attn_in['W_out'], 'L0_ffn_Wr': _L0_ffn_in['Wr'], 'L0_ffn_W1': _L0_ffn_in['W1'], 'L0_ffn_W2': _L0_ffn_in['W2'], 'L0_ffn_W3': _L0_ffn_in['W3'], 'L1_attn_wq': _L1_attn_in['wq'], 'L1_attn_wk': _L1_attn_in['wk'], 'L1_attn_wv': _L1_attn_in['wv'], 'L1_attn_wo': _L1_attn_in['wo'], 'L1_ffn_packed_weight': _L1_ffn_in['packed_weight'], 'L1_ffn_weight_scale': _L1_ffn_in['weight_scale'], 'L1_ffn_bias': _L1_ffn_in['bias'], 'L2_attn_Wq': _L2_attn_in['Wq'], 'L2_attn_Wk': _L2_attn_in['Wk'], 'L2_attn_Wv': _L2_attn_in['Wv'], 'L2_attn_Wr': _L2_attn_in['Wr'], 'L2_ffn_cn_w1': _L2_ffn_in['cn_w1'], 'L2_ffn_cn_b1': _L2_ffn_in['cn_b1'], 'L2_ffn_cn_w2': _L2_ffn_in['cn_w2'], 'L2_ffn_cn_b2': _L2_ffn_in['cn_b2'], 'L2_ffn_cn_w3': _L2_ffn_in['cn_w3'], 'L2_ffn_cn_b3': _L2_ffn_in['cn_b3'], 'L2_ffn_cn_w4': _L2_ffn_in['cn_w4'], 'L2_ffn_cn_b4': _L2_ffn_in['cn_b4'], 'L2_ffn_gc_w1': _L2_ffn_in['gc_w1'], 'L2_ffn_gc_b1': _L2_ffn_in['gc_b1'], 'L2_ffn_gc_w2': _L2_ffn_in['gc_w2'], 'L2_ffn_gc_b2': _L2_ffn_in['gc_b2'], 'L2_ffn_gc_w3': _L2_ffn_in['gc_w3'], 'L2_ffn_gc_b3': _L2_ffn_in['gc_b3'], 'L2_ffn_adaptive_range': _L2_ffn_in['adaptive_range'], 'L3_attn_Wq': _L3_attn_in['Wq'], 'L3_attn_Wk': _L3_attn_in['Wk'], 'L3_attn_Wv': _L3_attn_in['Wv'], 'L3_attn_Wg': _L3_attn_in['Wg'], 'L3_attn_Wgk1': _L3_attn_in['Wgk1'], 'L3_attn_Wgk2': _L3_attn_in['Wgk2'], 'L3_attn_bgk2': _L3_attn_in['bgk2'], 'L3_attn_Wo': _L3_attn_in['Wo'], 'L3_attn_g_norm_weight': _L3_attn_in['g_norm_weight'], 'L3_ffn_w1_w': _L3_ffn_in['w1_w'], 'L3_ffn_w1_s': _L3_ffn_in['w1_s'], 'L3_ffn_w2_w': _L3_ffn_in['w2_w'], 'L3_ffn_w2_s': _L3_ffn_in['w2_s'], 'L3_ffn_h1_w': _L3_ffn_in['h1_w'], 'L3_ffn_h1_s': _L3_ffn_in['h1_s'], 'L3_ffn_h2_w': _L3_ffn_in['h2_w'], 'L3_ffn_h2_s': _L3_ffn_in['h2_s'], 'L3_ffn_w3_w': _L3_ffn_in['w3_w'], 'L3_ffn_w3_s': _L3_ffn_in['w3_s']}

def reference(x, L0_tok_pixel_masks, L0_tok_conv_w, L0_tok_class_emb, L0_tok_la_ln_q_g, L0_tok_la_ln_q_b, L0_tok_la_wq, L0_tok_la_ln_kv_g, L0_tok_la_ln_kv_b, L0_tok_la_wkv, L0_tok_la_proj_w, L0_tok_la_proj_b, L0_tok_ga_ln_q_g, L0_tok_ga_ln_q_b, L0_tok_ga_wq, L0_tok_ga_ln_kv_g, L0_tok_ga_ln_kv_b, L0_tok_ga_wkv, L0_tok_ga_proj_w, L0_tok_ga_proj_b, L0_tok_mod_w, L0_tok_mod_b, L0_attn_W_in, L0_attn_W_conv, L0_attn_W_x, L0_attn_W_dt, L0_attn_b_dt, L0_attn_A_log, L0_attn_D_param, L0_attn_W_out, L0_ffn_Wr, L0_ffn_W1, L0_ffn_W2, L0_ffn_W3, L1_attn_wq, L1_attn_wk, L1_attn_wv, L1_attn_wo, L1_ffn_packed_weight, L1_ffn_weight_scale, L1_ffn_bias, L2_attn_Wq, L2_attn_Wk, L2_attn_Wv, L2_attn_Wr, L2_ffn_cn_w1, L2_ffn_cn_b1, L2_ffn_cn_w2, L2_ffn_cn_b2, L2_ffn_cn_w3, L2_ffn_cn_b3, L2_ffn_cn_w4, L2_ffn_cn_b4, L2_ffn_gc_w1, L2_ffn_gc_b1, L2_ffn_gc_w2, L2_ffn_gc_b2, L2_ffn_gc_w3, L2_ffn_gc_b3, L2_ffn_adaptive_range, L3_attn_Wq, L3_attn_Wk, L3_attn_Wv, L3_attn_Wg, L3_attn_Wgk1, L3_attn_Wgk2, L3_attn_bgk2, L3_attn_Wo, L3_attn_g_norm_weight, L3_ffn_w1_w, L3_ffn_w1_s, L3_ffn_w2_w, L3_ffn_w2_s, L3_ffn_h1_w, L3_ffn_h1_s, L3_ffn_h2_w, L3_ffn_h2_s, L3_ffn_w3_w, L3_ffn_w3_s):
    import jax
    import jax.numpy as jnp

    def _L0_tok_ref(pixel_values, pixel_masks, conv_w, class_emb, la_ln_q_g, la_ln_q_b, la_wq, la_ln_kv_g, la_ln_kv_b, la_wkv, la_proj_w, la_proj_b, ga_ln_q_g, ga_ln_q_b, ga_wq, ga_ln_kv_g, ga_ln_kv_b, ga_wkv, ga_proj_w, ga_proj_b, mod_w, mod_b):
        import jax, jax.numpy as jnp
        import numpy as np
        C = 256
        H8 = 8
        DH = C // H8
        PS = 14
        CS = 3
        IMG = 168
        B = 4

        def _ln(x, g, b):
            mu = jnp.mean(x, axis=-1, keepdims=True)
            xc = x - mu
            var = jnp.mean(xc * xc, axis=-1, keepdims=True)
            return xc * jax.lax.rsqrt(var + 1e-05) * g + b

        def _forward(pixel_values, conv_w, class_emb, la_ln_q_g, la_ln_q_b, la_wq, la_ln_kv_g, la_ln_kv_b, la_wkv, la_proj_w, la_proj_b, ga_ln_q_g, ga_ln_q_b, ga_wq, ga_ln_kv_g, ga_ln_kv_b, ga_wkv, ga_proj_w, ga_proj_b, mod_w, mod_b):
            b = pixel_values.shape[0]
            pe = jax.lax.conv_general_dilated(pixel_values, conv_w, (PS, PS), 'VALID', dimension_numbers=('NCHW', 'OIHW', 'NCHW'))
            HP = pe.shape[2]
            h = HP // CS
            hw, N = (h * h, CS * CS)
            scale = C ** (-0.5)
            grid = pe.reshape(b, C, h, CS, h, CS)
            red = grid.mean(axis=(3, 5)).reshape(b, C, hw).transpose(0, 2, 1)
            win = grid.transpose(0, 2, 4, 3, 5, 1).reshape(b, hw, N, C)
            q = _ln(red, la_ln_q_g, la_ln_q_b) @ la_wq
            q = q.reshape(b, hw, H8, DH).transpose(0, 2, 1, 3)
            kv = _ln(win, la_ln_kv_g, la_ln_kv_b) @ la_wkv
            kv = kv.reshape(b, hw, N, 2, H8, DH).transpose(3, 0, 4, 1, 2, 5)
            k_, v_ = (kv[0], kv[1])
            attn = jax.nn.softmax(jnp.einsum('bhnd,bhnkd->bhnk', q * scale, k_), axis=-1)
            agg = jnp.einsum('bhnk,bhnkd->bhnd', attn, v_)
            agg = agg.transpose(0, 2, 1, 3).reshape(b, hw, C)
            local_out = red + agg @ la_proj_w + la_proj_b
            cls = jnp.broadcast_to(class_emb, (b, 1, C))
            gq = (_ln(cls, ga_ln_q_g, ga_ln_q_b) @ ga_wq).reshape(b, H8, DH)
            gkv = _ln(local_out, ga_ln_kv_g, ga_ln_kv_b) @ ga_wkv
            gkv = gkv.reshape(b, hw, 2, H8, DH).transpose(2, 0, 3, 1, 4)
            gk, gv = (gkv[0], gkv[1])
            gattn = jax.nn.softmax(jnp.einsum('bhd,bhnd->bhn', gq * scale, gk), axis=-1)
            gagg = jnp.einsum('bhn,bhnd->bhd', gattn, gv).reshape(b, 1, C)
            cls_out = cls + gagg @ ga_proj_w + ga_proj_b
            patch_out = local_out @ mod_w + mod_b
            return jnp.concatenate([patch_out, cls_out], axis=1)
        del pixel_masks
        return _forward(pixel_values, conv_w, class_emb, la_ln_q_g, la_ln_q_b, la_wq, la_ln_kv_g, la_ln_kv_b, la_wkv, la_proj_w, la_proj_b, ga_ln_q_g, ga_ln_q_b, ga_wq, ga_ln_kv_g, ga_ln_kv_b, ga_wkv, ga_proj_w, ga_proj_b, mod_w, mod_b)

    def _L0_attn_ref(x, W_in, W_conv, W_x, W_dt, b_dt, A_log, D_param, W_out):
        import jax, jax.numpy as jnp
        import numpy as np
        D_MODEL = 256
        D_STATE = 16
        EXPAND = 2
        D_INNER = D_MODEL * EXPAND
        DT_RANK = (D_MODEL + 15) // 16
        BATCH = 2
        SEQ = 256

        def _s6_forward(x, W_in, W_conv, W_x, W_dt, b_dt, A_log, D_param, W_out):
            B, L, _ = x.shape
            u, res = jnp.split(x @ W_in, 2, axis=-1)
            up = jnp.pad(u, ((0, 0), (2, 0), (0, 0)))
            u = up[:, :L] * W_conv[:, 0] + up[:, 1:L + 1] * W_conv[:, 1] + up[:, 2:L + 2] * W_conv[:, 2]
            u = jax.nn.silu(u)
            x_dbl = u @ W_x
            dt, Bm, Cm = jnp.split(x_dbl, [DT_RANK, DT_RANK + D_STATE], axis=-1)
            delta = jax.nn.softplus(dt @ W_dt + b_dt)
            A = -jnp.exp(A_log)
            deltaA = jnp.exp(jnp.einsum('bld,dn->bldn', delta, A))
            deltaB_u = jnp.einsum('bld,bln->bldn', delta * u, Bm)

            def step(h, inp):
                dA, dbu, c = inp
                h = dA * h + dbu
                y = jnp.einsum('bdn,bn->bd', h, c)
                return (h, y)
            h0 = jnp.zeros((B, D_INNER, D_STATE), dtype=u.dtype)
            _, ys = jax.lax.scan(step, h0, (jnp.moveaxis(deltaA, 1, 0), jnp.moveaxis(deltaB_u, 1, 0), jnp.moveaxis(Cm, 1, 0)))
            y = jnp.moveaxis(ys, 0, 1)
            y = y + u * D_param
            y = y * jax.nn.silu(res)
            return y @ W_out
        return _s6_forward(x, W_in, W_conv, W_x, W_dt, b_dt, A_log, D_param, W_out)

    def _L0_ffn_ref(x, Wr, W1, W2, W3):
        import jax, jax.numpy as jnp
        import numpy as np
        DIM = 256
        NUM_EXPERTS = 8
        TOP_K = 2
        HIDDEN = int(DIM * 1.5)
        B, T, C = x.shape
        xf = x.reshape(-1, C)
        gate_logits = xf @ Wr
        w, idx = jax.lax.top_k(gate_logits, TOP_K)
        w = jax.nn.softmax(w, axis=-1)
        comb = jnp.sum(w[:, :, None] * jax.nn.one_hot(idx, NUM_EXPERTS, dtype=w.dtype), axis=1)
        h = jnp.einsum('nc,ech->neh', xf, W1)
        g = jnp.einsum('nc,ech->neh', xf, W3)
        y = jnp.einsum('neh,ehc->nec', jax.nn.silu(h) * g, W2)
        out = jnp.einsum('nec,ne->nc', y, comb)
        return out.reshape(B, T, C)

    def _L1_attn_ref(x, wq, wk, wv, wo):
        import jax, jax.numpy as jnp
        import numpy as np
        B, S, D = (2, 512, 256)
        H = 16
        HD = D // H
        THETA = 1000.0
        SCALE = 0.02

        def _rope(t, cos, sin):
            even = t[..., ::2]
            odd = t[..., 1::2]
            return jnp.concatenate([even * cos - odd * sin, odd * cos + even * sin], axis=-1)
        b, s, d = x.shape
        freqs = 1.0 / THETA ** (jnp.arange(0, HD, 2, dtype=jnp.float32) / HD)
        ang = jnp.arange(s, dtype=jnp.float32)[:, None] * freqs[None, :]
        cos, sin = (jnp.cos(ang), jnp.sin(ang))
        q = (x @ wq.T).reshape(b, s, H, HD).transpose(0, 2, 1, 3)
        k = x @ wk
        v = x @ wv
        q = _rope(q, cos[None, None], sin[None, None])
        k = _rope(k, cos[None], sin[None])
        scores = jnp.einsum('bhqd,bkd->bhqk', q, k) / np.float32(np.sqrt(HD))
        causal = jnp.triu(jnp.ones((s, s), dtype=bool), 1)
        scores = jnp.where(causal[None, None], -jnp.inf, scores)
        w = jax.nn.softmax(scores, axis=-1)
        out = jnp.einsum('bhqk,bkd->bhqd', w, v)
        out = out.transpose(0, 2, 1, 3).reshape(b, s, d)
        return out @ wo.T

    def _L1_ffn_ref(x, packed_weight, weight_scale, bias):
        import jax, jax.numpy as jnp
        import numpy as np
        IN_F = 256
        OUT_F = 256
        B, S = (8, 1024)

        def _pack_ternary(tern):
            enc = (tern + 1.0).astype(jnp.int32).reshape(-1)
            return (enc[0::4] | enc[1::4] << 2 | enc[2::4] << 4 | enc[3::4] << 6).astype(jnp.int32)
        n = OUT_F * IN_F
        shifts = jnp.array([0, 2, 4, 6], dtype=jnp.int32)
        enc = (packed_weight[None, :] >> shifts[:, None] & 3).reshape(-1)[:n]
        w = (enc.astype(jnp.float32) - 1.0).reshape(OUT_F, IN_F) * weight_scale
        act_scale = 127.0 / jnp.maximum(jnp.max(jnp.abs(x), axis=-1, keepdims=True), 1e-05)
        x_dq = jnp.clip(jnp.round(x * act_scale), -128.0, 127.0) / act_scale
        return jnp.einsum('bsi,oi->bso', x_dq, w) + bias

    def _L2_attn_ref(x, Wq, Wk, Wv, Wr):
        import jax, jax.numpy as jnp
        import numpy as np
        HEADS = 16
        HEAD_DIM = 64
        EMB = 256
        B, S = (4, 512)
        SCALE = 1.0 / 8.0
        MASK_PENALTY = -50.0
        b, s, _ = x.shape
        q = (x @ Wq).reshape(b, s, HEADS, HEAD_DIM)
        k = (x @ Wk).reshape(b, s, HEADS, HEAD_DIM)
        v = (x @ Wv).reshape(b, s, HEADS, HEAD_DIM)
        scores = SCALE * jnp.einsum('bqhd,bkhd->bhqk', q, k)
        causal = jnp.triu(jnp.ones((s, s), dtype=x.dtype), k=1)
        scores = scores + MASK_PENALTY * causal
        attn = jax.nn.softmax(scores, axis=-1)
        out = jnp.einsum('bhqk,bkhd->bqhd', attn, v).reshape(b, s, HEADS * HEAD_DIM)
        return out @ Wr

    def _L2_ffn_ref(x, cn_w1, cn_b1, cn_w2, cn_b2, cn_w3, cn_b3, cn_w4, cn_b4, gc_w1, gc_b1, gc_w2, gc_b2, gc_w3, gc_b3, adaptive_range):
        import jax, jax.numpy as jnp
        import numpy as np
        B, S, DIM = (4, 1024, 256)
        BASE_COUPLING = 0.1
        NUM_CYCLES = 3

        def _gelu(x):
            return jax.nn.gelu(x, approximate=False)

        def _coupling_net(h, w1, b1, w2, b2, w3, b3, w4, b4):
            h = _gelu(h @ w1 + b1)
            h = _gelu(h @ w2 + b2)
            h = _gelu(h @ w3 + b3)
            return jax.nn.sigmoid(h @ w4 + b4)

        def _global_net(h, w1, b1, w2, b2, w3, b3):
            h = _gelu(h @ w1 + b1)
            h = _gelu(h @ w2 + b2)
            return jax.nn.sigmoid(h @ w3 + b3)

        def _twist(x):
            o_r, o_i, p_r, p_i = jnp.split(x, 4, axis=-1)
            return jnp.concatenate([p_r, -p_i, -o_r, o_i], axis=-1)
        global_context = x.mean(axis=1, keepdims=True)
        gf = _global_net(global_context, gc_w1, gc_b1, gc_w2, gc_b2, gc_w3, gc_b3)
        out = x
        for _ in range(NUM_CYCLES):
            tf = _coupling_net(out, cn_w1, cn_b1, cn_w2, cn_b2, cn_w3, cn_b3, cn_w4, cn_b4)
            combined = 0.7 * gf + 0.3 * tf
            coupling = BASE_COUPLING + adaptive_range * (combined - 0.5) * 2.0
            out = out + coupling * _twist(out)
        return out

    def _L3_attn_ref(x, Wq, Wk, Wv, Wg, Wgk1, Wgk2, bgk2, Wo, g_norm_weight):
        import jax, jax.numpy as jnp
        import numpy as np
        HEADS = 4
        EPS = 1e-05
        GATE_LOGIT_NORMALIZER = 16.0
        B, N, D = (4, 512, 256)
        DK, DV, R = (256, 512, 16)

        def _gla_scan(q, k, v, gk):
            dk, dv = (q.shape[1], v.shape[1])

            def step(S, inp):
                q_t, k_t, v_t, g_t = inp
                S = S * jnp.exp(g_t)[:, None] + k_t[:, None] * v_t[None, :]
                return (S, q_t @ S)
            S0 = jnp.zeros((dk, dv), q.dtype)
            _, o = jax.lax.scan(step, S0, (q, k, v, gk))
            return o
        b, n, d = x.shape
        h = HEADS
        dk = Wq.shape[1] // h
        dv = Wv.shape[1] // h
        split = lambda t, hd: t.reshape(b, n, h, hd).transpose(0, 2, 1, 3)
        q = split(x @ Wq, dk) * dk ** (-0.5)
        k = split(x @ Wk, dk)
        v = split(x @ Wv, dv)
        gk = jax.nn.log_sigmoid(x @ Wgk1 @ Wgk2 + bgk2) / GATE_LOGIT_NORMALIZER
        gk = split(gk, dk)
        o = jax.vmap(jax.vmap(_gla_scan))(q, k, v, gk)
        o = o.transpose(0, 2, 1, 3)
        g = (x @ Wg).reshape(b, n, h, dv)
        o = o * jax.lax.rsqrt(jnp.mean(o * o, axis=-1, keepdims=True) + EPS) * g_norm_weight
        o = o * (g * jax.nn.sigmoid(g))
        return o.reshape(b, n, h * dv) @ Wo

    def _L3_ffn_ref(x, w1_w, w1_s, w2_w, w2_s, h1_w, h1_s, h2_w, h2_s, w3_w, w3_s):
        import jax, jax.numpy as jnp
        import numpy as np
        D_IN, D_HID = (256, 1024)

        def _ternary(key, shape):
            return jax.random.randint(key, shape, -1, 2).astype(jnp.float32)

        def _tlin(x, w, s):
            return jnp.einsum('bsi,oi->bso', x, w) * s
        h = jax.nn.silu(_tlin(x, w1_w, w1_s)) * _tlin(x, w2_w, w2_s)
        h = jax.nn.gelu(_tlin(h, h1_w, h1_s), approximate=False)
        h = jax.nn.gelu(_tlin(h, h2_w, h2_s), approximate=False)
        return _tlin(h, w3_w, w3_s)
    h = _L0_tok_ref(x, L0_tok_pixel_masks, L0_tok_conv_w, L0_tok_class_emb, L0_tok_la_ln_q_g, L0_tok_la_ln_q_b, L0_tok_la_wq, L0_tok_la_ln_kv_g, L0_tok_la_ln_kv_b, L0_tok_la_wkv, L0_tok_la_proj_w, L0_tok_la_proj_b, L0_tok_ga_ln_q_g, L0_tok_ga_ln_q_b, L0_tok_ga_wq, L0_tok_ga_ln_kv_g, L0_tok_ga_ln_kv_b, L0_tok_ga_wkv, L0_tok_ga_proj_w, L0_tok_ga_proj_b, L0_tok_mod_w, L0_tok_mod_b)
    h = _layernorm(h + _L0_attn_ref(h, L0_attn_W_in, L0_attn_W_conv, L0_attn_W_x, L0_attn_W_dt, L0_attn_b_dt, L0_attn_A_log, L0_attn_D_param, L0_attn_W_out), axis=-1)
    h = _layernorm(h + _L0_ffn_ref(h, L0_ffn_Wr, L0_ffn_W1, L0_ffn_W2, L0_ffn_W3), axis=-1)
    h = _layernorm(h + _L1_attn_ref(h, L1_attn_wq, L1_attn_wk, L1_attn_wv, L1_attn_wo), axis=-1)
    h = _layernorm(h + _L1_ffn_ref(h, L1_ffn_packed_weight, L1_ffn_weight_scale, L1_ffn_bias), axis=-1)
    h = _layernorm(h + _L2_attn_ref(h, L2_attn_Wq, L2_attn_Wk, L2_attn_Wv, L2_attn_Wr), axis=-1)
    h = _layernorm(h + _L2_ffn_ref(h, L2_ffn_cn_w1, L2_ffn_cn_b1, L2_ffn_cn_w2, L2_ffn_cn_b2, L2_ffn_cn_w3, L2_ffn_cn_b3, L2_ffn_cn_w4, L2_ffn_cn_b4, L2_ffn_gc_w1, L2_ffn_gc_b1, L2_ffn_gc_w2, L2_ffn_gc_b2, L2_ffn_gc_w3, L2_ffn_gc_b3, L2_ffn_adaptive_range), axis=-1)
    h = _layernorm(h + _L3_attn_ref(h, L3_attn_Wq, L3_attn_Wk, L3_attn_Wv, L3_attn_Wg, L3_attn_Wgk1, L3_attn_Wgk2, L3_attn_bgk2, L3_attn_Wo, L3_attn_g_norm_weight), axis=-1)
    h = _layernorm(h + _L3_ffn_ref(h, L3_ffn_w1_w, L3_ffn_w1_s, L3_ffn_w2_w, L3_ffn_w2_s, L3_ffn_h1_w, L3_ffn_h1_s, L3_ffn_h2_w, L3_ffn_h2_s, L3_ffn_w3_w, L3_ffn_w3_s), axis=-1)
    return h

_drawn_inputs = setup_inputs


def setup_inputs(seed=0):
    import zlib

    import numpy as np

    out = dict(_drawn_inputs(seed))
    spreads = {'L0_tok_pixel_masks': (1.0, 0.2),
     'L0_tok_la_ln_q_g': (1.0, 0.6),
     'L0_tok_la_ln_q_b': (0.0, 0.8),
     'L0_tok_la_ln_kv_g': (1.0, 0.6),
     'L0_tok_la_ln_kv_b': (0.0, 0.1),
     'L0_tok_la_proj_b': (0.0, 0.1),
     'L0_tok_ga_ln_q_g': (1.0, 0.6),
     'L0_tok_ga_ln_q_b': (0.0, 0.8),
     'L0_tok_ga_ln_kv_g': (1.0, 0.2),
     'L0_tok_ga_ln_kv_b': (0.0, 0.1),
     'L0_tok_ga_proj_b': (0.0, 0.1),
     'L0_tok_mod_b': (0.0, 0.1),
     'L0_attn_D_param': (1.0, 0.6),
     'L1_ffn_bias': (0.0, 0.1),
     'L2_ffn_cn_b1': (0.0, 0.8),
     'L2_ffn_cn_b2': (0.0, 2.0),
     'L2_ffn_cn_b3': (0.0, 2.0),
     'L2_ffn_gc_b1': (0.0, 2.0),
     'L2_ffn_gc_b2': (0.0, 2.0),
     'L3_attn_bgk2': (0.0, 2.0),
     'L3_attn_g_norm_weight': (1.0, 0.6)}
    factors = {'L0_tok_la_wq': 8.0,
     'L0_tok_ga_wq': 8.0,
     'L0_attn_W_x': 8.0,
     'L0_attn_W_dt': 8.0,
     'L0_attn_b_dt': 8.0,
     'L0_attn_A_log': 64.0,
     'L1_attn_wq': 8.0,
     'L1_attn_wk': 8.0,
     'L2_attn_Wq': 8.0,
     'L2_attn_Wk': 8.0,
     'L2_ffn_cn_w1': 7.354,
     'L2_ffn_cn_w2': 8.0,
     'L2_ffn_cn_w3': 8.0,
     'L2_ffn_cn_w4': 5.934,
     'L2_ffn_gc_w1': 62.624,
     'L2_ffn_gc_w2': 46.288,
     'L3_attn_Wgk1': 33.066,
     'L3_attn_Wgk2': 36.023,
     'L3_ffn_w1_w': 8.0,
     'L3_ffn_w1_s': 8.0,
     'L3_ffn_w2_w': 8.0,
     'L3_ffn_w2_s': 8.0,
     'L3_ffn_h1_w': 8.0,
     'L3_ffn_h1_s': 8.0,
     'L3_ffn_h2_w': 8.0,
     'L3_ffn_h2_s': 8.0,
     'L3_ffn_w3_w': 8.0,
     'L3_ffn_w3_s': 8.0}
    for name, (base, spread) in spreads.items():
        noise = np.random.default_rng([zlib.crc32(name.encode()), seed]).standard_normal(out[name].shape)
        drawn = base * np.exp(spread * noise) if base else spread * noise
        out[name] = jnp.asarray(drawn.astype(out[name].dtype))
    for name, factor in factors.items():
        out[name] = (out[name] * factor).astype(out[name].dtype)
    return out
```

```python
from contextlib import ExitStack

import numpy as np

import concourse.bass as bass
from concourse import mybir

F32 = mybir.dt.float32
BF16 = mybir.dt.bfloat16
I32 = mybir.dt.int32
ALU = mybir.AluOpType
ACT = mybir.ActivationFunctionType
AX = mybir.AxisListType

P = 128
C = 256
CT = C // P
B = 64
L = 5
N = B * L
TT = 4
TN = N // TT
PATCH = 14
TAPS = 9
WIN = 4
NW = B * WIN
NP = NW * TAPS
KC = 3 * PATCH * PATCH
KCT = -(-KC // P)
CHUNK = 512
NCH = -(-NP // CHUNK)
H8 = 8
DH = C // H8
DI = 512
DIT = DI // P
NS = 16
RANK = 16
NE = 8
HID = 384
HIDT = HID // P
H16 = 16
HD1 = 16
HD2 = 64
QT2 = H16 * HD2 // P
LAGS = range(L)
PAIR_OFF = [0]
for _d in LAGS:
    PAIR_OFF.append(PAIR_OFF[-1] + B * (L - _d))
PAIRS = PAIR_OFF[-1]
DH3 = 1024
HT3 = DH3 // P
EPS = 1e-5
MAGIC = 12582912.0
A_LOG_TOP = 88.7
EXP_FLOOR = -200.0
FAR = -1e30

SMALL = {}
for _n, _w in [("ident", 128), ("same32", 128), ("same16", 128), ("inv256", 1), ("inv128", 1), ("one", 1), ("eps", 1),
               ("sign", 1), ("before", 64), ("cosq", 5), ("sinq", 5), ("cosk", 5), ("sink", 5), ("attmask", 80),
               ("la_ln_q_g", 2), ("la_ln_q_b", 2), ("la_ln_kv_g", 2), ("la_ln_kv_b", 2), ("la_proj_b", 2),
               ("ga_ln_q_g", 2), ("ga_ln_q_b", 2), ("ga_ln_kv_g", 2), ("ga_ln_kv_b", 2), ("ga_proj_b", 2),
               ("mod_b", 2), ("class_emb", 2), ("W_conv", 12), ("b_dt", 4), ("A_log", 64), ("D_param", 4),
               ("Wr", 16), ("l1_bias", 256), ("l1_scale", 1), ("cn_b1", 2), ("cn_b2", 1), ("cn_b3", 1), ("cn_b4", 1),
               ("gc_b1", 1), ("gc_b2", 1), ("gc_b3", 1), ("range", 1), ("bgk2", 2), ("gnorm", 1),
               ("w1_s", 8), ("w2_s", 8), ("h1_s", 8), ("h2_s", 8), ("w3_s", 2)]:
    SMALL[_n] = (sum(w for _, w in SMALL.values()), _w)
NSMALL = sum(w for _, w in SMALL.values())


def columns(parts):
    out, at = {}, 0
    for name, kt, width in parts:
        out[name] = (at, kt, width)
        at += kt * width
    return out, at


W_TOK, N_TOK = columns([("conv", KCT, C), ("la_wq", 2, C), ("la_wkv", 2, 2 * C), ("la_proj", 2, C), ("ga_wq", 2, C),
                        ("ga_wkv", 2, 2 * C), ("ga_proj", 2, C), ("mod", 2, C)])
W_MAM, N_MAM = columns([("W_in", 2, 2 * DI), ("W_x", 4, 48), ("W_dt", 1, DI), ("W_out", 4, C)])
W_EXP, N_EXP = columns([("W1", 2, HID), ("W3", 2, HID), ("W2", 3, C)])
W_L2, N_L2 = columns([("wq", 2, 1024), ("wk", 2, 1024), ("wv", 2, 1024), ("wr", 8, C)])
W_L1, N_L1 = columns([("wqp", 2, C), ("wqr", 2, C), ("wkp", 2, P), ("wkr", 2, P), ("wv", 2, P), ("wo", 2, C)])
W_F1, N_F1 = columns([("w1", 2, DH3), ("w2", 2, DH3)])
W_F3, N_F3 = columns([("w3", 8, C), ("cn1", 2, C), ("cn2", 2, P), ("cn3", 1, 64), ("cn4", 1, 1),
                      ("gc1", 2, P), ("gc2", 1, 64), ("gc3", 1, 1)])
W_L3, N_L3 = columns([("wq", 2, C), ("wk", 2, C), ("wv", 2, 512), ("wg", 2, 512), ("gk1", 2, 16), ("gk2", 1, C),
                      ("wo", 4, C)])
W_FH, N_FH = columns([("h1", 8, DH3), ("h2", 8, DH3)])
N_PAT = max(KCT * NP, N_L2 + N_L1, N_L3)
N_BIG = max(NE * N_EXP, 4 * CT * NP, N_FH)
N_WTOK = max(N_TOK, N_F1)
N_WMAM = max(N_MAM, N_F3)
SLOT = DIT * N
N_SCR = 6 * SLOT

SIGNALS = """
small_in packed_in patches_in_0 patches_in_1 patches_in_2 patches_in_3 patches_in_4 conv_w_in tok_w_in mam_w_in
l2_w_in l1_w_in f1_w_in f3_w_in l3_w_in fh_w_in dve_step act_step pool_step cls_in ln_xc ln_sq ln_logvar ln_rstd ln_out
gq_read pe0_copied pe1_copied w_xc w_sq w_logvar w_rstd w_xn red q_copied kq_done v_copied la_shift la_exp agg
aggT_copied lo gk_copied gs_shift gs_exp gv_used gagg cls_out patch_out
u_conv u_silu res_silu xdbl_copied a_clip a_exp a_neg dt_relu dt_abs dt_exp dt_exp1 dt_log delta arg_zero arg decay b_used
scanned hc hc_added y_skip y_out z_mam
gate_copied gate_shift gate_exp comb comb_copied combine_copied silu_h gated moe_act act_used z_moe
rope1 v1_copied s1_clear s1_prod s1_copied s1_shift s1_exp a1_out z_attn1
x_tok_copied x_int xint_copied l1f_read l1f_var l1f_rstd h4_tok h4_copied
q2_copied k2_copied v2_copied s2_masked s2_shift s2_exp s2_prob pT_copied o2_copied z_attn2
gmean gc_act c1_act c2_act c3_act c4_act c_out z_ffn2
qkv3_copied g3_silu gk1_copied gk_min gk_abs gk_exp gk_log keep_set g_diff g_exp s3_prod s3_mul o3_sum
o3_sq o3_logvar o3_rstd o3_out z_attn3
f1_silu f_gate fh1_act fh2_act z_ffn3 tok_out stored
""".split()


class Counts:

    def __init__(self, sems, step):
        self.sems, self.step, self.count, self.last = sems, step, {}, None

    def __call__(self, signal=None):
        name = signal or self.step
        self.count[name] = self.count.get(name, 0) + 1
        self.last = name
        return self.sems[name], 1

    def latest(self):
        return self.sems[self.last], self.count[self.last]


def tower(nc, small, packed, patches, w_tok, w_mam, w_exp, w_l2, w_l1, w_f1, w_f3, w_l3, w_fh, out):
    ctx = ExitStack()
    with ctx:
        def sb(name, cols, dt=F32):
            return ctx.enter_context(nc.sbuf_tensor(name, [P, cols], dt))

        BIG = sb("BIG", N_BIG)
        PAT = sb("PAT", N_PAT)
        WTOK = sb("WTOK", N_WTOK)
        WMAM = sb("WMAM", N_WMAM)
        SCR = sb("SCR", N_SCR)
        SM = sb("SM", NSMALL)
        H = [sb(f"H{i}", CT * N) for i in range(2)]
        Z = sb("Z", CT * N)
        XC = sb("XC", CT * N)
        SQ = sb("SQ", CT * N)
        BANK = [ctx.enter_context(nc.psum_tensor(f"bank{i}", [P, 512], F32)) for i in range(8)]
        S = {name: ctx.enter_context(nc.semaphore(name)) for name in SIGNALS}
        bank_full = [ctx.enter_context(nc.semaphore(f"bank_full_{i}")) for i in range(8)]
        expert_in = [ctx.enter_context(nc.semaphore(f"experts_in_{i}")) for i in range(NE // 2)]

        def sm(name, i=None, rows=P):
            at, w = SMALL[name]
            return SM[0:rows, at:at + w] if i is None else SM[0:rows, at + i:at + i + 1]

        def view(buf, at, *dims, rows=P):
            n = int(np.prod(dims))
            v = buf[0:rows, at:at + n]
            if len(dims) == 2:
                v = v.rearrange("p (a b) -> p a b", b=dims[1])
            elif len(dims) == 3:
                v = v.rearrange("p (a b c) -> p a b c", b=dims[1], c=dims[2])
            elif len(dims) == 4:
                v = v.rearrange("p (a b c d) -> p a b c d", b=dims[1], c=dims[2], d=dims[3])
            return v

        def weight(buf, table, name, base=0, rows=P):
            at, kt, width = table[name]
            return view(buf, base + at, kt, width, rows=rows)

        def tokens(ap):
            if len(ap.shape) == 2:
                return ap.rearrange("p (b l) -> p b l", l=L)
            return ap.rearrange("p m (b l) -> p m b l", l=L)

        def over(ap, n):
            return ap.unsqueeze(1).to_broadcast([ap.shape[0], n] + list(ap.shape[1:]))

        def last(ap, n):
            return ap.unsqueeze(len(ap.shape)).to_broadcast(list(ap.shape) + [n])

        h = [view(H[i], 0, CT, N) for i in range(2)]
        z, xc, sq = view(Z, 0, CT, N), view(XC, 0, CT, N), view(SQ, 0, CT, N)
        ident = sm("ident")

        pe_all = view(BIG, 0, CT, NP)
        xn_all = view(BIG, CT * NP, CT, NP)
        prod_w = view(BIG, 2 * CT * NP, 2, TAPS, C)
        sq_all = view(BIG, 2 * CT * NP, CT, NP)
        v_w = view(BIG, 3 * CT * NP, 2, TAPS, C)
        red = view(SCR, 0, CT, NW)
        redn = view(SCR, 512, CT, NW)
        q_w = view(SCR, 1024, 2, C)
        sc = view(SCR, 1536, 2, TAPS, H8)
        sc_e = view(SCR, 1680, 2, TAPS, H8)
        sc_m = view(SCR, 1824, 2, H8)
        sc_s = view(SCR, 1840, 2, H8)
        sc_r = view(SCR, 1856, 2, H8)
        agg = view(SCR, 1880, 2, C)
        aggT = view(SCR, 2392, CT, NW)
        lo = view(SCR, 2904, CT, NW)
        lon = view(SCR, 3416, CT, NW)
        gkT = view(SCR, 3928, CT, NW)
        gs = view(SCR, 4440, CT, NW)
        gse = view(SCR, 4952, CT, NW)
        gm = view(SCR, 5464, CT, B)
        gr = view(SCR, 5592, CT, B)
        gaggT = view(SCR, 5720, CT, B)
        clsn = view(SCR, 5848, CT, 1)
        gq = view(SCR, 5850, CT, 1)
        gqm = view(SCR, 5852, CT, P)
        w_log = view(SCR, 6108, CHUNK)
        w_rs = view(SCR, 6620, CHUNK)

        u_raw, u, sres, delta, du, e1, az, rz = (view(PAT, i * SLOT, DIT, N) for i in range(8))
        arg = [view(SCR, i * SLOT, DIT, N) for i in range(2)]
        dbu = [view(SCR, (2 + i) * SLOT, DIT, N) for i in range(2)]
        hs = [view(SCR, (4 + i) * SLOT, DIT, N) for i in range(2)]
        hc = [e1, az]
        xdbl = view(PAT, 8 * SLOT, N, rows=48)
        negA = view(PAT, 8 * SLOT + N, DIT, NS)

        lg, ex = (view(SCR, i * 32, TT, NE, rows=TN) for i in range(2))
        gmax, gsum, grec = (view(SCR, 96 + 4 * i, TT, rows=TN) for i in range(3))
        cmp1, cmp2 = (view(SCR, 128 + i * 256, TT, NE, NE, rows=TN) for i in range(2))
        rank = view(SCR, 640, TT, NE, rows=TN)
        combT = view(SCR, 700, N, rows=NE)
        combb = [view(SCR, 1100 + i * N, N) for i in range(2)]
        sil = [view(SCR, 1800 + i * N, N) for i in range(2)]
        gated = [view(SCR, 2500 + i * N, N) for i in range(2)]
        mixed = [view(SCR, 3200 + i * HIDT * N, HIDT, N) for i in range(2)]

        q1, k1, v1, t1a, t1b = (view(BIG, at, *d) for at, d in
                                ((0, (CT, N)), (640, (N,)), (960, (N,)), (1280, (CT, N)), (1920, (CT, N))))
        kt1, kt2 = view(BIG, 2560, N), view(BIG, 2880, N)
        pr1 = [view(BIG, 3200 + CT * PAIR_OFF[d], CT, B * (L - d)) for d in LAGS]
        s1 = view(BIG, 5200, CT * N, L)
        s1e = view(BIG, 8400, CT * N, L)
        s1m, s1s, s1r = (view(BIG, 11600 + 640 * i, CT * N) for i in range(3))
        o1 = view(BIG, 13520, CT, N)
        t1 = view(BIG, 14160, CT, N)

        x_tok = view(SCR, 0, TT, C, rows=TN)
        xq = view(SCR, 1024, TT, C, rows=TN)
        y_tok = view(SCR, 2048, TT, C, rows=TN)
        amax, asc, ainv, tmean, trs = (view(SCR, 3072 + 8 * i, TT, rows=TN) for i in range(5))
        stats = view(SCR, 3120, TT, 6, rows=TN)
        aggr = view(SCR, 3150, TT, 2, rows=TN)
        xqT = sb("xqT", CT * N, BF16)
        wint = sb("wint", 2 * 64, I32)
        wenc = sb("wenc", 2 * C, I32)
        wT = sb("wT", 2 * C, BF16)

        q2, k2 = view(BIG, 0, QT2, N), view(BIG, 2560, QT2, N)
        v2 = view(BIG, 5120, TT, 1024, rows=TN)
        s2 = view(BIG, 9216, TT, H16, TN, rows=TN)
        o2 = view(BIG, 14336, QT2, N)
        s2m = view(SCR, 0, TT, H16, rows=TN)

        def slot2(hd):
            return 8 * (hd // 8) + 4 * (hd % 2) + hd % 8 // 2

        s2s = view(SCR, 64, TT, H16, rows=TN)
        s2r = view(SCR, 128, TT, H16, rows=TN)
        pT = [view(SCR, 256 + i * 1280, H16, TN, rows=TN) for i in range(2)]

        cn_a = view(SCR, 0, CT, N)
        cn_b = view(SCR, 640, N)
        cn_c = view(SCR, 960, N, rows=64)
        cn_t = view(SCR, 1280, N)
        coup = view(SCR, 1600, N)
        cup2 = view(SCR, 1920, N)
        ctmp = view(SCR, 2240, CT, N)
        cout = [view(SCR, 2880 + i * 640, CT, N) for i in range(2)]
        gmn = view(SCR, 4160, CT, B)
        gc_a = view(SCR, 4288, B)
        gc_b = view(SCR, 4352, B, rows=64)
        gf = view(SCR, 4416, B)
        r2 = view(SCR, 4480, 2)

        A3 = 5000
        q3, k3 = view(SCR, 0, CT, N), view(SCR, 640, CT, N)
        sg3 = view(SCR, 1280, 4, N)
        v3 = view(SCR, 2560, 4, N)
        o3 = view(SCR, 3840, 4, N)
        gk1 = view(SCR, 5120, N, rows=RANK)
        gaz = view(SCR, 5440, CT, N)
        gmin = view(SCR, 6080, CT, N)
        gcum = view(SCR, 6720, CT, N)
        keep = view(PAT, A3, CT * N)
        gdf = view(PAT, A3 + 640, CT * PAIRS)
        pr3 = view(PAT, A3 + 640 + 1920, CT * PAIRS)
        t3 = [view(PAT, A3 + 640 + 3840 + i * N, N) for i in range(4)]
        osq = view(PAT, A3 + 640, 4, N)
        rs3 = view(PAT, A3 + 640 + 1920, 4, N)
        gdf_d = [view(PAT, A3 + 640 + CT * PAIR_OFF[d], CT, B * (L - d)) for d in LAGS]
        pr3_d = [view(PAT, A3 + 640 + 1920 + CT * PAIR_OFF[d], CT, B * (L - d)) for d in LAGS]

        fa = view(PAT, 0, HT3, N)
        fb = view(PAT, 2560, HT3, N)
        fsil = [view(SCR, i * N, N) for i in range(2)]
        otok = view(SCR, 1024, TT, C, rows=TN)

        place = {}
        uses = [0] * 8
        reader = [(S["small_in"], 16)] * 8
        before = {}
        expected = {}

        block = ctx.enter_context(nc.Block())

        @block.tensor
        def _(pe):
            ring = {"banks": list(range(8)), "at": 0}

            def rotate(banks):
                ring["banks"], ring["at"] = list(banks), 0

            def take(key, signal, bank=None, count=None):
                if bank is None:
                    bank = ring["banks"][ring["at"] % len(ring["banks"])]
                    ring["at"] += 1
                if count is None:
                    expected[signal] = expected.get(signal, 0) + 1
                    count = expected[signal]
                before[key] = reader[bank]
                reader[bank] = (S[signal], count)
                uses[bank] += 1
                place[key] = (bank, uses[bank])
                return BANK[bank]

            def emptied(key):
                return before[key]

            def fills(key):
                return bank_full[place[key][0]], 1

            def product(out, w, m0, m1, x, tiles, xs=None):
                for k in range(tiles):
                    ins = pe.matmul(out, w[:, k, m0:m1], x[:, k] if xs is None else xs(k),
                                    start=(k == 0), stop=(k == tiles - 1))
                return ins

            ln_at = [0]

            def norm(key, x, sq_x, n, ready, count=1):
                i = ln_at[0] = ln_at[0] + 1
                pe.wait_ge(S[ready], count)
                o = take((key, "mean"), "ln_xc")
                pe.wait_ge(*emptied((key, "mean")))
                for k in range(CT):
                    ins = pe.matmul(o[:, 0:n], sm("inv256").to_broadcast([P, P]), x[:, k], start=(k == 0), stop=(k == CT - 1))
                ins.then_inc(*fills((key, "mean")))
                pe.wait_ge(S["ln_sq"], i)
                o = take((key, "var"), "ln_logvar")
                pe.wait_ge(*emptied((key, "var")))
                for k in range(CT):
                    ins = pe.matmul(o[:, 0:n], sm("inv256").to_broadcast([P, P]), sq_x[:, k], start=(k == 0), stop=(k == CT - 1))
                ins.then_inc(*fills((key, "var")))

            def tokenizer():
                w = {n: weight(WTOK, W_TOK, n) for n in W_TOK}
                pe.wait_ge(S["small_in"], 16)
                norm("cls", z[:, :, 0:1], sq[:, :, 0:1], 1, "cls_in")
                pe.wait_ge(S["conv_w_in"], 16)

                def conv(j):
                    n = min(CHUNK, NP - j * CHUNK)
                    pe.wait_ge(S[f"patches_in_{j}"], 16 * KCT)
                    for m in range(CT):
                        o = take(("conv", j, m), f"pe{m}_copied")
                        pe.wait_ge(*emptied(("conv", j, m)))
                        for k in range(KCT):
                            r = min(P, KC - k * P)
                            ins = pe.matmul(o[:, 0:n], w["conv"][0:r, k, m * P:(m + 1) * P],
                                            PAT[0:r, k * NP + j * CHUNK:k * NP + j * CHUNK + n],
                                            start=(k == 0), stop=(k == KCT - 1))
                        ins.then_inc(*fills(("conv", j, m)))

                def stat(kind, j, src, signal):
                    n = min(CHUNK, NP - j * CHUNK)
                    o = take((kind, j), signal)
                    pe.wait_ge(*emptied((kind, j)))
                    for k in range(CT):
                        ins = pe.matmul(o[:, 0:n], sm("inv256").to_broadcast([P, P]), src[:, k, j * CHUNK:j * CHUNK + n],
                                        start=(k == 0), stop=(k == CT - 1))
                    ins.then_inc(*fills((kind, j)))

                for j in range(NCH + 2):
                    if j < NCH:
                        conv(j)
                    if 1 <= j <= NCH:
                        pe.wait_ge(S["pe0_copied"], j)
                        pe.wait_ge(S["pe1_copied"], j)
                        stat("wmean", j - 1, pe_all, "w_xc")
                    if j >= 2:
                        pe.wait_ge(S["w_sq"], j - 1)
                        stat("wvar", j - 2, sq_all, "w_logvar")
                pe.wait_ge(S["tok_w_in"], 16)
                pe.wait_ge(S["ln_out"], 1)
                o = take("gq", "gq_read")
                pe.wait_ge(*emptied("gq"))
                for m in range(CT):
                    ins = product(o[:, m:m + 1], w["ga_wq"], m * P, (m + 1) * P, clsn, CT)
                ins.then_inc(*fills("gq"))
                norm("red", red, sq[:, :, 0:NW], NW, "red")
                pe.wait_ge(S["ln_out"], 2)
                for t in range(2):
                    o = take(("q", t), "q_copied")
                    pe.wait_ge(*emptied(("q", t)))
                    ins = product(o[:, 0:C], redn[:, :, t * P:(t + 1) * P], 0, P, w["la_wq"], CT)
                    ins.then_inc(*fills(("q", t)))
                for k in range(TAPS):
                    pe.wait_ge(S["w_xn"], k * NW // CHUNK + 1)
                    for t in range(2):
                        o = take(("kv", k, t), "v_copied")
                        pe.wait_ge(*emptied(("kv", k, t)))
                        at = k * NW + t * P
                        ins = product(o[:, :], xn_all[:, :, at:at + P], 0, P, w["la_wkv"], CT)
                        ins.then_inc(*fills(("kv", k, t)))
                pe.wait_ge(S["agg"], 2)
                o = take("aggT", "aggT_copied")
                pe.wait_ge(*emptied("aggT"))
                for m in range(CT):
                    for t in range(2):
                        ins = pe.transpose(o[:, m * NW + t * P:m * NW + (t + 1) * P], agg[:, t, m * P:(m + 1) * P], ident)
                ins.then_inc(*fills("aggT"))
                pe.wait_ge(S["aggT_copied"], 1)
                o = take("proj", "lo")
                pe.wait_ge(*emptied("proj"))
                for m in range(CT):
                    ins = product(o[:, m * NW:(m + 1) * NW], w["la_proj"], m * P, (m + 1) * P, aggT, CT)
                ins.then_inc(*fills("proj"))
                pe.wait_ge(S["lo"], 1)
                o = take("mod", "patch_out")
                pe.wait_ge(*emptied("mod"))
                for m in range(CT):
                    ins = product(o[:, m * NW:(m + 1) * NW], w["mod"], m * P, (m + 1) * P, lo, CT)
                ins.then_inc(*fills("mod"))
                norm("lo", lo, sq[:, :, 0:NW], NW, "lo")
                pe.wait_ge(S["ln_out"], 3)
                for key, sig, c0 in (("gk", "gk_copied", 0), ("gv", "gv_used", C)):
                    o = take(key, sig)
                    pe.wait_ge(*emptied(key))
                    for m in range(CT):
                        ins = product(o[:, m * NW:(m + 1) * NW], w["ga_wkv"], c0 + m * P, c0 + (m + 1) * P, lon, CT)
                    ins.then_inc(*fills(key))
                pe.wait_ge(S["gk_copied"], 1)
                pe.wait_ge(S["gq_read"], 1)
                o = take("gs", "gs_shift")
                pe.wait_ge(*emptied("gs"))
                for m in range(CT):
                    ins = pe.matmul(o[:, m * NW:(m + 1) * NW], gqm[:, m, :], gkT[:, m, :], start=True, stop=True)
                ins.then_inc(*fills("gs"))
                pe.wait_ge(S["gagg"], 1)
                o = take("gproj", "cls_out")
                pe.wait_ge(*emptied("gproj"))
                for m in range(CT):
                    ins = product(o[:, m * B:(m + 1) * B], w["ga_proj"], m * P, (m + 1) * P, gaggT, CT)
                ins.then_inc(*fills("gproj"))

            def state_space():
                w = {n: weight(WMAM, W_MAM, n) for n in W_MAM}
                pe.wait_ge(S["mam_w_in"], 16)
                pe.wait_ge(S["cls_out"], 1)
                pe.wait_ge(S["patch_out"], 1)
                for m in range(2 * DIT):
                    o = take(("win", m), "u_conv" if m < DIT else "res_silu")
                    pe.wait_ge(*emptied(("win", m)))
                    product(o[:, 0:N], w["W_in"], m * P, (m + 1) * P, h[0], CT).then_inc(*fills(("win", m)))
                pe.wait_ge(S["u_silu"], 1)
                o = take("xdbl", "xdbl_copied")
                pe.wait_ge(*emptied("xdbl"))
                product(o[0:48, 0:N], w["W_x"], 0, 48, u, DIT).then_inc(*fills("xdbl"))
                pe.wait_ge(S["xdbl_copied"], 1)
                for m in range(DIT):
                    o = take(("wdt", m), "dt_relu")
                    pe.wait_ge(*emptied(("wdt", m)))
                    pe.matmul(o[:, 0:N], w["W_dt"][0:RANK, 0, m * P:(m + 1) * P], xdbl[0:RANK, :],
                                               start=True, stop=True).then_inc(*fills(("wdt", m)))
                y = []
                for m in range(DIT):
                    o = take(("y", m), "y_skip", bank=4 + m)
                    pe.wait_ge(*emptied(("y", m)))
                    y.append(o)
                rotate(range(4))

                def add(n):
                    pe.wait_ge(S["hc"], n + 1)
                    for m in range(DIT):
                        ins = pe.matmul(y[m][:, 0:N], ident, hc[n % 2][:, m], start=(n == 0), stop=(n == NS - 1))
                        if n == NS - 1:
                            ins.then_inc(*fills(("y", m)))
                    if n < NS - 1:
                        ins.then_inc(S["hc_added"], 1)

                for n in range(NS):
                    for key, row, sig in (("B", RANK + n, "b_used"), ("C", RANK + NS + n, "hc")):
                        o = take((key, n), sig)
                        pe.wait_ge(*emptied((key, n)))
                        pe.matmul(o[:, 0:N], ident[0:48, row:row + 1].to_broadcast([48, P]), xdbl,
                                                 start=True, stop=True).then_inc(*fills((key, n)))
                    if n >= 1:
                        add(n - 1)
                add(NS - 1)
                rotate(range(8))
                pe.wait_ge(S["y_out"], DIT)
                for m in range(CT):
                    o = take(("wout", m), "z_mam")
                    pe.wait_ge(*emptied(("wout", m)))
                    product(o[:, 0:N], w["W_out"], m * P, (m + 1) * P, u_raw, DIT).then_inc(*fills(("wout", m)))
                norm("ln0", z, sq, N, "z_mam", 2)

            def experts():
                pe.wait_ge(S["ln_out"], 4)
                o = take("gate", "gate_copied")
                pe.wait_ge(*emptied("gate"))
                wr = view(SM, SMALL["Wr"][0], 2, NE)
                for t in range(TT):
                    ins = product(o[0:TN, t * NE:(t + 1) * NE], h[1][:, :, t * TN:(t + 1) * TN], 0, TN, wr, CT)
                ins.then_inc(*fills("gate"))
                rotate(range(6))

                def up(e):
                    pe.wait_ge(expert_in[e // 2], 16)
                    for m in range(HIDT):
                        for name, sig in (("W1", "silu_h"), ("W3", "gated")):
                            w = weight(BIG, W_EXP, name, base=e * N_EXP)
                            o = take((name, e, m), sig)
                            pe.wait_ge(*emptied((name, e, m)))
                            product(o[:, 0:N], w, m * P, (m + 1) * P, h[1], CT).then_inc(*fills((name, e, m)))

                acc = []
                for m in range(CT):
                    o = take(("moe", m), "z_moe", bank=6 + m)
                    pe.wait_ge(*emptied(("moe", m)))
                    acc.append(o)

                def combine(e):
                    o = take(("comb", e), "combine_copied")
                    pe.wait_ge(*emptied(("comb", e)))
                    pe.matmul(o[:, 0:N], ident[0:NE, e:e + 1].to_broadcast([NE, P]), combT,
                                                start=True, stop=True).then_inc(*fills(("comb", e)))

                def down(e):
                    w = weight(BIG, W_EXP, "W2", base=e * N_EXP)
                    for k in range(HIDT):
                        pe.wait_ge(S["moe_act"], e * HIDT + k + 1)
                        for m in range(CT):
                            ins = pe.matmul(acc[m][:, 0:N], w[:, k, m * P:(m + 1) * P], mixed[e % 2][:, k],
                                            start=(e == 0 and k == 0), stop=(e == NE - 1 and k == HIDT - 1))
                            if e == NE - 1 and k == HIDT - 1:
                                ins.then_inc(*fills(("moe", m)))
                    if e < NE - 1:
                        ins.then_inc(S["act_used"], 1)

                pe.wait_ge(S["comb"], 1)
                o = take("combT", "comb_copied")
                pe.wait_ge(*emptied("combT"))
                for t in range(TT):
                    ins = pe.transpose(o[0:NE, t * TN:(t + 1) * TN], ex[:, t, :], ident[0:TN, 0:TN])
                ins.then_inc(*fills("combT"))
                pe.wait_ge(S["comb_copied"], 1)
                for e in range(NE + 1):
                    if e < NE:
                        combine(e)
                        up(e)
                    if e >= 1:
                        down(e - 1)
                rotate(range(8))
                norm("ln1", z, sq, N, "z_moe", 2)

            def attention1():
                base = N_L2
                w = {n: weight(PAT, W_L1, n, base=base) for n in W_L1}
                pe.wait_ge(S["l1_w_in"], 16)
                pe.wait_ge(S["ln_out"], 5)
                for name, key, sig, tiles in (("wqp", "q1", "rope1", 2), ("wqr", "q1r", "rope1", 2),
                                              ("wkp", "k1", "rope1", 1), ("wkr", "k1r", "rope1", 1),
                                              ("wv", "v1", "v1_copied", 1)):
                    for m in range(tiles):
                        o = take((key, m), sig)
                        pe.wait_ge(*emptied((key, m)))
                        product(o[:, 0:N], w[name], m * P, (m + 1) * P, h[0], CT).then_inc(*fills((key, m)))
                for d in LAGS:
                    pe.wait_ge(S["s1_prod"], d + 1)
                    for m in range(CT):
                        o = take(("s1", d, m), "s1_copied")
                        pe.wait_ge(*emptied(("s1", d, m)))
                        pe.matmul(o[:, 0:B * (L - d)], sm("same16"), pr1[d][:, m],
                                                     start=True, stop=True).then_inc(*fills(("s1", d, m)))
                pe.wait_ge(S["a1_out"], 1)
                for m in range(CT):
                    o = take(("wo1", m), "z_attn1")
                    pe.wait_ge(*emptied(("wo1", m)))
                    product(o[:, 0:N], w["wo"], m * P, (m + 1) * P, o1, CT).then_inc(*fills(("wo1", m)))
                norm("ln2", z, sq, N, "z_attn1", 2)

            def ternary():
                pe.wait_ge(S["ln_out"], 6)
                for t in range(TT):
                    o = take(("xtok", t), "x_tok_copied")
                    pe.wait_ge(*emptied(("xtok", t)))
                    for m in range(CT):
                        ins = pe.transpose(o[0:TN, m * P:(m + 1) * P], h[1][:, m, t * TN:(t + 1) * TN], ident)
                    ins.then_inc(*fills(("xtok", t)))
                pe.wait_ge(S["x_int"], 1)
                for m in range(CT):
                    o = take(("xint", m), "xint_copied")
                    pe.wait_ge(*emptied(("xint", m)))
                    for t in range(TT):
                        ins = pe.transpose(o[:, t * TN:(t + 1) * TN], xq[:, t, m * P:(m + 1) * P], ident[0:TN, 0:TN])
                    ins.then_inc(*fills(("xint", m)))
                pe.wait_ge(S["xint_copied"], CT)
                xT = xqT[:, :].rearrange("p (m n) -> p m n", m=CT)
                wv = wT[:, :].rearrange("p (c o) -> p c o", c=2)
                for t in range(TT):
                    o = take(("l1f", t), "l1f_read")
                    pe.wait_ge(*emptied(("l1f", t)))
                    product(o[0:TN, 0:C], xT[:, :, t * TN:(t + 1) * TN], 0, TN, wv, CT).then_inc(*fills(("l1f", t)))
                pe.wait_ge(S["h4_tok"], 1)
                for m in range(CT):
                    o = take(("h4", m), "h4_copied")
                    pe.wait_ge(*emptied(("h4", m)))
                    for t in range(TT):
                        ins = pe.transpose(o[:, t * TN:(t + 1) * TN], y_tok[:, t, m * P:(m + 1) * P], ident[0:TN, 0:TN])
                    ins.then_inc(*fills(("h4", m)))

            def attention2():
                w = {n: weight(PAT, W_L2, n) for n in W_L2}
                pe.wait_ge(S["l2_w_in"], 16)
                pe.wait_ge(S["h4_copied"], CT)
                for m in range(QT2):
                    for name, key in (("wq", "q2"), ("wk", "k2")):
                        o = take((key, m), f"{key}_copied")
                        pe.wait_ge(*emptied((key, m)))
                        product(o[:, 0:N], w[name], m * P, (m + 1) * P, h[0], CT).then_inc(*fills((key, m)))

                def values(t):
                    for hf in range(2):
                        o = take(("v2", t, hf), "v2_copied")
                        pe.wait_ge(*emptied(("v2", t, hf)))
                        product(o[0:TN, :], h[0][:, :, t * TN:(t + 1) * TN], 0, TN,
                                                    w["wv"][:, :, hf * 512:(hf + 1) * 512], CT).then_inc(*fills(("v2", t, hf)))

                def scores(t):
                    for half in range(2):
                        pe.wait_ge(S["q2_copied"], 4 * half + 4)
                        pe.wait_ge(S["k2_copied"], 4 * half + 4)
                        o2h = []
                        for odd in range(2):
                            o = take(("s2", t, 2 * half + odd), "s2_masked")
                            pe.wait_ge(*emptied(("s2", t, 2 * half + odd)))
                            o2h.append(o)
                        for i in range(4):
                            for odd in range(2):
                                r = slice(HD2 * odd, HD2 * odd + HD2)
                                m = 4 * half + i
                                ins = pe.matmul(o2h[odd][0:TN, i * TN:(i + 1) * TN], q2[r, m, t * TN:(t + 1) * TN],
                                                k2[r, m, t * TN:(t + 1) * TN], start=True, stop=True)
                                if i == 3:
                                    ins.then_inc(*fills(("s2", t, 2 * half + odd)))

                def mix(t):
                    pe.wait_ge(S["s2_prob"], t + 1)
                    for g in range(4):
                        o = take(("pT", t, g), "pT_copied")
                        pe.wait_ge(*emptied(("pT", t, g)))
                        for i in range(4):
                            ins = pe.transpose(o[0:TN, i * TN:(i + 1) * TN], s2[:, t, 4 * g + i, :], ident[0:TN, 0:TN])
                        ins.then_inc(*fills(("pT", t, g)))
                    pe.wait_ge(S["v2_copied"], 2 * t + 2)
                    for g in range(2):
                        pe.wait_ge(S["pT_copied"], 4 * t + 2 * g + 2)
                        o = take(("o2", t, g), "o2_copied")
                        pe.wait_ge(*emptied(("o2", t, g)))
                        for i in range(8):
                            hd = 8 * g + i
                            r = slice(HD2 * (hd % 2), HD2 * (hd % 2) + HD2)
                            ins = pe.matmul(o[r, (i // 2) * TN:(i // 2 + 1) * TN], v2[:, t, hd * HD2:(hd + 1) * HD2],
                                            pT[t % 2][:, slot2(hd), :], start=True, stop=True)
                        ins.then_inc(*fills(("o2", t, g)))

                scores(0)
                for t in range(TT):
                    values(t)
                    if t + 1 < TT:
                        scores(t + 1)
                    mix(t)
                pe.wait_ge(S["o2_copied"], 2 * TT)
                for m in range(CT):
                    o = take(("r2", m), "z_attn2")
                    pe.wait_ge(*emptied(("r2", m)))
                    product(o[:, 0:N], w["wr"], m * P, (m + 1) * P, o2, QT2).then_inc(*fills(("r2", m)))
                norm("ln4", z, sq, N, "z_attn2", 2)

            def coupling():
                w = {n: weight(WMAM, W_F3, n) for n in W_F3}
                pe.wait_ge(S["f3_w_in"], 16)
                pe.wait_ge(S["gmean"], 1)
                o = take("gc1", "gc_act")
                pe.wait_ge(*emptied("gc1"))
                product(o[:, 0:B], w["gc1"], 0, P, gmn, CT).then_inc(*fills("gc1"))

                def first(cyc):
                    for m in range(CT):
                        o = take(("c1", cyc, m), "c1_act")
                        pe.wait_ge(*emptied(("c1", cyc, m)))
                        product(o[:, 0:N], w["cn1"], m * P, (m + 1) * P,
                                                     h[1] if cyc == 0 else cout[(cyc - 1) % 2], CT).then_inc(*fills(("c1", cyc, m)))

                first(0)
                pe.wait_ge(S["gc_act"], 1)
                o = take("gc2", "gc_act")
                pe.wait_ge(*emptied("gc2"))
                pe.matmul(o[0:64, 0:B], w["gc2"][:, 0, :], gc_a, start=True, stop=True).then_inc(*fills("gc2"))
                pe.wait_ge(S["gc_act"], 2)
                o = take("gc3", "gc_act")
                pe.wait_ge(*emptied("gc3"))
                pe.matmul(o[:, 0:B], w["gc3"][0:64, 0, :].to_broadcast([64, P]), gc_b, start=True, stop=True).then_inc(*fills("gc3"))
                for cyc in range(3):
                    if cyc:
                        pe.wait_ge(S["c_out"], cyc)
                        first(cyc)
                    pe.wait_ge(S["c1_act"], 2 * cyc + 2)
                    o = take(("c2", cyc), "c2_act")
                    pe.wait_ge(*emptied(("c2", cyc)))
                    product(o[:, 0:N], w["cn2"], 0, P, cn_a, CT).then_inc(*fills(("c2", cyc)))
                    pe.wait_ge(S["c2_act"], cyc + 1)
                    o = take(("c3", cyc), "c3_act")
                    pe.wait_ge(*emptied(("c3", cyc)))
                    pe.matmul(o[0:64, 0:N], w["cn3"][:, 0, :], cn_b, start=True, stop=True).then_inc(*fills(("c3", cyc)))
                    pe.wait_ge(S["c3_act"], cyc + 1)
                    o = take(("c4", cyc), "c4_act")
                    pe.wait_ge(*emptied(("c4", cyc)))
                    pe.matmul(o[:, 0:N], w["cn4"][0:64, 0, :].to_broadcast([64, P]), cn_c,
                                                start=True, stop=True).then_inc(*fills(("c4", cyc)))
                norm("ln5", z, sq, N, "z_ffn2", 1)

            def attention3():
                w = {n: weight(PAT, W_L3, n) for n in W_L3}
                pe.wait_ge(S["l3_w_in"], 16)
                pe.wait_ge(S["ln_out"], 8)
                o = take("gk1", "gk1_copied")
                pe.wait_ge(*emptied("gk1"))
                product(o[0:RANK, 0:N], w["gk1"], 0, RANK, h[0], CT).then_inc(*fills("gk1"))
                for key, name, tiles, sig in (("q3", "wq", 2, "qkv3_copied"), ("k3", "wk", 2, "qkv3_copied")):
                    for m in range(tiles):
                        o = take((key, m), sig)
                        pe.wait_ge(*emptied((key, m)))
                        product(o[:, 0:N], w[name], m * P, (m + 1) * P, h[0], CT).then_inc(*fills((key, m)))
                pe.wait_ge(S["gk1_copied"], 1)
                for m in range(CT):
                    o = take(("gk2", m), "gk_min")
                    pe.wait_ge(*emptied(("gk2", m)))
                    pe.matmul(o[:, 0:N], w["gk2"][0:RANK, 0, m * P:(m + 1) * P], gk1, start=True, stop=True).then_inc(*fills(("gk2", m)))
                for key, name, tiles, sig in (("v3", "wv", 4, "qkv3_copied"), ("g3", "wg", 4, "g3_silu")):
                    for m in range(tiles):
                        o = take((key, m), sig)
                        pe.wait_ge(*emptied((key, m)))
                        product(o[:, 0:N], w[name], m * P, (m + 1) * P, h[0], CT).then_inc(*fills((key, m)))
                for d in LAGS:
                    pe.wait_ge(S["s3_prod"], d + 1)
                    for hd in range(4):
                        o = take(("s3", d, hd), "s3_mul")
                        pe.wait_ge(*emptied(("s3", d, hd)))
                        r = slice(64 * (hd % 2), 64 * (hd % 2) + 64)
                        pe.matmul(o[:, 0:B * (L - d)], sm("one")[r, :].to_broadcast([64, P]),
                                                      pr3_d[d][r, hd // 2], start=True, stop=True).then_inc(*fills(("s3", d, hd)))
                pe.wait_ge(S["o3_sq"], 1)
                for hd in range(4):
                    o = take(("ms3", hd), "o3_logvar")
                    pe.wait_ge(*emptied(("ms3", hd)))
                    pe.matmul(o[:, 0:N], sm("inv128").to_broadcast([P, P]), osq[:, hd], start=True, stop=True).then_inc(*fills(("ms3", hd)))
                pe.wait_ge(S["o3_out"], 1)
                for m in range(CT):
                    o = take(("wo3", m), "z_attn3")
                    pe.wait_ge(*emptied(("wo3", m)))
                    product(o[:, 0:N], w["wo"], m * P, (m + 1) * P, o3, 4).then_inc(*fills(("wo3", m)))
                norm("ln6", z, sq, N, "z_attn3", 2)

            def last_ffn():
                w12 = {n: weight(WTOK, W_F1, n) for n in W_F1}
                w3 = weight(WMAM, W_F3, "w3")
                wh = {n: weight(BIG, W_FH, n) for n in W_FH}
                pe.wait_ge(S["f1_w_in"], 16)
                pe.wait_ge(S["ln_out"], 9)
                for m in range(HT3):
                    for name, sig in (("w1", "f1_silu"), ("w2", "f_gate")):
                        o = take((name, m), sig)
                        pe.wait_ge(*emptied((name, m)))
                        product(o[:, 0:N], w12[name], m * P, (m + 1) * P, h[1], CT).then_inc(*fills((name, m)))
                pe.wait_ge(S["fh_w_in"], 32)
                for name, src, need, sig in (("h1", fa, "f_gate", "fh1_act"), ("h2", fb, "fh1_act", "fh2_act")):
                    for m in range(HT3):
                        o = take((name, m), sig)
                        pe.wait_ge(*emptied((name, m)))
                        for k in range(HT3):
                            if m == 0:
                                pe.wait_ge(S[need], k + 1)
                            ins = pe.matmul(o[:, 0:N], wh[name][:, k, m * P:(m + 1) * P], src[:, k],
                                            start=(k == 0), stop=(k == HT3 - 1))
                        ins.then_inc(*fills((name, m)))
                pe.wait_ge(S["fh2_act"], HT3)
                for m in range(CT):
                    o = take(("f3", m), "z_ffn3")
                    pe.wait_ge(*emptied(("f3", m)))
                    product(o[:, 0:N], w3, m * P, (m + 1) * P, fa, HT3).then_inc(*fills(("f3", m)))
                norm("ln7", z, sq, N, "z_ffn3", 2)
                pe.wait_ge(S["ln_out"], 10)
                for t in range(TT):
                    o = take(("out", t), "tok_out")
                    pe.wait_ge(*emptied(("out", t)))
                    for m in range(CT):
                        ins = pe.transpose(o[0:TN, m * P:(m + 1) * P], h[0][:, m, t * TN:(t + 1) * TN], ident)
                    ins.then_inc(*fills(("out", t)))

            for f in [tokenizer, state_space, experts, attention1, ternary, attention2, coupling, attention3, last_ffn]:
                f()

        def filled(key):
            return bank_full[place[key][0]], place[key][1]

        def result(key):
            return BANK[place[key][0]]

        @block.vector
        def _(dve):
            did = Counts(S, "dve_step")
            tt, ts, copy = dve.tensor_tensor, dve.tensor_scalar, dve.tensor_copy

            def stt(out, a, s, b, op0, op1):
                return dve.scalar_tensor_tensor(out=out, in0=a, scalar=s, in1=b, op0=op0, op1=op1)

            def reduce(out, a, op):
                return dve.tensor_reduce(out, a, AX.X, op)

            ln_at = [0]

            def norm(key, x, n, out, gain=None, shift=None):
                i = ln_at[0] = ln_at[0] + 1
                c = xc[:, :, 0:n]
                dve.wait_ge(*filled((key, "mean")))
                mean = result((key, "mean"))[:, 0:n]
                tt(c, x, over(mean, CT), ALU.subtract).then_inc(*did("ln_xc"))
                dve.wait_ge(S["ln_rstd"], i)
                rstd = SQ[:, N:N + n]
                if gain is None:
                    tt(out, c, over(rstd, CT), ALU.mult).then_inc(*did("ln_out"))
                    return
                for m in range(CT):
                    stt(out[:, m], c[:, m], sm(gain, m), rstd, ALU.mult, ALU.mult).then_inc(*did())
                dve.wait_ge(*did.latest())
                for m in range(CT):
                    ts(out[:, m], out[:, m], sm(shift, m), None, ALU.add)\
                        .then_inc(*did("ln_out" if m == CT - 1 else None))

            def residual(key, h_in, signal):
                for m in range(CT):
                    dve.wait_ge(*filled((key, m)))
                    o = result((key, m))
                    tt(z[:, m], o[:, 0:N], h_in[:, m], ALU.add).then_inc(*did(signal))

            def tokenizer():
                dve.wait_ge(S["small_in"], 16)
                copy(z[:, :, 0:1], view(SM, SMALL["class_emb"][0], CT, 1)).then_inc(*did("cls_in"))
                norm("cls", z[:, :, 0:1], 1, clsn, "ga_ln_q_g", "ga_ln_q_b")
                for j in range(NCH + 2):
                    if j < NCH:
                        n = min(CHUNK, NP - j * CHUNK)
                        dve.wait_ge(*filled(("conv", j, 0)))
                        o = result(("conv", j, 0))
                        copy(pe_all[:, 0, j * CHUNK:j * CHUNK + n], o[:, 0:n]).then_inc(*did("pe0_copied"))
                    if 1 <= j <= NCH:
                        i = j - 1
                        n = min(CHUNK, NP - i * CHUNK)
                        c = slice(i * CHUNK, i * CHUNK + n)
                        dve.wait_ge(*filled(("wmean", i)))
                        o = result(("wmean", i))
                        tt(xn_all[:, :, c], pe_all[:, :, c], over(o[:, 0:n], CT), ALU.subtract).then_inc(*did("w_xc"))
                    if j >= 2:
                        i = j - 2
                        n = min(CHUNK, NP - i * CHUNK)
                        c = slice(i * CHUNK, i * CHUNK + n)
                        dve.wait_ge(S["w_rstd"], i + 1)
                        dve.wait_ge(S["w_sq"], i + 1)
                        for m in range(CT):
                            stt(xn_all[:, m, c], xn_all[:, m, c], sm("la_ln_kv_g", m), w_rs[:, 0:n], ALU.mult,
                                ALU.mult).then_inc(*did())
                        dve.wait_ge(*did.latest())
                        for m in range(CT):
                            ts(xn_all[:, m, c], xn_all[:, m, c], sm("la_ln_kv_b", m), None, ALU.add)\
                                .then_inc(*did("w_xn" if m == CT - 1 else None))
                dve.wait_ge(*filled("gq"))
                o = result("gq")
                for m in range(CT):
                    ts(gqm[:, m, :], sm("same32"), o[:, m:m + 1], float(C) ** -0.5, ALU.mult, ALU.mult)\
                        .then_inc(*did("gq_read" if m == CT - 1 else None))
                dve.wait_ge(S["pe1_copied"], NCH)
                for m in range(CT):
                    reduce(red[:, m], pe_all[:, m].rearrange("p (k w) -> p w k", k=TAPS), ALU.add).then_inc(*did())
                dve.wait_ge(*did.latest())
                ts(red, red, 1.0 / TAPS, None, ALU.mult).then_inc(*did("red"))
                norm("red", red, NW, redn, "la_ln_q_g", "la_ln_q_b")
                dve.wait_ge(S["q_copied"], 2)
                for k in range(TAPS):
                    for t in range(2):
                        dve.wait_ge(*filled(("kv", k, t)))
                        o = result(("kv", k, t))
                        tt(prod_w[:, t, k], o[:, 0:C], q_w[:, t], ALU.mult).then_inc(*did("kq_done"))
                dve.wait_ge(*did.latest())
                for t in range(2):
                    reduce(sc[:, t].rearrange("p k h -> p (k h)"),
                           prod_w[:, t].rearrange("p k (h d) -> p (k h) d", d=DH), ALU.add)\
                        .then_inc(*did())
                dve.wait_ge(*did.latest())
                reduce(sc_m, sc.rearrange("p t k h -> p t h k"), ALU.max).then_inc(*did())
                dve.wait_ge(*did.latest())
                tt(sc_e, sc, sc_m.unsqueeze(2).to_broadcast([P, 2, TAPS, H8]), ALU.subtract)\
                    .then_inc(*did("la_shift"))
                dve.wait_ge(S["la_exp"], 1)
                reduce(sc_s, sc_e.rearrange("p t k h -> p t h k"), ALU.add).then_inc(*did())
                dve.wait_ge(*did.latest())
                dve.reciprocal(sc_r, sc_s).then_inc(*did())
                dve.wait_ge(*did.latest())
                tt(sc, sc_e, sc_r.unsqueeze(2).to_broadcast([P, 2, TAPS, H8]), ALU.mult).then_inc(*did())
                dve.wait_ge(*did.latest())
                dve.wait_ge(S["v_copied"], 2 * TAPS)
                for t in range(2):
                    tt(prod_w[:, t].rearrange("p k (h d) -> p (k h) d", d=DH),
                       v_w[:, t].rearrange("p k (h d) -> p (k h) d", d=DH),
                       last(sc[:, t].rearrange("p k h -> p (k h)"), DH), ALU.mult)\
                        .then_inc(*did())
                dve.wait_ge(*did.latest())
                for t in range(2):
                    reduce(agg[:, t], prod_w[:, t].rearrange("p k c -> p c k"), ALU.add).then_inc(*did("agg"))
                dve.wait_ge(*filled("aggT"))
                o = result("aggT")
                copy(aggT.rearrange("p m w -> p (m w)"), o[:, :]).then_inc(*did("aggT_copied"))
                dve.wait_ge(*filled("proj"))
                o = result("proj")
                for m in range(CT):
                    stt(lo[:, m], o[:, m * NW:(m + 1) * NW], sm("la_proj_b", m), red[:, m], ALU.add, ALU.add)\
                        .then_inc(*did("lo" if m == CT - 1 else None))
                dve.wait_ge(*filled("mod"))
                o = result("mod")
                for m in range(CT):
                    ts(tokens(h[0])[:, m, :, 0:WIN],
                       o[:, m * NW:(m + 1) * NW].rearrange("p (b n) -> p b n", n=WIN), sm("mod_b", m), None,
                       ALU.add).then_inc(*did("patch_out" if m == CT - 1 else None))
                norm("lo", lo, NW, lon, "ga_ln_kv_g", "ga_ln_kv_b")
                dve.wait_ge(*filled("gs"))
                o = result("gs")
                four = o[:, :].rearrange("p (x n) -> p x n", n=WIN)
                gm_ = gm.rearrange("p m b -> p (m b)")
                gr_ = gr.rearrange("p m b -> p (m b)")
                gs_ = gs.rearrange("p m (b n) -> p (m b) n", n=WIN)
                gse_ = gse.rearrange("p m (b n) -> p (m b) n", n=WIN)
                reduce(gm_, four, ALU.max).then_inc(*did())
                dve.wait_ge(*did.latest())
                tt(gs_, four, last(gm_, WIN), ALU.subtract).then_inc(*did("gs_shift"))
                dve.wait_ge(S["gs_exp"], 1)
                reduce(gr_, gse_, ALU.add).then_inc(*did())
                dve.wait_ge(*did.latest())
                dve.reciprocal(gr_, gr_).then_inc(*did())
                dve.wait_ge(*did.latest())
                tt(gse_, gse_, last(gr_, WIN), ALU.mult).then_inc(*did())
                dve.wait_ge(*did.latest())
                dve.wait_ge(*filled("gv"))
                o = result("gv")
                tt(gs_, gse_, o[:, :].rearrange("p (x n) -> p x n", n=WIN), ALU.mult).then_inc(*did("gv_used"))
                dve.wait_ge(*did.latest())
                reduce(gaggT.rearrange("p m b -> p (m b)"), gs_, ALU.add).then_inc(*did("gagg"))
                dve.wait_ge(*filled("gproj"))
                o = result("gproj")
                for m in range(CT):
                    ts(tokens(h[0])[:, m, :, WIN], o[:, m * B:(m + 1) * B], sm("ga_proj_b", m), sm("class_emb", m),
                       ALU.add, ALU.add).then_inc(*did("cls_out" if m == CT - 1 else None))

            def state_space():
                flat = "p m n -> p (m n)"
                ts(negA, view(SM, SMALL["A_log"][0], DIT, NS), A_LOG_TOP, None, ALU.min).then_inc(*did("a_clip"))
                dve.wait_ge(S["a_exp"], 1)
                ts(negA, negA, -1.0, None, ALU.mult).then_inc(*did("a_neg"))
                for m in range(DIT):
                    dve.wait_ge(*filled(("win", m)))
                    o = result(("win", m))
                    src, dst = tokens(o[:, 0:N]), tokens(u_raw[:, m])
                    ts(u_raw[:, m], o[:, 0:N], sm("W_conv", 3 * m + 2), None, ALU.mult).then_inc(*did())
                    dve.wait_ge(*did.latest())
                    stt(dst[:, :, 1:], src[:, :, :L - 1], sm("W_conv", 3 * m + 1), dst[:, :, 1:], ALU.mult, ALU.add)\
                        .then_inc(*did())
                    dve.wait_ge(*did.latest())
                    stt(dst[:, :, 2:], src[:, :, :L - 2], sm("W_conv", 3 * m), dst[:, :, 2:], ALU.mult, ALU.add)\
                        .then_inc(*did("u_conv"))
                dve.wait_ge(*filled("xdbl"))
                o = result("xdbl")
                copy(xdbl, o[0:48, 0:N]).then_inc(*did("xdbl_copied"))
                for m in range(DIT):
                    dve.wait_ge(*filled(("wdt", m)))
                    o = result(("wdt", m))
                    ts(rz[:, m], o[:, 0:N], sm("b_dt", m), 0.0, ALU.add, ALU.max).then_inc(*did())
                    ts(az[:, m], o[:, 0:N], sm("b_dt", m), None, ALU.add).then_inc(*did("dt_relu"))
                dve.wait_ge(*did.latest())
                stt(az.rearrange(flat), rz.rearrange(flat), 2.0, az.rearrange(flat), ALU.mult, ALU.subtract)\
                    .then_inc(*did("dt_abs"))
                dve.wait_ge(S["dt_exp"], 1)
                ts(du, e1, 1.0, None, ALU.add).then_inc(*did("dt_exp1"))
                dve.wait_ge(*did.latest())
                ts(delta, du, -1.0, 1e-30, ALU.add, ALU.max).then_inc(*did())
                dve.wait_ge(*did.latest())
                dve.reciprocal(delta, delta).then_inc(*did())
                dve.wait_ge(*did.latest())
                dve.wait_ge(S["dt_log"], 1)
                tt(az, az, delta, ALU.mult).then_inc(*did())
                dve.wait_ge(*did.latest())
                stt(az.rearrange(flat), du.rearrange(flat), 1.0, az.rearrange(flat), ALU.is_equal, ALU.add)\
                    .then_inc(*did())
                dve.wait_ge(*did.latest())
                tt(az, az, e1, ALU.mult).then_inc(*did())
                dve.wait_ge(*did.latest())
                tt(delta, az, rz, ALU.add).then_inc(*did("delta"))
                dve.wait_ge(*did.latest())
                dve.wait_ge(S["u_silu"], 1)
                tt(du, delta, u, ALU.mult).then_inc(*did())
                dve.wait_ge(*did.latest())

                def dbu_of(n):
                    dve.wait_ge(*filled(("B", n)))
                    o = result(("B", n))
                    tt(dbu[n % 2], du, over(o[:, 0:N], DIT), ALU.mult).then_inc(*did("b_used"))

                dbu_of(0)
                for n in range(NS):
                    dve.wait_ge(S["b_used"], n + 1)
                    dve.wait_ge(S["decay"], n + 1)
                    dve.tensor_tensor_scan(hs[n % 2].rearrange(flat), arg[n % 2].rearrange(flat),
                                               dbu[n % 2].rearrange(flat), 0.0, ALU.mult, ALU.add).then_inc(*did("scanned"))
                    if n + 1 < NS:
                        dbu_of(n + 1)
                    dve.wait_ge(*filled(("C", n)))
                    o = result(("C", n))
                    dve.wait_ge(S["scanned"], n + 1)
                    if n >= 2:
                        dve.wait_ge(S["hc_added"], n - 1)
                    tt(hc[n % 2], hs[n % 2], over(o[:, 0:N], DIT), ALU.mult).then_inc(*did("hc"))
                for m in range(DIT):
                    dve.wait_ge(*filled(("y", m)))
                    o = result(("y", m))
                    stt(u_raw[:, m], u[:, m], sm("D_param", m), o[:, 0:N], ALU.mult, ALU.add).then_inc(*did("y_skip"))
                dve.wait_ge(S["res_silu"], DIT)
                for m in range(DIT):
                    dve.wait_ge(S["y_skip"], m + 1)
                    tt(u_raw[:, m], u_raw[:, m], sres[:, m], ALU.mult).then_inc(*did("y_out"))
                residual("wout", h[0], "z_mam")
                norm("ln0", z, N, h[1])

            def experts():
                dve.wait_ge(*filled("gate"))
                o = result("gate")
                copy(lg.rearrange("p t e -> p (t e)"), o[0:TN, 0:TT * NE]).then_inc(*did("gate_copied"))
                dve.wait_ge(*did.latest())
                reduce(gmax, lg, ALU.max).then_inc(*did())
                dve.wait_ge(*did.latest())
                tt(ex, lg, last(gmax, NE), ALU.subtract).then_inc(*did("gate_shift"))
                other, own = lg.unsqueeze(2).to_broadcast([TN, TT, NE, NE]), last(lg, NE)
                tt(cmp1, other, own, ALU.is_gt).then_inc(*did())
                tt(cmp2, other, own, ALU.is_equal).then_inc(*did())
                dve.wait_ge(*did.latest())
                c2 = cmp2.rearrange("p t e f -> p t (e f)")
                tt(c2, c2, over(sm("before", rows=TN), TT), ALU.mult).then_inc(*did())
                dve.wait_ge(*did.latest())
                tt(cmp1, cmp1, cmp2, ALU.add).then_inc(*did())
                dve.wait_ge(*did.latest())
                reduce(rank, cmp1, ALU.add).then_inc(*did())
                dve.wait_ge(*did.latest())
                dve.wait_ge(S["gate_exp"], 1)
                stt(ex, rank, 1.5, ex, ALU.is_lt, ALU.mult).then_inc(*did())
                dve.wait_ge(*did.latest())
                reduce(gsum, ex, ALU.add).then_inc(*did())
                dve.wait_ge(*did.latest())
                dve.reciprocal(grec, gsum).then_inc(*did())
                dve.wait_ge(*did.latest())
                tt(ex, ex, last(grec, NE), ALU.mult).then_inc(*did("comb"))
                dve.wait_ge(*filled("combT"))
                o = result("combT")
                copy(combT, o[0:NE, 0:N]).then_inc(*did("comb_copied"))
                for e in range(NE):
                    dve.wait_ge(S["combine_copied"], e + 1)
                    if e >= 2:
                        dve.wait_ge(S["act_used"], e - 1)
                    for m in range(HIDT):
                        i = e * HIDT + m
                        dve.wait_ge(S["silu_h"], i + 1)
                        dve.wait_ge(*filled(("W3", e, m)))
                        o = result(("W3", e, m))
                        tt(gated[i % 2], sil[i % 2], o[:, 0:N], ALU.mult).then_inc(*did("gated"))
                        dve.wait_ge(*did.latest())
                        tt(mixed[e % 2][:, m], gated[i % 2], combb[e % 2], ALU.mult).then_inc(*did("moe_act"))
                residual("moe", h[1], "z_moe")
                norm("ln1", z, N, h[0])

            def attention1():
                def table(name):
                    return sm(name).unsqueeze(1).to_broadcast([P, B, L])

                for m in range(CT):
                    dve.wait_ge(*filled(("q1", m)))
                    o = result(("q1", m))
                    tt(tokens(t1a)[:, m], tokens(o[:, 0:N]), table("cosq"), ALU.mult).then_inc(*did("rope1"))
                for m in range(CT):
                    dve.wait_ge(*filled(("q1r", m)))
                    o = result(("q1r", m))
                    tt(tokens(t1b)[:, m], tokens(o[:, 0:N]), table("sinq"), ALU.mult).then_inc(*did("rope1"))
                dve.wait_ge(*filled(("k1", 0)))
                o = result(("k1", 0))
                tt(tokens(kt1), tokens(o[:, 0:N]), table("cosk"), ALU.mult).then_inc(*did("rope1"))
                dve.wait_ge(*filled(("k1r", 0)))
                o = result(("k1r", 0))
                tt(tokens(kt2), tokens(o[:, 0:N]), table("sink"), ALU.mult).then_inc(*did("rope1"))
                dve.wait_ge(*did.latest())
                tt(q1, t1a, t1b, ALU.add).then_inc(*did())
                tt(k1, kt1, kt2, ALU.add).then_inc(*did())
                dve.wait_ge(*did.latest())
                for d in LAGS:
                    tt(pr1[d].rearrange("p m (b l) -> p m b l", l=L - d), tokens(q1)[:, :, :, d:],
                       over(tokens(k1)[:, :, :L - d], CT), ALU.mult).then_inc(*did("s1_prod"))
                dve.wait_ge(S["s1_copied"], CT * L)
                reduce(s1m, s1, ALU.max).then_inc(*did())
                dve.wait_ge(*did.latest())
                tt(s1, s1, last(s1m, L), ALU.subtract).then_inc(*did("s1_shift"))
                dve.wait_ge(S["s1_exp"], 1)
                reduce(s1s, s1e, ALU.add).then_inc(*did())
                dve.wait_ge(*did.latest())
                dve.reciprocal(s1r, s1s).then_inc(*did())
                dve.wait_ge(*did.latest())
                dve.wait_ge(S["v1_copied"], 1)
                by = s1e.rearrange("p (m b l) d -> p m b l d", m=CT, l=L)
                ov, tv = tokens(o1), tokens(t1)
                tt(ov, by[:, :, :, :, 0], over(tokens(v1), CT), ALU.mult).then_inc(*did())
                for d in range(1, L):
                    tt(tv[:, :, :, d:], by[:, :, :, d:, d], over(tokens(v1)[:, :, :L - d], CT), ALU.mult)\
                        .then_inc(*did())
                    dve.wait_ge(*did.latest())
                    tt(ov[:, :, :, d:], ov[:, :, :, d:], tv[:, :, :, d:], ALU.add).then_inc(*did())
                    dve.wait_ge(*did.latest())
                tt(o1, o1, s1r.rearrange("p (m n) -> p m n", m=CT), ALU.mult).then_inc(*did("a1_out"))
                residual("wo1", h[0], "z_attn1")
                norm("ln2", z, N, h[1])

            def ternary():
                dve.wait_ge(S["packed_in"], 16)
                wi = wint[:, :].rearrange("p (c r) -> p c r", c=2)
                we = wenc[:, :].rearrange("p (c o) -> p c o", c=2)
                for k in range(4):
                    ts(we[:, :, k * 64:(k + 1) * 64], wi, 2 * k, 3, ALU.logical_shift_right, ALU.bitwise_and)\
                        .then_inc(*did())
                dve.wait_ge(*did.latest())
                ts(wT[:, :], wenc[:, :], -1.0, None, ALU.add).then_inc(*did())
                for t in range(TT):
                    dve.wait_ge(*filled(("xtok", t)))
                    o = result(("xtok", t))
                    copy(x_tok[:, t], o[0:TN, 0:C]).then_inc(*did("x_tok_copied"))
                dve.wait_ge(*did.latest())
                dve.tensor_reduce(amax, x_tok, AX.X, ALU.max, apply_absolute_value=True).then_inc(*did())
                dve.wait_ge(*did.latest())
                ts(amax, amax, 1e-5, None, ALU.max).then_inc(*did())
                dve.wait_ge(*did.latest())
                dve.reciprocal(asc, amax).then_inc(*did())
                dve.wait_ge(*did.latest())
                ts(asc, asc, 127.0, None, ALU.mult).then_inc(*did())
                ts(ainv, amax, 1.0 / 127.0, sm("l1_scale", 0, TN), ALU.mult, ALU.mult).then_inc(*did())
                dve.wait_ge(*did.latest())
                for t in range(TT):
                    ts(xq[:, t], x_tok[:, t], asc[:, t:t + 1], MAGIC, ALU.mult, ALU.add).then_inc(*did())
                dve.wait_ge(*did.latest())
                ts(xq, xq, -MAGIC, 127.0, ALU.add, ALU.min).then_inc(*did())
                dve.wait_ge(*did.latest())
                ts(xq, xq, -128.0, None, ALU.max).then_inc(*did("x_int"))
                for m in range(CT):
                    dve.wait_ge(*filled(("xint", m)))
                    o = result(("xint", m))
                    copy(xqT[:, m * N:(m + 1) * N], o[:, 0:N]).then_inc(*did("xint_copied"))
                for t in range(TT):
                    dve.wait_ge(*filled(("l1f", t)))
                    o = result(("l1f", t))
                    stt(y_tok[:, t], o[0:TN, 0:C], ainv[:, t:t + 1], sm("l1_bias", rows=TN), ALU.mult, ALU.add)\
                        .then_inc(*did("l1f_read"))
                dve.wait_ge(*did.latest())
                tt(y_tok, y_tok, x_tok, ALU.add).then_inc(*did())
                dve.wait_ge(*did.latest())
                for t in range(TT):
                    dve.bn_stats(stats[:, t], y_tok[:, t]).then_inc(*did())
                dve.wait_ge(*did.latest())
                for t in range(TT):
                    dve.bn_aggr(aggr[:, t], stats[:, t]).then_inc(*did("l1f_var" if t == TT - 1 else None))
                dve.wait_ge(S["l1f_rstd"], 1)
                for t in range(TT):
                    ts(y_tok[:, t], y_tok[:, t], aggr[:, t, 0:1], trs[:, t:t + 1], ALU.subtract, ALU.mult)\
                        .then_inc(*did("h4_tok" if t == TT - 1 else None))
                for m in range(CT):
                    dve.wait_ge(*filled(("h4", m)))
                    o = result(("h4", m))
                    copy(h[0][:, m], o[:, 0:N]).then_inc(*did("h4_copied"))

            def attention2():
                for m in range(QT2):
                    dve.wait_ge(*filled(("k2", m)))
                    o = result(("k2", m))
                    copy(k2[:, m], o[:, 0:N]).then_inc(*did("k2_copied"))

                def shifted(t):
                    for g in range(4):
                        dve.wait_ge(*filled(("s2", t, g)))
                        o = result(("s2", t, g))
                        tt(s2[:, t, 4 * g:4 * g + 4], o[0:TN, 0:4 * TN].rearrange("p (h k) -> p h k", h=4),
                           over(sm("attmask", rows=TN), 4), ALU.add)\
                            .then_inc(*did("s2_masked"))
                    dve.wait_ge(*did.latest())
                    reduce(s2m[:, t], s2[:, t], ALU.max).then_inc(*did())
                    dve.wait_ge(*did.latest())
                    tt(s2[:, t], s2[:, t], last(s2m[:, t], TN), ALU.subtract).then_inc(*did("s2_shift"))

                def weights(t):
                    dve.wait_ge(S["s2_exp"], t + 1)
                    reduce(s2s[:, t], s2[:, t], ALU.add).then_inc(*did())
                    dve.wait_ge(*did.latest())
                    dve.reciprocal(s2r[:, t], s2s[:, t]).then_inc(*did())
                    dve.wait_ge(*did.latest())
                    tt(s2[:, t], s2[:, t], last(s2r[:, t], TN), ALU.mult).then_inc(*did("s2_prob"))

                shifted(0)
                for t in range(TT):
                    if t + 1 < TT:
                        shifted(t + 1)
                    weights(t)
                    for g in range(2):
                        dve.wait_ge(*filled(("o2", t, g)))
                        o = result(("o2", t, g))
                        copy(o2[:, 4 * g:4 * g + 4, t * TN:(t + 1) * TN],
                             o[:, 0:4 * TN].rearrange("p (m q) -> p m q", m=4))\
                            .then_inc(*did("o2_copied"))
                residual("r2", h[0], "z_attn2")
                norm("ln4", z, N, h[1])

            def coupling():
                dve.wait_ge(*did.latest())
                for m in range(CT):
                    reduce(gmn[:, m], tokens(h[1])[:, m], ALU.add).then_inc(*did())
                dve.wait_ge(*did.latest())
                ts(r2[:, 0:1], sm("gc_b3"), 0.5, None, ALU.mult).then_inc(*did())
                ts(r2[:, 1:2], sm("cn_b4"), 0.5, None, ALU.mult).then_inc(*did())
                ts(gmn, gmn, 1.0 / L, None, ALU.mult).then_inc(*did("gmean"))
                dve.wait_ge(S["gc_act"], 3)
                ts(gf, gf, 0.7, None, ALU.mult).then_inc(*did())
                dve.wait_ge(*did.latest())
                for cyc in range(3):
                    x = h[1] if cyc == 0 else cout[(cyc - 1) % 2]
                    y = cout[cyc % 2]
                    dve.wait_ge(S["c4_act"], cyc + 1)
                    stt(tokens(coup), tokens(cn_t), 0.3, last(gf, L), ALU.mult, ALU.add).then_inc(*did())
                    dve.wait_ge(*did.latest())
                    ts(coup, coup, sm("range"), 0.1, ALU.mult, ALU.add).then_inc(*did())
                    dve.wait_ge(*did.latest())
                    ts(coup, coup, sm("sign"), None, ALU.mult).then_inc(*did())
                    dve.wait_ge(*did.latest())
                    tt(ctmp[:, 0], coup, x[:, 1], ALU.mult).then_inc(*did())
                    tt(ctmp[:, 1], coup, x[:, 0], ALU.mult).then_inc(*did())
                    dve.wait_ge(*did.latest())
                    tt(y[:, 0], x[:, 0], ctmp[:, 0], ALU.add).then_inc(*did())
                    tt(y[:, 1], x[:, 1], ctmp[:, 1], ALU.subtract).then_inc(*did("c_out"))
                dve.wait_ge(*did.latest())
                tt(z, h[1], cout[0], ALU.add).then_inc(*did("z_ffn2"))
                norm("ln5", z, N, h[0])

            def attention3():
                for m in range(CT):
                    dve.wait_ge(*filled(("gk2", m)))
                    o = result(("gk2", m))
                    ts(gmin[:, m], o[:, 0:N], sm("bgk2", m), 0.0, ALU.add, ALU.min).then_inc(*did())
                    ts(gaz[:, m], o[:, 0:N], sm("bgk2", m), None, ALU.add).then_inc(*did("gk_min"))
                dve.wait_ge(*did.latest())
                stt(gaz, gmin, -2.0, gaz, ALU.mult, ALU.add).then_inc(*did("gk_abs"))
                dve.wait_ge(S["gk_log"], 1)
                tt(gmin, gmin, gaz, ALU.subtract).then_inc(*did())
                dve.wait_ge(*did.latest())
                ts(gmin, gmin, 1.0 / 16.0, None, ALU.mult).then_inc(*did())
                dve.wait_ge(*did.latest())
                dve.wait_ge(S["keep_set"], 1)
                dve.tensor_tensor_scan(gcum.rearrange("p m n -> p (m n)"), keep, gmin.rearrange("p m n -> p (m n)"),
                                           0.0, ALU.mult, ALU.add).then_inc(*did())
                dve.wait_ge(*did.latest())
                gt, qt, kt = tokens(gcum), tokens(q3), tokens(k3)
                for d in range(1, L):
                    tt(gdf_d[d].rearrange("p m (b l) -> p m b l", l=L - d), gt[:, :, :, d:], gt[:, :, :, :L - d],
                       ALU.subtract).then_inc(*did("g_diff" if d == L - 1 else None))
                dve.wait_ge(S["qkv3_copied"], 2 * CT)
                for d in LAGS:
                    dst = pr3_d[d].rearrange("p m (b l) -> p m b l", l=L - d)
                    tt(dst, qt[:, :, :, d:], kt[:, :, :, :L - d], ALU.mult)\
                        .then_inc(*did("s3_prod" if d == 0 else None))
                    if d:
                        if d == 1:
                            dve.wait_ge(S["g_exp"], 1)
                        dve.wait_ge(*did.latest())
                        tt(pr3_d[d], pr3_d[d], gdf_d[d], ALU.mult).then_inc(*did("s3_prod"))
                dve.wait_ge(S["qkv3_copied"], 2 * CT + 4)
                adds = []
                for d in LAGS:
                    for hd in range(4):
                        dve.wait_ge(*filled(("s3", d, hd)))
                        o = result(("s3", d, hd))
                        i = 4 * d + hd
                        vt = tokens(v3[:, hd])[:, :, :L - d]
                        dst = tokens(o3[:, hd])[:, :, d:]
                        src = o[:, 0:B * (L - d)].rearrange("p (b l) -> p b l", l=L - d)
                        tmp = dst if d == 0 else tokens(t3[i % 4])[:, :, d:]
                        tt(tmp, src, vt, ALU.mult).then_inc(*did("s3_mul"))
                        if adds:
                            a_dst, a_tmp, a_i = adds.pop()
                            dve.wait_ge(S["s3_mul"], a_i + 1)
                            tt(a_dst, a_dst, a_tmp, ALU.add).then_inc(*did())
                        if d:
                            adds.append((dst, tmp, i))
                a_dst, a_tmp, a_i = adds.pop()
                dve.wait_ge(S["s3_mul"], a_i + 1)
                tt(a_dst, a_dst, a_tmp, ALU.add).then_inc(*did("o3_sum"))
                dve.wait_ge(S["o3_rstd"], 1)
                flat = "p m n -> p (m n)"
                stt(o3.rearrange(flat), o3.rearrange(flat), sm("gnorm"), rs3.rearrange(flat), ALU.mult, ALU.mult)\
                    .then_inc(*did())
                dve.wait_ge(*did.latest())
                dve.wait_ge(S["g3_silu"], 4)
                tt(o3, o3, sg3, ALU.mult).then_inc(*did("o3_out"))
                residual("wo3", h[0], "z_attn3")
                norm("ln6", z, N, h[1])

            def last_ffn():
                for m in range(HT3):
                    dve.wait_ge(S["f1_silu"], m + 1)
                    dve.wait_ge(*filled(("w2", m)))
                    o = result(("w2", m))
                    stt(fa[:, m], o[:, 0:N], sm("w2_s", m), fsil[m % 2], ALU.mult, ALU.mult).then_inc(*did("f_gate"))
                for m in range(CT):
                    dve.wait_ge(*filled(("f3", m)))
                    o = result(("f3", m))
                    stt(z[:, m], o[:, 0:N], sm("w3_s", m), h[1][:, m], ALU.mult, ALU.add).then_inc(*did("z_ffn3"))
                norm("ln7", z, N, h[0])
                for t in range(TT):
                    dve.wait_ge(*filled(("out", t)))
                    o = result(("out", t))
                    copy(otok[:, t], o[0:TN, 0:C]).then_inc(*did("tok_out"))

            for f in [tokenizer, state_space, experts, attention1, ternary, attention2, coupling, attention3, last_ffn]:
                f()

        @block.scalar
        def _(act):
            did = Counts(S, "act_step")
            act_fn = act.activation

            ln_at = [0]

            def norm(key, n):
                i = ln_at[0] = ln_at[0] + 1
                act.wait_ge(S["ln_xc"], i)
                act_fn(sq[:, :, 0:n], xc[:, :, 0:n], ACT.Square).then_inc(*did("ln_sq"))
                act.wait_ge(*filled((key, "var")))
                var = result((key, "var"))[:, 0:n]
                act_fn(SQ[:, 0:n], var, ACT.Ln, bias=sm("eps")).then_inc(*did("ln_logvar"))
                act.wait_ge(*did.latest())
                act_fn(SQ[:, N:N + n], SQ[:, 0:n], ACT.Exp, scale=-0.5).then_inc(*did("ln_rstd"))

            def tokenizer():
                act.wait_ge(S["small_in"], 16)
                norm("cls", 1)
                for j in range(NCH + 2):
                    if j < NCH:
                        n = min(CHUNK, NP - j * CHUNK)
                        act.wait_ge(*filled(("conv", j, 1)))
                        o = result(("conv", j, 1))
                        act_fn(pe_all[:, 1, j * CHUNK:j * CHUNK + n], o[:, 0:n], ACT.Copy)\
                            .then_inc(*did("pe1_copied"))
                    if 1 <= j <= NCH:
                        i = j - 1
                        n = min(CHUNK, NP - i * CHUNK)
                        c = slice(i * CHUNK, i * CHUNK + n)
                        act.wait_ge(S["w_xc"], i + 1)
                        act_fn(sq_all[:, :, c], xn_all[:, :, c], ACT.Square).then_inc(*did("w_sq"))
                    if j >= 2:
                        i = j - 2
                        n = min(CHUNK, NP - i * CHUNK)
                        act.wait_ge(*filled(("wvar", i)))
                        o = result(("wvar", i))
                        if i:
                            act.wait_ge(S["w_rstd"], i)
                        act_fn(w_log[:, 0:n], o[:, 0:n], ACT.Ln, bias=sm("eps")).then_inc(*did("w_logvar"))
                        act.wait_ge(*did.latest())
                        if i:
                            act.wait_ge(S["w_xn"], i)
                        act_fn(w_rs[:, 0:n], w_log[:, 0:n], ACT.Exp, scale=-0.5).then_inc(*did("w_rstd"))
                norm("red", NW)
                for t in range(2):
                    act.wait_ge(*filled(("q", t)))
                    o = result(("q", t))
                    act_fn(q_w[:, t], o[:, 0:C], ACT.Copy, scale=float(C) ** -0.5).then_inc(*did("q_copied"))
                i = 0
                for k in range(TAPS):
                    for t in range(2):
                        i += 1
                        act.wait_ge(S["kq_done"], i)
                        act.wait_ge(*filled(("kv", k, t)))
                        o = result(("kv", k, t))
                        act_fn(v_w[:, t, k], o[:, C:2 * C], ACT.Copy).then_inc(*did("v_copied"))
                act.wait_ge(S["la_shift"], 1)
                act_fn(sc_e, sc_e, ACT.Exp).then_inc(*did("la_exp"))
                norm("lo", NW)
                act.wait_ge(*filled("gk"))
                o = result("gk")
                act_fn(gkT.rearrange("p m w -> p (m w)"), o[:, :], ACT.Copy).then_inc(*did("gk_copied"))
                act.wait_ge(S["gs_shift"], 1)
                act_fn(gse, gs, ACT.Exp).then_inc(*did("gs_exp"))

            def state_space():
                act.wait_ge(S["a_clip"], 1)
                act_fn(negA, negA, ACT.Exp).then_inc(*did("a_exp"))
                act.wait_ge(S["u_conv"], DIT)
                act_fn(u, u_raw, ACT.Silu).then_inc(*did("u_silu"))
                for m in range(DIT):
                    act.wait_ge(*filled(("win", DIT + m)))
                    o = result(("win", DIT + m))
                    act_fn(sres[:, m], o[:, 0:N], ACT.Silu).then_inc(*did("res_silu"))
                act.wait_ge(S["dt_abs"], 1)
                act_fn(e1, az, ACT.Exp, scale=-1.0).then_inc(*did("dt_exp"))
                act.wait_ge(S["dt_exp1"], 1)
                act_fn(az, du, ACT.Ln).then_inc(*did("dt_log"))
                for n in range(NS):
                    act.wait_ge(S["arg"], n + 1)
                    if n == 0:
                        act.wait_ge(S["arg_zero"], 2)
                    a = arg[n % 2].rearrange("p m (b l) -> p (m b) l", l=L)[:, :, 1:]
                    act_fn(a, a, ACT.Exp).then_inc(*did("decay"))
                norm("ln0", N)

            def experts():
                act.wait_ge(S["gate_shift"], 1)
                act_fn(ex, ex, ACT.Exp).then_inc(*did("gate_exp"))
                for e in range(NE):
                    act.wait_ge(*filled(("comb", e)))
                    o = result(("comb", e))
                    if e >= 2:
                        act.wait_ge(S["moe_act"], HIDT * (e - 1))
                    act_fn(combb[e % 2], o[:, 0:N], ACT.Copy).then_inc(*did("combine_copied"))
                    for m in range(HIDT):
                        i = e * HIDT + m
                        act.wait_ge(*filled(("W1", e, m)))
                        o = result(("W1", e, m))
                        if i >= 2:
                            act.wait_ge(S["gated"], i - 1)
                        act_fn(sil[i % 2], o[:, 0:N], ACT.Silu).then_inc(*did("silu_h"))
                norm("ln1", N)

            def attention1():
                act.wait_ge(*filled(("v1", 0)))
                o = result(("v1", 0))
                act_fn(v1, o[:, 0:N], ACT.Copy).then_inc(*did("v1_copied"))
                act.wait_ge(S["s1_clear"], 1)
                by = s1.rearrange("p (m b l) d -> p m b l d", m=CT, l=L)
                for d in LAGS:
                    for m in range(CT):
                        act.wait_ge(*filled(("s1", d, m)))
                        o = result(("s1", d, m))
                        act_fn(by[:, m, :, d:, d], o[:, 0:B * (L - d)].rearrange("p (b l) -> p b l", l=L - d),
                               ACT.Copy).then_inc(*did("s1_copied"))
                act.wait_ge(S["s1_shift"], 1)
                act_fn(s1e, s1, ACT.Exp).then_inc(*did("s1_exp"))
                norm("ln2", N)

            def ternary():
                act.wait_ge(S["l1f_var"], 1)
                act_fn(tmean, aggr[:, :, 1], ACT.Ln, bias=sm("eps", rows=TN)).then_inc(*did())
                act.wait_ge(*did.latest())
                act_fn(trs, tmean, ACT.Exp, scale=-0.5).then_inc(*did("l1f_rstd"))

            def attention2():
                for m in range(QT2):
                    act.wait_ge(*filled(("q2", m)))
                    o = result(("q2", m))
                    act_fn(q2[:, m], o[:, 0:N], ACT.Copy, scale=float(HD2) ** -0.5).then_inc(*did("q2_copied"))
                for t in range(TT):
                    for hf in range(2):
                        act.wait_ge(*filled(("v2", t, hf)))
                        o = result(("v2", t, hf))
                        act_fn(v2[:, t, hf * 512:(hf + 1) * 512], o[0:TN, :], ACT.Copy).then_inc(*did("v2_copied"))
                    act.wait_ge(S["s2_shift"], t + 1)
                    act_fn(s2[:, t], s2[:, t], ACT.Exp).then_inc(*did("s2_exp"))
                    for g in range(4):
                        act.wait_ge(*filled(("pT", t, g)))
                        o = result(("pT", t, g))
                        act_fn(pT[t % 2][:, 4 * g:4 * g + 4], o[0:TN, 0:4 * TN].rearrange("p (h q) -> p h q", h=4),
                               ACT.Copy).then_inc(*did("pT_copied"))
                norm("ln4", N)

            def coupling():
                act.wait_ge(*filled("gc1"))
                o = result("gc1")
                act_fn(gc_a, o[:, 0:B], ACT.Gelu, bias=sm("gc_b1")).then_inc(*did("gc_act"))

                def first(cyc):
                    for m in range(CT):
                        act.wait_ge(*filled(("c1", cyc, m)))
                        o = result(("c1", cyc, m))
                        act_fn(cn_a[:, m], o[:, 0:N], ACT.Gelu, bias=sm("cn_b1", m)).then_inc(*did("c1_act"))

                first(0)
                act.wait_ge(*filled("gc2"))
                o = result("gc2")
                act_fn(gc_b, o[0:64, 0:B], ACT.Gelu, bias=sm("gc_b2", rows=64)).then_inc(*did("gc_act"))
                act.wait_ge(*filled("gc3"))
                o = result("gc3")
                act_fn(gf, o[:, 0:B], ACT.Tanh, scale=0.5, bias=r2[:, 0:1]).then_inc(*did("gc_act"))
                for cyc in range(3):
                    if cyc:
                        first(cyc)
                    act.wait_ge(*filled(("c2", cyc)))
                    o = result(("c2", cyc))
                    act_fn(cn_b, o[:, 0:N], ACT.Gelu, bias=sm("cn_b2")).then_inc(*did("c2_act"))
                    act.wait_ge(*filled(("c3", cyc)))
                    o = result(("c3", cyc))
                    act_fn(cn_c, o[0:64, 0:N], ACT.Gelu, bias=sm("cn_b3", rows=64)).then_inc(*did("c3_act"))
                    act.wait_ge(*filled(("c4", cyc)))
                    o = result(("c4", cyc))
                    act_fn(cn_t, o[:, 0:N], ACT.Tanh, scale=0.5, bias=r2[:, 1:2]).then_inc(*did("c4_act"))
                norm("ln5", N)

            def attention3():
                act.wait_ge(*filled("gk1"))
                o = result("gk1")
                act_fn(gk1, o[0:RANK, 0:N], ACT.Copy).then_inc(*did("gk1_copied"))
                for m in range(CT):
                    act.wait_ge(*filled(("q3", m)))
                    o = result(("q3", m))
                    act_fn(q3[:, m], o[:, 0:N], ACT.Copy, scale=0.125).then_inc(*did("qkv3_copied"))
                for m in range(CT):
                    act.wait_ge(*filled(("k3", m)))
                    o = result(("k3", m))
                    act_fn(k3[:, m], o[:, 0:N], ACT.Copy).then_inc(*did("qkv3_copied"))
                act.wait_ge(S["gk_abs"], 1)
                act_fn(gaz, gaz, ACT.Exp, scale=-1.0).then_inc(*did("gk_exp"))
                act.wait_ge(*did.latest())
                act_fn(gaz, gaz, ACT.Ln, bias=sm("one")).then_inc(*did("gk_log"))
                for m in range(4):
                    act.wait_ge(*filled(("v3", m)))
                    o = result(("v3", m))
                    act_fn(v3[:, m], o[:, 0:N], ACT.Copy).then_inc(*did("qkv3_copied"))
                act.wait_ge(S["g_diff"], 1)
                late = view(PAT, A3 + 640 + CT * PAIR_OFF[1], CT * (PAIRS - PAIR_OFF[1]))
                act_fn(late, late, ACT.Exp).then_inc(*did("g_exp"))
                for m in range(4):
                    act.wait_ge(*filled(("g3", m)))
                    o = result(("g3", m))
                    act_fn(sg3[:, m], o[:, 0:N], ACT.Silu).then_inc(*did("g3_silu"))
                act.wait_ge(S["o3_sum"], 1)
                act_fn(osq, o3, ACT.Square).then_inc(*did("o3_sq"))
                for hd in range(4):
                    act.wait_ge(*filled(("ms3", hd)))
                    o = result(("ms3", hd))
                    act_fn(rs3[:, hd], o[:, 0:N], ACT.Ln, bias=sm("eps")).then_inc(*did("o3_logvar"))
                act.wait_ge(*did.latest())
                act_fn(rs3, rs3, ACT.Exp, scale=-0.5).then_inc(*did("o3_rstd"))
                norm("ln6", N)

            def last_ffn():
                for m in range(HT3):
                    act.wait_ge(*filled(("w1", m)))
                    o = result(("w1", m))
                    if m >= 2:
                        act.wait_ge(S["f_gate"], m - 1)
                    act_fn(fsil[m % 2], o[:, 0:N], ACT.Silu, scale=sm("w1_s", m)).then_inc(*did("f1_silu"))
                for m in range(HT3):
                    act.wait_ge(*filled(("h1", m)))
                    o = result(("h1", m))
                    act_fn(fb[:, m], o[:, 0:N], ACT.Gelu, scale=sm("h1_s", m)).then_inc(*did("fh1_act"))
                for m in range(HT3):
                    act.wait_ge(*filled(("h2", m)))
                    o = result(("h2", m))
                    act_fn(fa[:, m], o[:, 0:N], ACT.Gelu, scale=sm("h2_s", m)).then_inc(*did("fh2_act"))
                norm("ln7", N)

            for f in [tokenizer, state_space, experts, attention1, ternary, attention2, coupling, attention3, last_ffn]:
                f()

        @block.gpsimd
        def _(pool):
            did = Counts(S, "pool_step")

            def state_space():
                pool.wait_ge(S["cls_out"], 1)
                for i in range(2):
                    pool.memset(arg[i], 0.0).then_inc(*did("arg_zero"))
                pool.wait_ge(*did.latest())
                pool.wait_ge(S["a_neg"], 1)
                pool.wait_ge(S["delta"], 1)
                for n in range(NS):
                    if n >= 2:
                        pool.wait_ge(S["scanned"], n - 1)
                    for m in range(DIT):
                        pool.tensor_scalar(tokens(arg[n % 2][:, m])[:, :, 1:], tokens(delta[:, m])[:, :, 1:],
                                                 negA[:, m, n:n + 1], EXP_FLOOR, ALU.mult, ALU.max).then_inc(*did("arg" if m == DIT - 1 else None))

            def attention1():
                pool.wait_ge(S["z_moe"], CT)
                pool.memset(s1, FAR).then_inc(*did("s1_clear"))

            def attention3():
                pool.wait_ge(S["z_attn2"], CT)
                pool.memset(keep, 1.0).then_inc(*did())
                pool.wait_ge(*did.latest())
                pool.memset(keep.rearrange("p (x l) -> p x l", l=L)[:, :, 0], 0.0).then_inc(*did("keep_set"))

            for f in (state_space, attention1, attention3):
                f()

        @block.sync
        def _(sync):
            def load(dst, src, signal):
                sync.dma_start(dst, src).then_inc(S[signal], 16)

            load(SM[:, :], small, "small_in")
            nconv = KCT * C
            load(WTOK[:, 0:nconv], w_tok[:, 0:nconv], "conv_w_in")
            for j in range(NCH):
                n = min(CHUNK, NP - j * CHUNK)
                for k in range(KCT):
                    r = min(P, KC - k * P)
                    load(PAT[0:r, k * NP + j * CHUNK:k * NP + j * CHUNK + n],
                         patches[k * P:k * P + r, j * CHUNK:j * CHUNK + n], f"patches_in_{j}")
            load(WTOK[:, nconv:N_TOK], w_tok[:, nconv:], "tok_w_in")
            load(WMAM[:, 0:N_MAM], w_mam, "mam_w_in")
            load(wint[:, :], packed, "packed_in")
            sync.wait_ge(S["cls_out"], 1)
            for i in range(NE // 2):
                c = slice(2 * i * N_EXP, 2 * (i + 1) * N_EXP)
                sync.dma_start(BIG[:, c], w_exp[:, c]).then_inc(expert_in[i], 16)
            sync.wait_ge(S["z_mam"], CT)
            load(PAT[:, N_L2:N_L2 + N_L1], w_l1, "l1_w_in")
            load(PAT[:, 0:N_L2], w_l2, "l2_w_in")
            load(WMAM[:, 0:N_F3], w_f3, "f3_w_in")
            load(WTOK[:, 0:N_F1], w_f1, "f1_w_in")
            sync.wait_ge(S["z_attn2"], CT)
            load(PAT[:, 0:N_L3], w_l3, "l3_w_in")
            half = N_FH // 2
            for i in range(2):
                load(BIG[:, i * half:(i + 1) * half], w_fh[:, i * half:(i + 1) * half], "fh_w_in")
            for t in range(TT):
                sync.wait_ge(S["tok_out"], t + 1)
                sync.dma_start(out[t * TN:(t + 1) * TN, :], otok[:, t]).then_inc(S["stored"], 16)
            sync.wait_ge(S["stored"], 16 * TT)


def layout(x):
    def cols(v):
        return np.ascontiguousarray(v.reshape(-1, P).T)

    def wt(w):
        k = w.shape[0] // P
        return w.reshape(k, P, w.shape[1]).transpose(1, 0, 2).reshape(P, -1)

    def low(w):
        return np.concatenate([w, np.zeros((P - w.shape[0], w.shape[1]), w.dtype)])

    def rep(v):
        return np.broadcast_to(v.reshape(1, -1), (P, v.size))

    f = np.float32
    p = np.arange(P)
    pos = np.arange(L, dtype=np.float64)
    freq = 1.0 / 1000.0 ** (np.arange(0, HD1, 2) / HD1)
    ang = pos[None, :] * freq[p % 8][:, None]
    side = np.where(p % HD1 < 8, -1.0, 1.0)[:, None]
    tok = np.arange(TN)
    same = (tok[:, None] // L) == (tok[None, :] // L)
    mask = np.where(same, np.where(tok[None, :] > tok[:, None], -50.0, 0.0), FAR)
    e = np.arange(NE)
    g = {k: v for k, v in x.items()}
    parts = {
        "ident": np.eye(P), "same32": p[:, None] // 32 == p[None] // 32, "same16": p[:, None] // 16 == p[None] // 16,
        "inv256": np.full((P, 1), 1 / 256), "inv128": np.full((P, 1), 1 / 128), "one": np.ones((P, 1)),
        "eps": np.full((P, 1), EPS), "sign": np.where(p < 64, 1.0, -1.0)[:, None],
        "before": rep((e[None, :] < e[:, None]).astype(f)), "cosq": np.cos(ang) / 4, "sinq": side * np.sin(ang) / 4,
        "cosk": np.cos(ang), "sink": side * np.sin(ang), "attmask": low(mask),
        "W_conv": g["L0_attn_W_conv"].reshape(4, P, 3).transpose(1, 0, 2).reshape(P, 12),
        "b_dt": cols(g["L0_attn_b_dt"]), "A_log": g["L0_attn_A_log"].reshape(4, P, NS).transpose(1, 0, 2).reshape(P, 64),
        "D_param": cols(g["L0_attn_D_param"]), "Wr": wt(g["L0_ffn_Wr"]),
        "l1_bias": rep(g["L1_ffn_bias"]), "l1_scale": rep(g["L1_ffn_weight_scale"]),
        "cn_b1": cols(g["L2_ffn_cn_b1"]), "cn_b2": cols(g["L2_ffn_cn_b2"]), "cn_b3": low(g["L2_ffn_cn_b3"].reshape(-1, 1)),
        "cn_b4": rep(g["L2_ffn_cn_b4"]), "gc_b1": cols(g["L2_ffn_gc_b1"]), "gc_b2": low(g["L2_ffn_gc_b2"].reshape(-1, 1)),
        "gc_b3": rep(g["L2_ffn_gc_b3"]), "range": rep(g["L2_ffn_adaptive_range"]), "bgk2": cols(g["L3_attn_bgk2"]),
        "gnorm": g["L3_attn_g_norm_weight"].reshape(P, 1), "w1_s": cols(g["L3_ffn_w1_s"]), "w2_s": cols(g["L3_ffn_w2_s"]),
        "h1_s": cols(g["L3_ffn_h1_s"]), "h2_s": cols(g["L3_ffn_h2_s"]), "w3_s": cols(g["L3_ffn_w3_s"]),
    }
    for n in ("la_ln_q_g", "la_ln_q_b", "la_ln_kv_g", "la_ln_kv_b", "la_proj_b", "ga_ln_q_g", "ga_ln_q_b", "ga_ln_kv_g",
              "ga_ln_kv_b", "ga_proj_b", "mod_b", "class_emb"):
        parts[n] = cols(g["L0_tok_" + n])
    small = np.concatenate([np.asarray(parts[n]).astype(f) if parts[n].dtype != f else parts[n] for n in SMALL], axis=1)
    im = g["x"][:, :, :84, :84].reshape(B, 3, 2, 3, PATCH, 2, 3, PATCH)
    patches = im.transpose(1, 4, 7, 3, 6, 0, 2, 5).reshape(KC, NP)
    conv = g["L0_tok_conv_w"].reshape(C, KC).T
    conv = np.concatenate([conv, np.zeros((KCT * P - KC, C), f)])
    t = "L0_tok_"
    w_tok = [wt(conv)] + [wt(g[t + n]) for n in ("la_wq", "la_wkv", "la_proj_w", "ga_wq", "ga_wkv", "ga_proj_w", "mod_w")]
    a = "L0_attn_"
    w_mam = [wt(g[a + "W_in"]), wt(g[a + "W_x"]), low(g[a + "W_dt"]), wt(g[a + "W_out"])]
    w_exp = [wt(g["L0_ffn_" + n][i]) for i in range(NE) for n in ("W1", "W3", "W2")]
    w_l2 = [wt(g["L2_attn_" + n]) for n in ("Wq", "Wk", "Wv", "Wr")]
    straight = np.concatenate([np.arange(0, HD1, 2), np.arange(1, HD1, 2)])
    turned = np.concatenate([np.arange(1, HD1, 2), np.arange(0, HD1, 2)])
    heads = np.arange(H16)[:, None] * HD1
    wq, wk, wv = g["L1_attn_wq"].T, g["L1_attn_wk"], g["L1_attn_wv"]
    w_l1 = [wt(wq[:, (heads + straight).reshape(-1)]), wt(wq[:, (heads + turned).reshape(-1)]),
            wt(np.tile(wk[:, straight], (1, 8))), wt(np.tile(wk[:, turned], (1, 8))), wt(np.tile(wv, (1, 8))),
            wt(g["L1_attn_wo"].T)]
    w_f1 = [wt(g["L3_ffn_w1_w"].T), wt(g["L3_ffn_w2_w"].T)]
    n2 = "L2_ffn_"
    w_f3 = [wt(g["L3_ffn_w3_w"].T), wt(g[n2 + "cn_w1"]), wt(g[n2 + "cn_w2"]), g[n2 + "cn_w3"], low(g[n2 + "cn_w4"]),
            wt(g[n2 + "gc_w1"]), g[n2 + "gc_w2"], low(g[n2 + "gc_w3"])]
    b = "L3_attn_"
    w_l3 = [wt(g[b + "Wq"]), wt(g[b + "Wk"]), wt(g[b + "Wv"]), wt(g[b + "Wg"]), wt(g[b + "Wgk1"]), low(g[b + "Wgk2"]),
            wt(g[b + "Wo"])]
    w_fh = [wt(g["L3_ffn_h1_w"].T), wt(g["L3_ffn_h2_w"].T)]
    packed = wt(g["L1_ffn_packed_weight"].reshape(64, C).T)
    side_by_side = {"w_tok": w_tok, "w_mam": w_mam, "w_exp": w_exp, "w_l2": w_l2, "w_l1": w_l1, "w_f1": w_f1,
                    "w_f3": w_f3, "w_l3": w_l3, "w_fh": w_fh}
    arrays = {"small": small, "packed": packed, "patches": patches}
    arrays.update({k: np.concatenate(v, axis=1) for k, v in side_by_side.items()})
    return {k: np.ascontiguousarray(v) for k, v in arrays.items()}


def kernel(**inputs):
    import concourse.bacc as bacc
    from concourse.bass_utils import run_bass_kernel_spmd

    arrays = layout({k: np.asarray(v) for k, v in inputs.items()})
    nc = bacc.Bacc("TRN2", target_bir_lowering=False, num_devices=1)
    args = {k: nc.dram_tensor("in_" + k, v.shape, mybir.dt.from_np(v.dtype), kind="ExternalInput").ap()
            for k, v in arrays.items()}
    out = nc.dram_tensor("out_0", (N, C), F32, kind="ExternalOutput").ap()
    tower(nc, out=out, **args)
    r = run_bass_kernel_spmd(nc, [{"in_" + k: v for k, v in arrays.items()}], core_ids=[0])
    return r.results[0]["out_0"].reshape(B, L, C)
```

```python
from contextlib import ExitStack

import numpy as np

import concourse.bass as bass
from concourse import mybir

F32 = mybir.dt.float32
BF16 = mybir.dt.bfloat16
I32 = mybir.dt.int32
ALU = mybir.AluOpType
ACT = mybir.ActivationFunctionType
AX = mybir.AxisListType

P = 128
C = 256
CT = C // P
B = 64
L = 5
N = B * L
TT = 4
TN = N // TT
HALVES = (0, 1)
BH = B // 2
NH = N // 2
PATCH = 14
TAPS = 9
WIN = 4
NW = B * WIN
NP = NW * TAPS
KC = 3 * PATCH * PATCH
KCT = -(-KC // P)
CHUNK = 512
NCH = -(-NP // CHUNK)
H8 = 8
DH = C // H8
DI = 512
DIT = DI // P
NS = 16
RANK = 16
NE = 8
HID = 384
HIDT = HID // P
H16 = 16
HD1 = 16
HD2 = 64
QT2 = H16 * HD2 // P
LAGS = range(L)
PAIR_OFF = [0]
for _d in LAGS:
    PAIR_OFF.append(PAIR_OFF[-1] + BH * (L - _d))
PAIRS = PAIR_OFF[-1]
DH3 = 1024
HT3 = DH3 // P
EPS = 1e-5
MAGIC = 12582912.0
A_LOG_TOP = 88.7
EXP_FLOOR = -200.0
FAR = -1e30

SMALL = {}
for _n, _w in [("ident", 128), ("same32", 128), ("same16", 128), ("inv256", 1), ("inv128", 1), ("one", 1), ("eps", 1),
               ("sign", 1), ("before", 64), ("cosq", 5), ("sinq", 5), ("cosk", 5), ("sink", 5), ("attmask", 80),
               ("la_ln_q_g", 2), ("la_ln_q_b", 2), ("la_ln_kv_g", 2), ("la_ln_kv_b", 2), ("la_proj_b", 2),
               ("ga_ln_q_g", 2), ("ga_ln_q_b", 2), ("ga_ln_kv_g", 2), ("ga_ln_kv_b", 2), ("ga_proj_b", 2),
               ("mod_b", 2), ("class_emb", 2), ("W_conv", 12), ("b_dt", 4), ("A_log", 64), ("D_param", 4),
               ("Wr", 16), ("l1_bias", 256), ("l1_scale", 1), ("cn_b1", 2), ("cn_b2", 1), ("cn_b3", 1), ("cn_b4", 1),
               ("gc_b1", 1), ("gc_b2", 1), ("gc_b3", 1), ("range", 1), ("bgk2", 2), ("gnorm", 1),
               ("w1_s", 8), ("w2_s", 8), ("h1_s", 8), ("h2_s", 8), ("w3_s", 2)]:
    SMALL[_n] = (sum(w for _, w in SMALL.values()), _w)
NSMALL = sum(w for _, w in SMALL.values())


def columns(parts):
    out, at = {}, 0
    for name, kt, width in parts:
        out[name] = (at, kt, width)
        at += kt * width
    return out, at


W_TOK, N_TOK = columns([("conv", KCT, C), ("la_wq", 2, C), ("la_wkv", 2, 2 * C), ("la_proj", 2, C), ("ga_wq", 2, C),
                        ("ga_wkv", 2, 2 * C), ("ga_proj", 2, C), ("mod", 2, C)])
W_MAM, N_MAM = columns([("W_in", 2, 2 * DI), ("W_x", 4, 48), ("W_dt", 1, DI), ("W_out", 4, C)])
W_EXP, N_EXP = columns([("W1", 2, HID), ("W3", 2, HID), ("W2", 3, C)])
W_L2, N_L2 = columns([("wq", 2, 1024), ("wk", 2, 1024), ("wv", 2, 1024), ("wr", 8, C)])
W_L1, N_L1 = columns([("wqp", 2, C), ("wqr", 2, C), ("wkp", 2, P), ("wkr", 2, P), ("wv", 2, P), ("wo", 2, C)])
W_F1, N_F1 = columns([("w1", 2, DH3), ("w2", 2, DH3)])
W_F3, N_F3 = columns([("w3", 8, C), ("cn1", 2, C), ("cn2", 2, P), ("cn3", 1, 64), ("cn4", 1, 1),
                      ("gc1", 2, P), ("gc2", 1, 64), ("gc3", 1, 1)])
W_L3, N_L3 = columns([("wq", 2, C), ("wk", 2, C), ("wv", 2, 512), ("wg", 2, 512), ("gk1", 2, 16), ("gk2", 1, C),
                      ("wo", 4, C)])
W_FH, N_FH = columns([("h1", 8, DH3), ("h2", 8, DH3)])
N_PAT = max(KCT * NP, N_L2 + N_L1, N_L3)
N_BIG = max(NE * N_EXP, 4 * CT * NP, N_FH)
N_WTOK = max(N_TOK, N_F1)
N_WMAM = max(N_MAM, N_F3)
SLOT = DIT * N
N_SCR = 6 * SLOT

SIGNALS = """
small_in packed_in patches_in_0 patches_in_1 patches_in_2 patches_in_3 patches_in_4 conv_w_in tok_w_in mam_w_in
l2_w_in l1_w_in f1_w_in f3_w_in l3_w_in fh_w_in dve_step act_step pool_step cls_in ln_xc ln_sq ln_logvar ln_rstd ln_out
gq_read pe0_copied pe1_copied w_xc w_sq w_logvar w_rstd w_xn red q_copied kq_done v_copied la_shift la_exp agg
aggT_copied lo gk_copied gs_shift gs_exp gv_used gagg cls_out patch_out
u_conv u_silu res_silu xdbl_copied a_clip a_exp a_neg dt_relu dt_abs dt_exp dt_exp1 dt_log delta arg_zero arg decay b_used
scanned hc hc_added y_skip y_out z_mam
gate_copied gate_shift gate_exp comb comb_copied combine_copied silu_h gated moe_act act_used z_moe
rope1 v1_copied s1_clear s1_prod s1_copied s1_shift s1_exp a1_out z_attn1
x_tok_copied x_int xint_copied l1f_read l1f_var l1f_rstd h4_tok h4_copied
q2_copied k2_copied v2_copied s2_masked s2_shift s2_exp s2_prob pT_copied o2_copied z_attn2
gmean gc_act c1_act c2_act c3_act c4_act c_out z_ffn2
qkv3_copied g3_silu gk1_copied gk_min gk_abs gk_exp gk_log keep_set g_diff g_exp s3_prod s3_mul o3_sum
o3_sq o3_logvar o3_rstd o3_out z_attn3
f1_silu f_gate fh1_act fh2_act z_ffn3 tok_out stored
""".split()


class Counts:

    def __init__(self, sems, step):
        self.sems, self.step, self.count, self.last = sems, step, {}, None

    def __call__(self, signal=None):
        name = signal or self.step
        self.count[name] = self.count.get(name, 0) + 1
        self.last = name
        return self.sems[name], 1

    def latest(self):
        return self.sems[self.last], self.count[self.last]


def tower(nc, small, packed, patches, w_tok, w_mam, w_exp, w_l2, w_l1, w_f1, w_f3, w_l3, w_fh, out):
    ctx = ExitStack()
    with ctx:
        def sb(name, cols, dt=F32):
            return ctx.enter_context(nc.sbuf_tensor(name, [P, cols], dt))

        BIG = sb("BIG", N_BIG)
        PAT = sb("PAT", N_PAT)
        WTOK = sb("WTOK", N_WTOK)
        WMAM = sb("WMAM", N_WMAM)
        SCR = sb("SCR", N_SCR)
        SM = sb("SM", NSMALL)
        H = [sb(f"H{i}", CT * N) for i in range(2)]
        Z = sb("Z", CT * N)
        XC = sb("XC", CT * N)
        SQ = sb("SQ", CT * N)
        BANK = [ctx.enter_context(nc.psum_tensor(f"bank{i}", [P, 512], F32)) for i in range(8)]
        S = {name: ctx.enter_context(nc.semaphore(name)) for name in SIGNALS}
        bank_full = [ctx.enter_context(nc.semaphore(f"bank_full_{i}")) for i in range(8)]
        expert_in = [ctx.enter_context(nc.semaphore(f"experts_in_{i}")) for i in range(NE // 2)]

        def sm(name, i=None, rows=P):
            at, w = SMALL[name]
            return SM[0:rows, at:at + w] if i is None else SM[0:rows, at + i:at + i + 1]

        def view(buf, at, *dims, rows=P):
            n = int(np.prod(dims))
            v = buf[0:rows, at:at + n]
            if len(dims) == 2:
                v = v.rearrange("p (a b) -> p a b", b=dims[1])
            elif len(dims) == 3:
                v = v.rearrange("p (a b c) -> p a b c", b=dims[1], c=dims[2])
            elif len(dims) == 4:
                v = v.rearrange("p (a b c d) -> p a b c d", b=dims[1], c=dims[2], d=dims[3])
            return v

        def weight(buf, table, name, base=0, rows=P):
            at, kt, width = table[name]
            return view(buf, base + at, kt, width, rows=rows)

        def half(ap, f):
            c = slice(f * NH, (f + 1) * NH)
            return ap[:, c] if len(ap.shape) == 2 else ap[:, :, c]

        def norm_at(i, f):
            return 3 + CT * i + f + 1

        def tokens(ap):
            if len(ap.shape) == 2:
                return ap.rearrange("p (b l) -> p b l", l=L)
            return ap.rearrange("p m (b l) -> p m b l", l=L)

        def over(ap, n):
            return ap.unsqueeze(1).to_broadcast([ap.shape[0], n] + list(ap.shape[1:]))

        def last(ap, n):
            return ap.unsqueeze(len(ap.shape)).to_broadcast(list(ap.shape) + [n])

        h = [view(H[i], 0, CT, N) for i in range(2)]
        z, xc, sq = view(Z, 0, CT, N), view(XC, 0, CT, N), view(SQ, 0, CT, N)
        sqh = [view(SQ, CT * NH * f, CT, NH) for f in HALVES]
        ident = sm("ident")

        pe_all = view(BIG, 0, CT, NP)
        xn_all = view(BIG, CT * NP, CT, NP)
        prod_w = view(BIG, 2 * CT * NP, 2, TAPS, C)
        sq_all = view(BIG, 2 * CT * NP, CT, NP)
        v_w = view(BIG, 3 * CT * NP, 2, TAPS, C)
        red = view(SCR, 0, CT, NW)
        redn = view(SCR, 512, CT, NW)
        q_w = view(SCR, 1024, 2, C)
        sc = view(SCR, 1536, 2, TAPS, H8)
        sc_e = view(SCR, 1680, 2, TAPS, H8)
        sc_m = view(SCR, 1824, 2, H8)
        sc_s = view(SCR, 1840, 2, H8)
        sc_r = view(SCR, 1856, 2, H8)
        agg = view(SCR, 1880, 2, C)
        aggT = view(SCR, 2392, CT, NW)
        lo = view(SCR, 2904, CT, NW)
        lon = view(SCR, 3416, CT, NW)
        gkT = view(SCR, 3928, CT, NW)
        gs = view(SCR, 4440, CT, NW)
        gse = view(SCR, 4952, CT, NW)
        gm = view(SCR, 5464, CT, B)
        gr = view(SCR, 5592, CT, B)
        gaggT = view(SCR, 5720, CT, B)
        clsn = view(SCR, 5848, CT, 1)
        gq = view(SCR, 5850, CT, 1)
        gqm = view(SCR, 5852, CT, P)
        w_log = view(SCR, 6108, CHUNK)
        w_rs = view(SCR, 6620, CHUNK)

        u_raw, u, sres, delta, du, e1, az, rz = (view(PAT, i * SLOT, DIT, N) for i in range(8))
        arg = [view(SCR, i * SLOT, DIT, N) for i in range(2)]
        dbu = [view(SCR, (2 + i) * SLOT, DIT, N) for i in range(2)]
        hs = [view(SCR, (4 + i) * SLOT, DIT, N) for i in range(2)]
        hc = [e1, az]
        w1, lost = delta, du
        xdbl = view(PAT, 8 * SLOT, N, rows=48)
        negA = view(PAT, 8 * SLOT + N, DIT, NS)

        lg, ex = (view(SCR, i * 32, TT, NE, rows=TN) for i in range(2))
        gmax, gsum, grec = (view(SCR, 96 + 4 * i, TT, rows=TN) for i in range(3))
        cmp1, cmp2 = (view(SCR, 128 + i * 256, TT, NE, NE, rows=TN) for i in range(2))
        rank = view(SCR, 640, TT, NE, rows=TN)
        combT = view(SCR, 700, N, rows=NE)
        combb = [view(SCR, 1100 + i * N, N) for i in range(2)]
        sil = [view(SCR, 1800 + i * N, N) for i in range(2)]
        gated = [view(SCR, 2500 + i * N, N) for i in range(2)]
        mixed = [view(SCR, 3200 + i * HIDT * N, HIDT, N) for i in range(2)]

        q1, t1a, t1b, o1, t1 = ([view(BIG, 640 * i + CT * NH * f, CT, NH) for f in HALVES] for i in range(5))
        k1, v1, kt1, kt2 = ([view(BIG, 3200 + 320 * i + NH * f, NH) for f in HALVES] for i in range(4))
        pr1 = [[view(BIG, 4480 + CT * (PAIRS * f + PAIR_OFF[d]), CT, BH * (L - d)) for d in LAGS] for f in HALVES]
        s1 = [view(BIG, 6400 + 1600 * f, CT * NH, L) for f in HALVES]
        s1e = [view(BIG, 9600 + 1600 * f, CT * NH, L) for f in HALVES]
        s1m, s1s, s1r = ([view(BIG, 12800 + 640 * i + 320 * f, CT * NH) for f in HALVES] for i in range(3))

        x_tok = view(SCR, 0, TT, C, rows=TN)
        xq = view(SCR, 1024, TT, C, rows=TN)
        y_tok = view(SCR, 2048, TT, C, rows=TN)
        amax, asc, ainv, tmean, trs = (view(SCR, 3072 + 8 * i, TT, rows=TN) for i in range(5))
        stats = view(SCR, 3120, TT, 6, rows=TN)
        aggr = view(SCR, 3150, TT, 2, rows=TN)
        xqT = sb("xqT", CT * N, BF16)
        wint = sb("wint", 2 * 64, I32)
        wenc = sb("wenc", 2 * C, I32)
        wT = sb("wT", 2 * C, BF16)
        xT = xqT[:, :].rearrange("p (m n) -> p m n", m=CT)

        q2, k2 = view(BIG, 0, QT2, N), view(BIG, 2560, QT2, N)
        v2 = view(BIG, 5120, TT, 1024, rows=TN)
        s2 = view(BIG, 9216, TT, H16, TN, rows=TN)
        o2 = view(BIG, 14336, QT2, N)
        s2m = view(SCR, 0, TT, H16, rows=TN)

        def slot2(hd):
            return 8 * (hd // 8) + 4 * (hd % 2) + hd % 8 // 2

        s2s = view(SCR, 64, TT, H16, rows=TN)
        s2r = view(SCR, 128, TT, H16, rows=TN)
        pT = [view(SCR, 256 + i * 1280, H16, TN, rows=TN) for i in range(2)]

        cn_a = [view(SCR, 320 * f, CT, NH) for f in HALVES]
        cn_b = [view(SCR, 640 + NH * f, NH) for f in HALVES]
        cn_c = [view(SCR, 960 + NH * f, NH, rows=64) for f in HALVES]
        cn_t = [view(SCR, 1280 + NH * f, NH) for f in HALVES]
        coup = [view(SCR, 1600 + NH * f, NH) for f in HALVES]
        ctmp = [view(SCR, 1920 + 320 * f, CT, NH) for f in HALVES]
        cout = [[view(SCR, 2560 + 640 * i + 320 * f, CT, NH) for f in HALVES] for i in range(2)]
        gmn = [view(SCR, 3840 + 64 * f, CT, BH) for f in HALVES]
        gc_a = [view(SCR, 3968 + BH * f, BH) for f in HALVES]
        gc_b = [view(SCR, 4032 + BH * f, BH, rows=64) for f in HALVES]
        gf = [view(SCR, 4096 + BH * f, BH) for f in HALVES]
        r2 = view(SCR, 4160, 2)

        A3 = 5000
        q3, k3, gaz, gmin, gcum = ([view(SCR, 640 * i + 320 * f, CT, NH) for f in HALVES] for i in range(5))
        sg3 = [view(SCR, 3200 + 640 * f, 4, NH) for f in HALVES]
        v3 = [view(SCR, 4480 + 640 * f, 4, NH) for f in HALVES]
        o3 = [view(SCR, 5760 + 640 * f, 4, NH) for f in HALVES]
        gk1 = [view(SCR, 7040 + NH * f, NH, rows=RANK) for f in HALVES]
        keep = view(PAT, A3, CT * NH)
        t3 = [view(PAT, A3 + 320 + i * 320, 2, NH) for i in range(4)]
        D3, P3 = A3 + 1600, A3 + 1600 + 2 * CT * PAIRS
        gdf_d = [[view(PAT, D3 + CT * (PAIRS * f + PAIR_OFF[d]), CT, BH * (L - d)) for d in LAGS] for f in HALVES]
        pr3_d = [[view(PAT, P3 + CT * (PAIRS * f + PAIR_OFF[d]), CT, BH * (L - d)) for d in LAGS] for f in HALVES]
        osq = [view(PAT, D3 + CT * PAIRS * f, 4, NH) for f in HALVES]
        rs3 = [view(PAT, P3 + CT * PAIRS * f, 4, NH) for f in HALVES]

        fa = view(PAT, 0, HT3, N)
        fb = view(PAT, 2560, HT3, N)
        fsil = [view(SCR, i * NH, NH) for i in range(2)]
        otok = view(SCR, 1024, TT, C, rows=TN)

        place = {}
        uses = [0] * 8
        reader = [(S["small_in"], 16)] * 8
        before = {}
        expected = {}

        block = ctx.enter_context(nc.Block())

        @block.tensor
        def _(pe):
            ring = {"banks": list(range(8)), "at": 0}

            def rotate(banks):
                ring["banks"], ring["at"] = list(banks), 0

            def take(key, signal, bank=None, count=None):
                if bank is None:
                    bank = ring["banks"][ring["at"] % len(ring["banks"])]
                    ring["at"] += 1
                if count is None:
                    expected[signal] = expected.get(signal, 0) + 1
                    count = expected[signal]
                before[key] = reader[bank]
                reader[bank] = (S[signal], count)
                uses[bank] += 1
                place[key] = (bank, uses[bank])
                return BANK[bank]

            def emptied(key):
                return before[key]

            def fills(key):
                return bank_full[place[key][0]], 1

            def product(out, w, m0, m1, x, tiles, xs=None):
                for k in range(tiles):
                    ins = pe.matmul(out, w[:, k, m0:m1], x[:, k] if xs is None else xs(k),
                                    start=(k == 0), stop=(k == tiles - 1))
                return ins

            ln_at = [0]

            def norm(key, x, sq_x, n, ready, count=1):
                i = ln_at[0] = ln_at[0] + 1
                pe.wait_ge(S[ready], count)
                o = take((key, "mean"), "ln_xc")
                pe.wait_ge(*emptied((key, "mean")))
                for k in range(CT):
                    ins = pe.matmul(o[:, 0:n], sm("inv256").to_broadcast([P, P]), x[:, k], start=(k == 0), stop=(k == CT - 1))
                ins.then_inc(*fills((key, "mean")))
                pe.wait_ge(S["ln_sq"], i)
                o = take((key, "var"), "ln_logvar")
                pe.wait_ge(*emptied((key, "var")))
                for k in range(CT):
                    ins = pe.matmul(o[:, 0:n], sm("inv256").to_broadcast([P, P]), sq_x[:, k], start=(k == 0), stop=(k == CT - 1))
                ins.then_inc(*fills((key, "var")))

            def mean_of(i, f, ready, count):
                pe.wait_ge(S[ready], count)
                o = take(("mean", i, f), "ln_xc")
                pe.wait_ge(*emptied(("mean", i, f)))
                product(o[:, 0:NH], inv, 0, P, half(z, f), CT).then_inc(*fills(("mean", i, f)))

            def var_of(i, f):
                pe.wait_ge(S["ln_sq"], norm_at(i, f))
                o = take(("var", i, f), "ln_logvar")
                pe.wait_ge(*emptied(("var", i, f)))
                product(o[:, 0:NH], inv, 0, P, sqh[f], CT).then_inc(*fills(("var", i, f)))

            def norm_half(i, ready, count=lambda f: f + 1):
                for f in HALVES:
                    mean_of(i, f, ready, count(f))
                for f in HALVES:
                    var_of(i, f)

            def pair(o, w, x, tiles, at=0):
                for m in range(CT):
                    ins = product(o[:, m * NH:(m + 1) * NH], w, at + m * P, at + (m + 1) * P, x, tiles)
                return ins

            inv = sm("inv256").unsqueeze(2).to_broadcast([P, CT, P])

            def tokenizer():
                w = {n: weight(WTOK, W_TOK, n) for n in W_TOK}
                pe.wait_ge(S["small_in"], 16)
                norm("cls", z[:, :, 0:1], sq[:, :, 0:1], 1, "cls_in")
                pe.wait_ge(S["conv_w_in"], 16)

                def conv(j):
                    n = min(CHUNK, NP - j * CHUNK)
                    pe.wait_ge(S[f"patches_in_{j}"], 16 * KCT)
                    for m in range(CT):
                        o = take(("conv", j, m), f"pe{m}_copied")
                        pe.wait_ge(*emptied(("conv", j, m)))
                        for k in range(KCT):
                            r = min(P, KC - k * P)
                            ins = pe.matmul(o[:, 0:n], w["conv"][0:r, k, m * P:(m + 1) * P],
                                            PAT[0:r, k * NP + j * CHUNK:k * NP + j * CHUNK + n],
                                            start=(k == 0), stop=(k == KCT - 1))
                        ins.then_inc(*fills(("conv", j, m)))

                def stat(kind, j, src, signal):
                    n = min(CHUNK, NP - j * CHUNK)
                    o = take((kind, j), signal)
                    pe.wait_ge(*emptied((kind, j)))
                    for k in range(CT):
                        ins = pe.matmul(o[:, 0:n], sm("inv256").to_broadcast([P, P]), src[:, k, j * CHUNK:j * CHUNK + n],
                                        start=(k == 0), stop=(k == CT - 1))
                    ins.then_inc(*fills((kind, j)))

                for j in range(NCH + 2):
                    if j < NCH:
                        conv(j)
                    if 1 <= j <= NCH:
                        pe.wait_ge(S["pe0_copied"], j)
                        pe.wait_ge(S["pe1_copied"], j)
                        stat("wmean", j - 1, pe_all, "w_xc")
                    if j >= 2:
                        pe.wait_ge(S["w_sq"], j - 1)
                        stat("wvar", j - 2, sq_all, "w_logvar")
                pe.wait_ge(S["tok_w_in"], 16)
                pe.wait_ge(S["ln_out"], 1)
                o = take("gq", "gq_read")
                pe.wait_ge(*emptied("gq"))
                for m in range(CT):
                    ins = product(o[:, m:m + 1], w["ga_wq"], m * P, (m + 1) * P, clsn, CT)
                ins.then_inc(*fills("gq"))
                norm("red", red, sq[:, :, 0:NW], NW, "red")
                pe.wait_ge(S["ln_out"], 2)
                for t in range(2):
                    o = take(("q", t), "q_copied")
                    pe.wait_ge(*emptied(("q", t)))
                    ins = product(o[:, 0:C], redn[:, :, t * P:(t + 1) * P], 0, P, w["la_wq"], CT)
                    ins.then_inc(*fills(("q", t)))
                for t in range(2):
                    for k in range(TAPS):
                        pe.wait_ge(S["w_xn"], k * NW // CHUNK + 1)
                        o = take(("kv", k, t), "v_copied")
                        pe.wait_ge(*emptied(("kv", k, t)))
                        at = k * NW + t * P
                        ins = product(o[:, :], xn_all[:, :, at:at + P], 0, P, w["la_wkv"], CT)
                        ins.then_inc(*fills(("kv", k, t)))
                o = take("aggT", "aggT_copied")
                pe.wait_ge(*emptied("aggT"))
                for t in range(2):
                    pe.wait_ge(S["agg"], t + 1)
                    for m in range(CT):
                        ins = pe.transpose(o[:, m * NW + t * P:m * NW + (t + 1) * P], agg[:, t, m * P:(m + 1) * P], ident)
                ins.then_inc(*fills("aggT"))
                pe.wait_ge(S["aggT_copied"], 1)
                o = take("proj", "lo")
                pe.wait_ge(*emptied("proj"))
                for m in range(CT):
                    ins = product(o[:, m * NW:(m + 1) * NW], w["la_proj"], m * P, (m + 1) * P, aggT, CT)
                ins.then_inc(*fills("proj"))
                pe.wait_ge(S["lo"], 1)
                o = take("mod", "patch_out")
                pe.wait_ge(*emptied("mod"))
                for m in range(CT):
                    ins = product(o[:, m * NW:(m + 1) * NW], w["mod"], m * P, (m + 1) * P, lo, CT)
                ins.then_inc(*fills("mod"))
                norm("lo", lo, sq[:, :, 0:NW], NW, "lo")
                pe.wait_ge(S["ln_out"], 3)
                for key, sig, c0 in (("gk", "gk_copied", 0), ("gv", "gv_used", C)):
                    o = take(key, sig)
                    pe.wait_ge(*emptied(key))
                    for m in range(CT):
                        ins = product(o[:, m * NW:(m + 1) * NW], w["ga_wkv"], c0 + m * P, c0 + (m + 1) * P, lon, CT)
                    ins.then_inc(*fills(key))
                pe.wait_ge(S["gk_copied"], 1)
                pe.wait_ge(S["gq_read"], 1)
                o = take("gs", "gs_shift")
                pe.wait_ge(*emptied("gs"))
                for m in range(CT):
                    ins = pe.matmul(o[:, m * NW:(m + 1) * NW], gqm[:, m, :], gkT[:, m, :], start=True, stop=True)
                ins.then_inc(*fills("gs"))
                pe.wait_ge(S["gagg"], 1)
                o = take("gproj", "cls_out")
                pe.wait_ge(*emptied("gproj"))
                for m in range(CT):
                    ins = product(o[:, m * B:(m + 1) * B], w["ga_proj"], m * P, (m + 1) * P, gaggT, CT)
                ins.then_inc(*fills("gproj"))

            def state_space():
                w = {n: weight(WMAM, W_MAM, n) for n in W_MAM}
                pe.wait_ge(S["mam_w_in"], 16)
                pe.wait_ge(S["cls_out"], 1)
                pe.wait_ge(S["patch_out"], 1)
                for m in range(2 * DIT):
                    o = take(("win", m), "u_conv" if m < DIT else "res_silu")
                    pe.wait_ge(*emptied(("win", m)))
                    product(o[:, 0:N], w["W_in"], m * P, (m + 1) * P, h[0], CT).then_inc(*fills(("win", m)))
                pe.wait_ge(S["u_silu"], 1)
                o = take("xdbl", "xdbl_copied")
                pe.wait_ge(*emptied("xdbl"))
                product(o[0:48, 0:N], w["W_x"], 0, 48, u, DIT).then_inc(*fills("xdbl"))
                pe.wait_ge(S["xdbl_copied"], 1)
                for m in range(DIT):
                    o = take(("wdt", m), "dt_relu")
                    pe.wait_ge(*emptied(("wdt", m)))
                    pe.matmul(o[:, 0:N], w["W_dt"][0:RANK, 0, m * P:(m + 1) * P], xdbl[0:RANK, :],
                                               start=True, stop=True).then_inc(*fills(("wdt", m)))
                y = []
                for m in range(DIT):
                    o = take(("y", m), "y_skip", bank=4 + m)
                    pe.wait_ge(*emptied(("y", m)))
                    y.append(o)
                rotate(range(4))

                def add(n):
                    pe.wait_ge(S["hc"], n + 1)
                    for m in range(DIT):
                        ins = pe.matmul(y[m][:, 0:N], ident, hc[n % 2][:, m], start=(n == 0), stop=(n == NS - 1))
                        if n == NS - 1:
                            ins.then_inc(*fills(("y", m)))
                    if n < NS - 1:
                        ins.then_inc(S["hc_added"], 1)

                def spread(n):
                    for key, row, sig in (("B", RANK + n, "b_used"), ("C", RANK + NS + n, "hc")):
                        o = take((key, n), sig)
                        pe.wait_ge(*emptied((key, n)))
                        pe.matmul(o[:, 0:N], ident[0:48, row:row + 1].to_broadcast([48, P]), xdbl,
                                                 start=True, stop=True).then_inc(*fills((key, n)))

                spread(0)
                spread(1)
                for n in range(NS):
                    if n + 2 < NS:
                        spread(n + 2)
                    add(n)
                rotate(range(8))
                pe.wait_ge(S["y_out"], DIT)
                for f in HALVES:
                    o = take(("wout", f), "z_mam")
                    pe.wait_ge(*emptied(("wout", f)))
                    pair(o, w["W_out"], half(u_raw, f), DIT).then_inc(*fills(("wout", f)))
                norm_half(0, "z_mam")

            def experts():
                pe.wait_ge(S["ln_out"], norm_at(0, 1))
                o = take("gate", "gate_copied")
                pe.wait_ge(*emptied("gate"))
                wr = view(SM, SMALL["Wr"][0], 2, NE)
                for t in range(TT):
                    ins = product(o[0:TN, t * NE:(t + 1) * NE], h[1][:, :, t * TN:(t + 1) * TN], 0, TN, wr, CT)
                ins.then_inc(*fills("gate"))
                rotate(range(6))

                def up(e):
                    pe.wait_ge(expert_in[e // 2], 16)
                    for m in range(HIDT):
                        for name, sig in (("W1", "silu_h"), ("W3", "gated")):
                            w = weight(BIG, W_EXP, name, base=e * N_EXP)
                            o = take((name, e, m), sig)
                            pe.wait_ge(*emptied((name, e, m)))
                            product(o[:, 0:N], w, m * P, (m + 1) * P, h[1], CT).then_inc(*fills((name, e, m)))

                acc = []
                for m in range(CT):
                    o = take(("moe", m), "z_moe", bank=6 + m, count=2)
                    pe.wait_ge(*emptied(("moe", m)))
                    acc.append(o)

                def combine(e):
                    o = take(("comb", e), "combine_copied")
                    pe.wait_ge(*emptied(("comb", e)))
                    pe.matmul(o[:, 0:N], ident[0:NE, e:e + 1].to_broadcast([NE, P]), combT,
                                                start=True, stop=True).then_inc(*fills(("comb", e)))

                def down(e):
                    w = weight(BIG, W_EXP, "W2", base=e * N_EXP)
                    for k in range(HIDT):
                        pe.wait_ge(S["moe_act"], e * HIDT + k + 1)
                        for m in range(CT):
                            ins = pe.matmul(acc[m][:, 0:N], w[:, k, m * P:(m + 1) * P], mixed[e % 2][:, k],
                                            start=(e == 0 and k == 0), stop=(e == NE - 1 and k == HIDT - 1))
                            if e == NE - 1 and k == HIDT - 1:
                                ins.then_inc(*fills(("moe", m)))
                    if e < NE - 1:
                        ins.then_inc(S["act_used"], 1)

                pe.wait_ge(S["comb"], 1)
                o = take("combT", "comb_copied")
                pe.wait_ge(*emptied("combT"))
                for t in range(TT):
                    ins = pe.transpose(o[0:NE, t * TN:(t + 1) * TN], ex[:, t, :], ident[0:TN, 0:TN])
                ins.then_inc(*fills("combT"))
                pe.wait_ge(S["comb_copied"], 1)
                for e in range(NE + 1):
                    if e < NE:
                        combine(e)
                        up(e)
                    if e >= 1:
                        down(e - 1)
                rotate(range(8))
                norm_half(1, "z_moe")

            def attention1():
                base = N_L2
                w = {n: weight(PAT, W_L1, n, base=base) for n in W_L1}
                pe.wait_ge(S["l1_w_in"], 16)
                for f in HALVES:
                    pe.wait_ge(S["ln_out"], norm_at(1, f))
                    x = half(h[0], f)
                    o = take(("q1", f), "rope1")
                    pe.wait_ge(*emptied(("q1", f)))
                    pair(o, w["wqp"], x, CT).then_inc(*fills(("q1", f)))
                    o = take(("q1r", f), "rope1")
                    pe.wait_ge(*emptied(("q1r", f)))
                    pair(o, w["wqr"], x, CT).then_inc(*fills(("q1r", f)))
                    o = take(("k1", f), "rope1")
                    pe.wait_ge(*emptied(("k1", f)))
                    product(o[:, 0:NH], w["wkp"], 0, P, x, CT)
                    product(o[:, NH:2 * NH], w["wkr"], 0, P, x, CT).then_inc(*fills(("k1", f)))
                    o = take(("v1", f), "v1_copied")
                    pe.wait_ge(*emptied(("v1", f)))
                    product(o[:, 0:NH], w["wv"], 0, P, x, CT).then_inc(*fills(("v1", f)))
                for f in HALVES:
                    for d in LAGS:
                        pe.wait_ge(S["s1_prod"], L * f + d + 1)
                        o = take(("s1", f, d), "s1_copied")
                        pe.wait_ge(*emptied(("s1", f, d)))
                        for m in range(CT):
                            ins = pe.matmul(o[:, m * NH:m * NH + BH * (L - d)], sm("same16"), pr1[f][d][:, m],
                                            start=True, stop=True)
                        ins.then_inc(*fills(("s1", f, d)))
                for f in HALVES:
                    pe.wait_ge(S["a1_out"], f + 1)
                    o = take(("wo1", f), "z_attn1")
                    pe.wait_ge(*emptied(("wo1", f)))
                    pair(o, w["wo"], o1[f], CT).then_inc(*fills(("wo1", f)))
                norm_half(2, "z_attn1")

            def ternary():
                for f in HALVES:
                    pe.wait_ge(S["ln_out"], norm_at(2, f))
                    o = take(("xtok", f), "x_tok_copied")
                    pe.wait_ge(*emptied(("xtok", f)))
                    for i in range(2):
                        for m in range(CT):
                            c = (2 * f + i) * TN
                            ins = pe.transpose(o[0:TN, i * C + m * P:i * C + (m + 1) * P], h[1][:, m, c:c + TN], ident)
                    ins.then_inc(*fills(("xtok", f)))
                for f in HALVES:
                    pe.wait_ge(S["x_int"], f + 1)
                    o = take(("xint", f), "xint_copied")
                    pe.wait_ge(*emptied(("xint", f)))
                    for m in range(CT):
                        for i in range(2):
                            ins = pe.transpose(o[:, m * NH + i * TN:m * NH + (i + 1) * TN],
                                               xq[:, 2 * f + i, m * P:(m + 1) * P], ident[0:TN, 0:TN])
                    ins.then_inc(*fills(("xint", f)))
                wv = wT[:, :].rearrange("p (c o) -> p c o", c=2)
                for f in HALVES:
                    pe.wait_ge(S["xint_copied"], f + 1)
                    o = take(("l1f", f), "l1f_read")
                    pe.wait_ge(*emptied(("l1f", f)))
                    for i in range(2):
                        ins = product(o[0:TN, i * C:(i + 1) * C], xT[:, :, (2 * f + i) * TN:(2 * f + i + 1) * TN], 0, TN, wv, CT)
                    ins.then_inc(*fills(("l1f", f)))
                for f in HALVES:
                    pe.wait_ge(S["h4_tok"], f + 1)
                    o = take(("h4", f), "h4_copied")
                    pe.wait_ge(*emptied(("h4", f)))
                    for m in range(CT):
                        for i in range(2):
                            ins = pe.transpose(o[:, m * NH + i * TN:m * NH + (i + 1) * TN],
                                               y_tok[:, 2 * f + i, m * P:(m + 1) * P], ident[0:TN, 0:TN])
                    ins.then_inc(*fills(("h4", f)))

            def attention2():
                w = {n: weight(PAT, W_L2, n) for n in W_L2}
                pe.wait_ge(S["l2_w_in"], 16)
                for f in HALVES:
                    pe.wait_ge(S["h4_copied"], f + 1)
                    for j in range(QT2 // 2):
                        for name, key in (("wq", "q2"), ("wk", "k2")):
                            o = take((key, f, j), f"{key}_copied")
                            pe.wait_ge(*emptied((key, f, j)))
                            pair(o, w[name], half(h[0], f), CT, at=2 * j * P).then_inc(*fills((key, f, j)))

                def values(t):
                    for hf in range(2):
                        o = take(("v2", t, hf), "v2_copied")
                        pe.wait_ge(*emptied(("v2", t, hf)))
                        product(o[0:TN, :], h[0][:, :, t * TN:(t + 1) * TN], 0, TN,
                                                    w["wv"][:, :, hf * 512:(hf + 1) * 512], CT).then_inc(*fills(("v2", t, hf)))

                def scores(t):
                    for q in range(2):
                        pe.wait_ge(S["q2_copied"], 4 * (t // 2) + 2 * q + 2)
                        pe.wait_ge(S["k2_copied"], 4 * (t // 2) + 2 * q + 2)
                        banks = []
                        for odd in range(2):
                            o = take(("s2", t, 2 * q + odd), "s2_masked")
                            pe.wait_ge(*emptied(("s2", t, 2 * q + odd)))
                            banks.append(o)
                        for i in range(4):
                            for odd in range(2):
                                r = slice(HD2 * odd, HD2 * odd + HD2)
                                m = 4 * q + i
                                ins = pe.matmul(banks[odd][0:TN, i * TN:(i + 1) * TN], q2[r, m, t * TN:(t + 1) * TN],
                                                k2[r, m, t * TN:(t + 1) * TN], start=True, stop=True)
                                if i == 3:
                                    ins.then_inc(*fills(("s2", t, 2 * q + odd)))

                def mix(t):
                    pe.wait_ge(S["s2_prob"], t + 1)
                    for g in range(4):
                        o = take(("pT", t, g), "pT_copied")
                        pe.wait_ge(*emptied(("pT", t, g)))
                        for i in range(4):
                            ins = pe.transpose(o[0:TN, i * TN:(i + 1) * TN], s2[:, t, 4 * g + i, :], ident[0:TN, 0:TN])
                        ins.then_inc(*fills(("pT", t, g)))
                    pe.wait_ge(S["v2_copied"], 2 * t + 2)
                    for g in range(2):
                        pe.wait_ge(S["pT_copied"], 4 * t + 2 * g + 2)
                        o = take(("o2", t, g), "o2_copied")
                        pe.wait_ge(*emptied(("o2", t, g)))
                        for i in range(8):
                            hd = 8 * g + i
                            r = slice(HD2 * (hd % 2), HD2 * (hd % 2) + HD2)
                            ins = pe.matmul(o[r, (i // 2) * TN:(i // 2 + 1) * TN], v2[:, t, hd * HD2:(hd + 1) * HD2],
                                            pT[t % 2][:, slot2(hd), :], start=True, stop=True)
                        ins.then_inc(*fills(("o2", t, g)))

                def output(f):
                    pe.wait_ge(S["o2_copied"], 4 * f + 4)
                    o = take(("r2", f), "z_attn2")
                    pe.wait_ge(*emptied(("r2", f)))
                    pair(o, w["wr"], half(o2, f), QT2).then_inc(*fills(("r2", f)))

                scores(0)
                scores(1)
                for t in range(TT):
                    values(t)
                    if t + 2 < TT:
                        scores(t + 2)
                    mix(t)
                    if t == 2:
                        output(0)
                        mean_of(3, 0, "z_attn2", 1)
                var_of(3, 0)
                output(1)
                mean_of(3, 1, "z_attn2", 2)
                var_of(3, 1)

            def coupling():
                w = {n: weight(WMAM, W_F3, n) for n in W_F3}
                pe.wait_ge(S["f3_w_in"], 16)

                def first(cyc, f):
                    if cyc:
                        pe.wait_ge(S["c_out"], CT * (cyc - 1) + f + 1)
                    o = take(("c1", cyc, f), "c1_act")
                    pe.wait_ge(*emptied(("c1", cyc, f)))
                    pair(o, w["cn1"], half(h[1], f) if cyc == 0 else cout[(cyc - 1) % 2][f], CT).then_inc(*fills(("c1", cyc, f)))

                for f in HALVES:
                    pe.wait_ge(S["gmean"], f + 1)
                    o = take(("gc1", f), "gc_act")
                    pe.wait_ge(*emptied(("gc1", f)))
                    product(o[:, 0:BH], w["gc1"], 0, P, gmn[f], CT).then_inc(*fills(("gc1", f)))
                    first(0, f)
                for f in HALVES:
                    pe.wait_ge(S["gc_act"], f + 1)
                    o = take(("gc2", f), "gc_act")
                    pe.wait_ge(*emptied(("gc2", f)))
                    pe.matmul(o[0:64, 0:BH], w["gc2"][:, 0, :], gc_a[f], start=True, stop=True).then_inc(*fills(("gc2", f)))
                for f in HALVES:
                    pe.wait_ge(S["gc_act"], 2 + f + 1)
                    o = take(("gc3", f), "gc_act")
                    pe.wait_ge(*emptied(("gc3", f)))
                    pe.matmul(o[:, 0:BH], w["gc3"][0:64, 0, :].to_broadcast([64, P]), gc_b[f],
                                               start=True, stop=True).then_inc(*fills(("gc3", f)))
                for cyc in range(3):
                    n = CT * cyc + 1
                    if cyc:
                        for f in HALVES:
                            first(cyc, f)
                    for f in HALVES:
                        pe.wait_ge(S["c1_act"], n + f)
                        o = take(("c2", cyc, f), "c2_act")
                        pe.wait_ge(*emptied(("c2", cyc, f)))
                        product(o[:, 0:NH], w["cn2"], 0, P, cn_a[f], CT).then_inc(*fills(("c2", cyc, f)))
                    for f in HALVES:
                        pe.wait_ge(S["c2_act"], n + f)
                        o = take(("c3", cyc, f), "c3_act")
                        pe.wait_ge(*emptied(("c3", cyc, f)))
                        pe.matmul(o[0:64, 0:NH], w["cn3"][:, 0, :], cn_b[f], start=True, stop=True).then_inc(*fills(("c3", cyc, f)))
                    for f in HALVES:
                        pe.wait_ge(S["c3_act"], n + f)
                        o = take(("c4", cyc, f), "c4_act")
                        pe.wait_ge(*emptied(("c4", cyc, f)))
                        pe.matmul(o[:, 0:NH], w["cn4"][0:64, 0, :].to_broadcast([64, P]), cn_c[f],
                                                       start=True, stop=True).then_inc(*fills(("c4", cyc, f)))
                norm_half(4, "z_ffn2")

            def attention3():
                w = {n: weight(PAT, W_L3, n) for n in W_L3}
                pe.wait_ge(S["l3_w_in"], 16)
                for f in HALVES:
                    pe.wait_ge(S["ln_out"], norm_at(4, f))
                    x = half(h[0], f)
                    o = take(("gk1", f), "gk1_copied")
                    pe.wait_ge(*emptied(("gk1", f)))
                    product(o[0:RANK, 0:NH], w["gk1"], 0, RANK, x, CT).then_inc(*fills(("gk1", f)))
                    for key, name in (("q3", "wq"), ("k3", "wk")):
                        o = take((key, f), "qkv3_copied")
                        pe.wait_ge(*emptied((key, f)))
                        pair(o, w[name], x, CT).then_inc(*fills((key, f)))
                for f in HALVES:
                    pe.wait_ge(S["gk1_copied"], f + 1)
                    o = take(("gk2", f), "gk_min")
                    pe.wait_ge(*emptied(("gk2", f)))
                    for m in range(CT):
                        ins = pe.matmul(o[:, m * NH:(m + 1) * NH], w["gk2"][0:RANK, 0, m * P:(m + 1) * P], gk1[f],
                                        start=True, stop=True)
                    ins.then_inc(*fills(("gk2", f)))
                for key, name, sig in (("v3", "wv", "qkv3_copied"), ("g3", "wg", "g3_silu")):
                    for f in HALVES:
                        for j in range(2):
                            o = take((key, f, j), sig)
                            pe.wait_ge(*emptied((key, f, j)))
                            pair(o, w[name], half(h[0], f), CT, at=2 * j * P).then_inc(*fills((key, f, j)))
                for f in HALVES:
                    for d in LAGS:
                        pe.wait_ge(S["s3_prod"], L * f + d + 1)
                        for odd in range(2):
                            o = take(("s3", f, d, odd), "s3_mul")
                            pe.wait_ge(*emptied(("s3", f, d, odd)))
                            r = slice(64 * odd, 64 * odd + 64)
                            for m in range(CT):
                                ins = pe.matmul(o[:, m * NH:m * NH + BH * (L - d)], sm("one")[r, :].to_broadcast([64, P]),
                                                pr3_d[f][d][r, m], start=True, stop=True)
                            ins.then_inc(*fills(("s3", f, d, odd)))
                for f in HALVES:
                    pe.wait_ge(S["o3_sq"], f + 1)
                    for j in range(2):
                        o = take(("ms3", f, j), "o3_logvar")
                        pe.wait_ge(*emptied(("ms3", f, j)))
                        for i in range(2):
                            ins = pe.matmul(o[:, i * NH:(i + 1) * NH], sm("inv128").to_broadcast([P, P]),
                                            osq[f][:, 2 * j + i], start=True, stop=True)
                        ins.then_inc(*fills(("ms3", f, j)))
                for f in HALVES:
                    pe.wait_ge(S["o3_out"], f + 1)
                    o = take(("wo3", f), "z_attn3")
                    pe.wait_ge(*emptied(("wo3", f)))
                    pair(o, w["wo"], o3[f], 4).then_inc(*fills(("wo3", f)))
                norm_half(5, "z_attn3")

            def last_ffn():
                w12 = {n: weight(WTOK, W_F1, n) for n in W_F1}
                w3 = weight(WMAM, W_F3, "w3")
                wh = {n: weight(BIG, W_FH, n) for n in W_FH}
                pe.wait_ge(S["f1_w_in"], 16)
                for f in HALVES:
                    pe.wait_ge(S["ln_out"], norm_at(5, f))
                    for m in range(HT3):
                        for name, sig in (("w1", "f1_silu"), ("w2", "f_gate")):
                            o = take((name, f, m), sig)
                            pe.wait_ge(*emptied((name, f, m)))
                            product(o[:, 0:NH], w12[name], m * P, (m + 1) * P, half(h[1], f), CT).then_inc(*fills((name, f, m)))
                pe.wait_ge(S["fh_w_in"], 32)
                for name, src, need, n0, sig in (("h1", fa, "f_gate", HT3, "fh1_act"), ("h2", fb, "fh1_act", 0, "fh2_act")):
                    for m in range(HT3):
                        o = take((name, m), sig)
                        pe.wait_ge(*emptied((name, m)))
                        for k in range(HT3):
                            if m == 0:
                                pe.wait_ge(S[need], n0 + k + 1)
                            ins = pe.matmul(o[:, 0:N], wh[name][:, k, m * P:(m + 1) * P], src[:, k],
                                            start=(k == 0), stop=(k == HT3 - 1))
                        ins.then_inc(*fills((name, m)))
                pe.wait_ge(S["fh2_act"], HT3)
                for f in HALVES:
                    o = take(("f3", f), "z_ffn3")
                    pe.wait_ge(*emptied(("f3", f)))
                    pair(o, w3, half(fa, f), HT3).then_inc(*fills(("f3", f)))
                norm_half(6, "z_ffn3")
                for f in HALVES:
                    pe.wait_ge(S["ln_out"], norm_at(6, f))
                    o = take(("out", f), "tok_out")
                    pe.wait_ge(*emptied(("out", f)))
                    for i in range(2):
                        for m in range(CT):
                            c = (2 * f + i) * TN
                            ins = pe.transpose(o[0:TN, i * C + m * P:i * C + (m + 1) * P], h[0][:, m, c:c + TN], ident)
                    ins.then_inc(*fills(("out", f)))

            for f in [tokenizer, state_space, experts, attention1, ternary, attention2, coupling, attention3, last_ffn]:
                f()

        def two(bank, rows=P):
            return bank[0:rows, 0:2 * NH].rearrange("p (m n) -> p m n", m=2)

        def filled(key):
            return bank_full[place[key][0]], place[key][1]

        def result(key):
            return BANK[place[key][0]]

        @block.vector
        def _(dve):
            did = Counts(S, "dve_step")
            tt, ts, copy = dve.tensor_tensor, dve.tensor_scalar, dve.tensor_copy

            def stt(out, a, s, b, op0, op1):
                return dve.scalar_tensor_tensor(out=out, in0=a, scalar=s, in1=b, op0=op0, op1=op1)

            def reduce(out, a, op):
                return dve.tensor_reduce(out, a, AX.X, op)

            ln_at = [0]

            def norm(key, x, n, out, gain=None, shift=None):
                i = ln_at[0] = ln_at[0] + 1
                c = xc[:, :, 0:n]
                dve.wait_ge(*filled((key, "mean")))
                mean = result((key, "mean"))[:, 0:n]
                tt(c, x, over(mean, CT), ALU.subtract).then_inc(*did("ln_xc"))
                dve.wait_ge(S["ln_rstd"], i)
                rstd = SQ[:, N:N + n]
                if gain is None:
                    tt(out, c, over(rstd, CT), ALU.mult).then_inc(*did("ln_out"))
                    return
                for m in range(CT):
                    stt(out[:, m], c[:, m], sm(gain, m), rstd, ALU.mult, ALU.mult).then_inc(*did())
                dve.wait_ge(*did.latest())
                for m in range(CT):
                    ts(out[:, m], out[:, m], sm(shift, m), None, ALU.add)\
                        .then_inc(*did("ln_out" if m == CT - 1 else None))

            def residual(key, h_in, f, signal):
                dve.wait_ge(*filled((key, f)))
                o = result((key, f))
                tt(half(z, f), two(o), half(h_in, f), ALU.add).then_inc(*did(signal))

            def centre(i, f):
                dve.wait_ge(*filled(("mean", i, f)))
                o = result(("mean", i, f))
                tt(half(xc, f), half(z, f), over(o[:, 0:NH], CT), ALU.subtract).then_inc(*did("ln_xc"))

            def scale(i, f, out):
                dve.wait_ge(S["ln_rstd"], norm_at(i, f))
                tt(half(out, f), half(xc, f), over(sqh[f][:, 1], CT), ALU.mult).then_inc(*did("ln_out"))

            def norm_half(i, out):
                for f in HALVES:
                    centre(i, f)
                for f in HALVES:
                    scale(i, f, out)

            def tokenizer():
                dve.wait_ge(S["small_in"], 16)
                copy(z[:, :, 0:1], view(SM, SMALL["class_emb"][0], CT, 1)).then_inc(*did("cls_in"))
                norm("cls", z[:, :, 0:1], 1, clsn, "ga_ln_q_g", "ga_ln_q_b")
                for j in range(NCH + 2):
                    if j < NCH:
                        n = min(CHUNK, NP - j * CHUNK)
                        dve.wait_ge(*filled(("conv", j, 0)))
                        o = result(("conv", j, 0))
                        copy(pe_all[:, 0, j * CHUNK:j * CHUNK + n], o[:, 0:n]).then_inc(*did("pe0_copied"))
                    if 1 <= j <= NCH:
                        i = j - 1
                        n = min(CHUNK, NP - i * CHUNK)
                        c = slice(i * CHUNK, i * CHUNK + n)
                        dve.wait_ge(*filled(("wmean", i)))
                        o = result(("wmean", i))
                        tt(xn_all[:, :, c], pe_all[:, :, c], over(o[:, 0:n], CT), ALU.subtract).then_inc(*did("w_xc"))
                    if j >= 2:
                        i = j - 2
                        n = min(CHUNK, NP - i * CHUNK)
                        c = slice(i * CHUNK, i * CHUNK + n)
                        dve.wait_ge(S["w_rstd"], i + 1)
                        dve.wait_ge(S["w_sq"], i + 1)
                        for m in range(CT):
                            stt(xn_all[:, m, c], xn_all[:, m, c], sm("la_ln_kv_g", m), w_rs[:, 0:n], ALU.mult,
                                ALU.mult).then_inc(*did())
                        dve.wait_ge(*did.latest())
                        for m in range(CT):
                            ts(xn_all[:, m, c], xn_all[:, m, c], sm("la_ln_kv_b", m), None, ALU.add)\
                                .then_inc(*did("w_xn" if m == CT - 1 else None))
                    if 1 <= j <= NCH:
                        dve.wait_ge(S["pe0_copied"], j)
                        dve.wait_ge(S["pe1_copied"], j)
                        for k in range((j - 1) * CHUNK // NW, min(j * CHUNK, NP) // NW):
                            tap = pe_all[:, :, k * NW:(k + 1) * NW]
                            if k == 0:
                                copy(red, tap).then_inc(*did())
                            else:
                                dve.wait_ge(*did.latest())
                                tt(red, red, tap, ALU.add).then_inc(*did())
                dve.wait_ge(*filled("gq"))
                o = result("gq")
                for m in range(CT):
                    ts(gqm[:, m, :], sm("same32"), o[:, m:m + 1], float(C) ** -0.5, ALU.mult, ALU.mult)\
                        .then_inc(*did("gq_read" if m == CT - 1 else None))
                dve.wait_ge(*did.latest())
                ts(red, red, 1.0 / TAPS, None, ALU.mult).then_inc(*did("red"))
                norm("red", red, NW, redn, "la_ln_q_g", "la_ln_q_b")
                dve.wait_ge(S["q_copied"], 2)
                def products(t):
                    for k in range(TAPS):
                        dve.wait_ge(*filled(("kv", k, t)))
                        o = result(("kv", k, t))
                        tt(prod_w[:, t, k], o[:, 0:C], q_w[:, t], ALU.mult).then_inc(*did("kq_done"))

                def shifted(t):
                    dve.wait_ge(*did.latest())
                    reduce(sc[:, t].rearrange("p k h -> p (k h)"),
                           prod_w[:, t].rearrange("p k (h d) -> p (k h) d", d=DH), ALU.add)\
                        .then_inc(*did())
                    dve.wait_ge(*did.latest())
                    reduce(sc_m[:, t], sc[:, t].rearrange("p k h -> p h k"), ALU.max).then_inc(*did())
                    dve.wait_ge(*did.latest())
                    tt(sc_e[:, t], sc[:, t], over(sc_m[:, t], TAPS), ALU.subtract).then_inc(*did("la_shift"))

                def weighted(t):
                    dve.wait_ge(S["la_exp"], t + 1)
                    reduce(sc_s[:, t], sc_e[:, t].rearrange("p k h -> p h k"), ALU.add).then_inc(*did())
                    dve.wait_ge(*did.latest())
                    dve.reciprocal(sc_r[:, t], sc_s[:, t]).then_inc(*did())
                    dve.wait_ge(*did.latest())
                    tt(sc[:, t], sc_e[:, t], over(sc_r[:, t], TAPS), ALU.mult).then_inc(*did())
                    dve.wait_ge(*did.latest())
                    dve.wait_ge(S["v_copied"], TAPS * (t + 1))
                    tt(prod_w[:, t].rearrange("p k (h d) -> p (k h) d", d=DH),
                       v_w[:, t].rearrange("p k (h d) -> p (k h) d", d=DH),
                       last(sc[:, t].rearrange("p k h -> p (k h)"), DH), ALU.mult)\
                        .then_inc(*did())
                    dve.wait_ge(*did.latest())
                    reduce(agg[:, t], prod_w[:, t].rearrange("p k c -> p c k"), ALU.add).then_inc(*did("agg"))

                products(0)
                shifted(0)
                weighted(0)
                products(1)
                shifted(1)
                weighted(1)
                dve.wait_ge(*filled("aggT"))
                o = result("aggT")
                copy(aggT.rearrange("p m w -> p (m w)"), o[:, :]).then_inc(*did("aggT_copied"))
                dve.wait_ge(*filled("proj"))
                o = result("proj")
                for m in range(CT):
                    stt(lo[:, m], o[:, m * NW:(m + 1) * NW], sm("la_proj_b", m), red[:, m], ALU.add, ALU.add)\
                        .then_inc(*did("lo" if m == CT - 1 else None))
                dve.wait_ge(*filled("mod"))
                o = result("mod")
                for m in range(CT):
                    ts(tokens(h[0])[:, m, :, 0:WIN],
                       o[:, m * NW:(m + 1) * NW].rearrange("p (b n) -> p b n", n=WIN), sm("mod_b", m), None,
                       ALU.add).then_inc(*did("patch_out" if m == CT - 1 else None))
                norm("lo", lo, NW, lon, "ga_ln_kv_g", "ga_ln_kv_b")
                dve.wait_ge(*filled("gs"))
                o = result("gs")
                four = o[:, :].rearrange("p (x n) -> p x n", n=WIN)
                gm_ = gm.rearrange("p m b -> p (m b)")
                gr_ = gr.rearrange("p m b -> p (m b)")
                gs_ = gs.rearrange("p m (b n) -> p (m b) n", n=WIN)
                gse_ = gse.rearrange("p m (b n) -> p (m b) n", n=WIN)
                reduce(gm_, four, ALU.max).then_inc(*did())
                dve.wait_ge(*did.latest())
                tt(gs_, four, last(gm_, WIN), ALU.subtract).then_inc(*did("gs_shift"))
                dve.wait_ge(S["gs_exp"], 1)
                reduce(gr_, gse_, ALU.add).then_inc(*did())
                dve.wait_ge(*did.latest())
                dve.reciprocal(gr_, gr_).then_inc(*did())
                dve.wait_ge(*did.latest())
                tt(gse_, gse_, last(gr_, WIN), ALU.mult).then_inc(*did())
                dve.wait_ge(*did.latest())
                dve.wait_ge(*filled("gv"))
                o = result("gv")
                tt(gs_, gse_, o[:, :].rearrange("p (x n) -> p x n", n=WIN), ALU.mult).then_inc(*did("gv_used"))
                dve.wait_ge(*did.latest())
                reduce(gaggT.rearrange("p m b -> p (m b)"), gs_, ALU.add).then_inc(*did("gagg"))
                dve.wait_ge(*filled("gproj"))
                o = result("gproj")
                for m in range(CT):
                    ts(tokens(h[0])[:, m, :, WIN], o[:, m * B:(m + 1) * B], sm("ga_proj_b", m), sm("class_emb", m),
                       ALU.add, ALU.add).then_inc(*did("cls_out" if m == CT - 1 else None))

            def state_space():
                flat = "p m n -> p (m n)"
                ts(negA, view(SM, SMALL["A_log"][0], DIT, NS), A_LOG_TOP, None, ALU.min).then_inc(*did("a_clip"))
                dve.wait_ge(S["a_exp"], 1)
                ts(negA, negA, -1.0, None, ALU.mult).then_inc(*did("a_neg"))
                for m in range(DIT):
                    dve.wait_ge(*filled(("win", m)))
                    o = result(("win", m))
                    src, dst = tokens(o[:, 0:N]), tokens(u_raw[:, m])
                    ts(u_raw[:, m], o[:, 0:N], sm("W_conv", 3 * m + 2), None, ALU.mult).then_inc(*did())
                    dve.wait_ge(*did.latest())
                    stt(dst[:, :, 1:], src[:, :, :L - 1], sm("W_conv", 3 * m + 1), dst[:, :, 1:], ALU.mult, ALU.add)\
                        .then_inc(*did())
                    dve.wait_ge(*did.latest())
                    stt(dst[:, :, 2:], src[:, :, :L - 2], sm("W_conv", 3 * m), dst[:, :, 2:], ALU.mult, ALU.add)\
                        .then_inc(*did("u_conv"))
                dve.wait_ge(*filled("xdbl"))
                o = result("xdbl")
                copy(xdbl, o[0:48, 0:N]).then_inc(*did("xdbl_copied"))
                for m in range(DIT):
                    dve.wait_ge(S["dt_abs"], m + 1)
                    dve.wait_ge(*filled(("wdt", m)))
                    o = result(("wdt", m))
                    ts(rz[:, m], o[:, 0:N], sm("b_dt", m), 0.0, ALU.add, ALU.max).then_inc(*did("dt_relu"))
                dve.wait_ge(S["dt_exp"], 1)
                ts(w1, e1, 1.0, None, ALU.add).then_inc(*did("dt_exp1"))
                dve.wait_ge(*did.latest())
                stt(lost.rearrange(flat), w1.rearrange(flat), -1.0, e1.rearrange(flat), ALU.add, ALU.subtract)\
                    .then_inc(*did())
                dve.wait_ge(*did.latest())
                tt(rz, rz, lost, ALU.subtract).then_inc(*did())
                dve.wait_ge(*did.latest())
                dve.wait_ge(S["dt_log"], 1)
                tt(delta, az, rz, ALU.add).then_inc(*did("delta"))
                dve.wait_ge(*did.latest())
                dve.wait_ge(S["u_silu"], 1)
                tt(du, delta, u, ALU.mult).then_inc(*did())
                dve.wait_ge(*did.latest())

                def dbu_of(n):
                    dve.wait_ge(*filled(("B", n)))
                    o = result(("B", n))
                    tt(dbu[n % 2], du, over(o[:, 0:N], DIT), ALU.mult).then_inc(*did("b_used"))

                def arg_of(n):
                    if n >= 2:
                        dve.wait_ge(S["scanned"], n - 1)
                    for m in range(DIT):
                        ts(tokens(arg[n % 2][:, m])[:, :, 1:], tokens(delta[:, m])[:, :, 1:], negA[:, m, n:n + 1],
                           EXP_FLOOR, ALU.mult, ALU.max)\
                            .then_inc(*did("arg" if m == DIT - 1 else None))

                dve.wait_ge(S["arg_zero"], 2)
                arg_of(0)
                dbu_of(0)
                arg_of(1)
                for n in range(NS):
                    dve.wait_ge(S["b_used"], n + 1)
                    dve.wait_ge(S["decay"], n + 1)
                    dve.tensor_tensor_scan(hs[n % 2].rearrange(flat), arg[n % 2].rearrange(flat),
                                               dbu[n % 2].rearrange(flat), 0.0, ALU.mult, ALU.add).then_inc(*did("scanned"))
                    if n + 1 < NS:
                        dbu_of(n + 1)
                    dve.wait_ge(*filled(("C", n)))
                    o = result(("C", n))
                    dve.wait_ge(S["scanned"], n + 1)
                    if n >= 2:
                        dve.wait_ge(S["hc_added"], n - 1)
                    tt(hc[n % 2], hs[n % 2], over(o[:, 0:N], DIT), ALU.mult).then_inc(*did("hc"))
                    if n + 2 < NS:
                        arg_of(n + 2)
                for m in range(DIT):
                    dve.wait_ge(*filled(("y", m)))
                    o = result(("y", m))
                    stt(u_raw[:, m], u[:, m], sm("D_param", m), o[:, 0:N], ALU.mult, ALU.add).then_inc(*did("y_skip"))
                dve.wait_ge(S["res_silu"], DIT)
                for m in range(DIT):
                    dve.wait_ge(S["y_skip"], m + 1)
                    tt(u_raw[:, m], u_raw[:, m], sres[:, m], ALU.mult).then_inc(*did("y_out"))
                for f in HALVES:
                    residual("wout", h[0], f, "z_mam")
                norm_half(0, h[1])

            def experts():
                dve.wait_ge(*filled("gate"))
                o = result("gate")
                copy(lg.rearrange("p t e -> p (t e)"), o[0:TN, 0:TT * NE]).then_inc(*did("gate_copied"))
                dve.wait_ge(*did.latest())
                reduce(gmax, lg, ALU.max).then_inc(*did())
                dve.wait_ge(*did.latest())
                tt(ex, lg, last(gmax, NE), ALU.subtract).then_inc(*did("gate_shift"))
                other, own = lg.unsqueeze(2).to_broadcast([TN, TT, NE, NE]), last(lg, NE)
                tt(cmp1, other, own, ALU.is_gt).then_inc(*did())
                tt(cmp2, other, own, ALU.is_equal).then_inc(*did())
                dve.wait_ge(*did.latest())
                c2 = cmp2.rearrange("p t e f -> p t (e f)")
                tt(c2, c2, over(sm("before", rows=TN), TT), ALU.mult).then_inc(*did())
                dve.wait_ge(*did.latest())
                tt(cmp1, cmp1, cmp2, ALU.add).then_inc(*did())
                dve.wait_ge(*did.latest())
                reduce(rank, cmp1, ALU.add).then_inc(*did())
                dve.wait_ge(*did.latest())
                dve.wait_ge(S["gate_exp"], 1)
                stt(ex, rank, 1.5, ex, ALU.is_lt, ALU.mult).then_inc(*did())
                dve.wait_ge(*did.latest())
                reduce(gsum, ex, ALU.add).then_inc(*did())
                dve.wait_ge(*did.latest())
                dve.reciprocal(grec, gsum).then_inc(*did())
                dve.wait_ge(*did.latest())
                tt(ex, ex, last(grec, NE), ALU.mult).then_inc(*did("comb"))
                dve.wait_ge(*filled("combT"))
                o = result("combT")
                copy(combT, o[0:NE, 0:N]).then_inc(*did("comb_copied"))
                for e in range(NE):
                    dve.wait_ge(S["combine_copied"], e + 1)
                    if e >= 2:
                        dve.wait_ge(S["act_used"], e - 1)
                    for m in range(HIDT):
                        i = e * HIDT + m
                        dve.wait_ge(S["silu_h"], i + 1)
                        dve.wait_ge(*filled(("W3", e, m)))
                        o = result(("W3", e, m))
                        tt(gated[i % 2], sil[i % 2], o[:, 0:N], ALU.mult).then_inc(*did("gated"))
                        dve.wait_ge(*did.latest())
                        tt(mixed[e % 2][:, m], gated[i % 2], combb[e % 2], ALU.mult).then_inc(*did("moe_act"))
                for f in HALVES:
                    for m in range(CT):
                        dve.wait_ge(*filled(("moe", m)))
                        o = result(("moe", m))
                        tt(half(z, f)[:, m], half(o, f), half(h[1], f)[:, m], ALU.add)\
                            .then_inc(*did("z_moe" if m == CT - 1 else None))
                norm_half(1, h[0])

            def attention1():
                def rows(ap):
                    return ap.rearrange("p m (b l) -> p (m b) l", l=L)

                def table(name, n):
                    return sm(name).unsqueeze(1).to_broadcast([P, n, L])

                for f in HALVES:
                    dve.wait_ge(*filled(("q1", f)))
                    o = result(("q1", f))
                    tt(rows(t1a[f]), rows(two(o)), table("cosq", 2 * BH), ALU.mult).then_inc(*did("rope1"))
                    dve.wait_ge(*filled(("q1r", f)))
                    o = result(("q1r", f))
                    tt(rows(t1b[f]), rows(two(o)), table("sinq", 2 * BH), ALU.mult).then_inc(*did("rope1"))
                    dve.wait_ge(*filled(("k1", f)))
                    o = result(("k1", f))
                    tt(tokens(kt1[f]), tokens(o[:, 0:NH]), table("cosk", BH), ALU.mult).then_inc(*did())
                    tt(tokens(kt2[f]), tokens(o[:, NH:2 * NH]), table("sink", BH), ALU.mult).then_inc(*did("rope1"))
                    dve.wait_ge(*did.latest())
                    tt(q1[f], t1a[f], t1b[f], ALU.add).then_inc(*did())
                    tt(k1[f], kt1[f], kt2[f], ALU.add).then_inc(*did())
                    dve.wait_ge(*did.latest())
                    for d in LAGS:
                        tt(pr1[f][d].rearrange("p m (b l) -> p m b l", l=L - d), tokens(q1[f])[:, :, :, d:],
                           over(tokens(k1[f])[:, :, :L - d], CT), ALU.mult)\
                            .then_inc(*did("s1_prod"))
                for f in HALVES:
                    dve.wait_ge(S["s1_copied"], L * (f + 1))
                    reduce(s1m[f], s1[f], ALU.max).then_inc(*did())
                    dve.wait_ge(*did.latest())
                    tt(s1[f], s1[f], last(s1m[f], L), ALU.subtract).then_inc(*did("s1_shift"))
                for f in HALVES:
                    dve.wait_ge(S["s1_exp"], f + 1)
                    reduce(s1s[f], s1e[f], ALU.add).then_inc(*did())
                    dve.wait_ge(*did.latest())
                    dve.reciprocal(s1r[f], s1s[f]).then_inc(*did())
                    dve.wait_ge(*did.latest())
                    dve.wait_ge(S["v1_copied"], f + 1)
                    by = s1e[f].rearrange("p (m b l) d -> p m b l d", m=CT, l=L)
                    ov, tv = tokens(o1[f]), tokens(t1[f])
                    tt(ov, by[:, :, :, :, 0], over(tokens(v1[f]), CT), ALU.mult).then_inc(*did())
                    for d in range(1, L):
                        tt(tv[:, :, :, d:], by[:, :, :, d:, d], over(tokens(v1[f])[:, :, :L - d], CT), ALU.mult)\
                            .then_inc(*did())
                        dve.wait_ge(*did.latest())
                        tt(ov[:, :, :, d:], ov[:, :, :, d:], tv[:, :, :, d:], ALU.add).then_inc(*did())
                        dve.wait_ge(*did.latest())
                    tt(o1[f], o1[f], s1r[f].rearrange("p (m n) -> p m n", m=CT), ALU.mult).then_inc(*did("a1_out"))
                for f in HALVES:
                    residual("wo1", h[0], f, "z_attn1")
                norm_half(2, h[1])

            def ternary():
                dve.wait_ge(S["packed_in"], 16)
                wi = wint[:, :].rearrange("p (c r) -> p c r", c=2)
                we = wenc[:, :].rearrange("p (c o) -> p c o", c=2)
                for k in range(4):
                    ts(we[:, :, k * 64:(k + 1) * 64], wi, 2 * k, 3, ALU.logical_shift_right, ALU.bitwise_and)\
                        .then_inc(*did())
                dve.wait_ge(*did.latest())
                ts(wT[:, :], wenc[:, :], -1.0, None, ALU.add).then_inc(*did())
                for f in HALVES:
                    t2 = slice(2 * f, 2 * f + 2)
                    dve.wait_ge(*filled(("xtok", f)))
                    o = result(("xtok", f))
                    copy(x_tok[:, t2], o[0:TN, :].rearrange("p (t c) -> p t c", t=2)).then_inc(*did("x_tok_copied"))
                    dve.wait_ge(*did.latest())
                    dve.tensor_reduce(amax[:, t2], x_tok[:, t2], AX.X, ALU.max, apply_absolute_value=True).then_inc(*did())
                    dve.wait_ge(*did.latest())
                    ts(amax[:, t2], amax[:, t2], 1e-5, None, ALU.max).then_inc(*did())
                    dve.wait_ge(*did.latest())
                    dve.reciprocal(asc[:, t2], amax[:, t2]).then_inc(*did())
                    dve.wait_ge(*did.latest())
                    ts(asc[:, t2], asc[:, t2], 127.0, None, ALU.mult).then_inc(*did())
                    ts(ainv[:, t2], amax[:, t2], 1.0 / 127.0, sm("l1_scale", 0, TN), ALU.mult, ALU.mult)\
                        .then_inc(*did())
                    dve.wait_ge(*did.latest())
                    for t in range(2 * f, 2 * f + 2):
                        ts(xq[:, t], x_tok[:, t], asc[:, t:t + 1], MAGIC, ALU.mult, ALU.add).then_inc(*did())
                    dve.wait_ge(*did.latest())
                    ts(xq[:, t2], xq[:, t2], -MAGIC, 127.0, ALU.add, ALU.min).then_inc(*did())
                    dve.wait_ge(*did.latest())
                    ts(xq[:, t2], xq[:, t2], -128.0, None, ALU.max).then_inc(*did("x_int"))
                for f in HALVES:
                    dve.wait_ge(*filled(("xint", f)))
                    o = result(("xint", f))
                    copy(half(xT, f), two(o)).then_inc(*did("xint_copied"))
                for f in HALVES:
                    t2 = slice(2 * f, 2 * f + 2)
                    dve.wait_ge(*filled(("l1f", f)))
                    o = result(("l1f", f))
                    for i in range(2):
                        stt(y_tok[:, 2 * f + i], o[0:TN, i * C:(i + 1) * C], ainv[:, 2 * f + i:2 * f + i + 1],
                            sm("l1_bias", rows=TN), ALU.mult, ALU.add)\
                            .then_inc(*did("l1f_read" if i else None))
                    dve.wait_ge(*did.latest())
                    tt(y_tok[:, t2], y_tok[:, t2], x_tok[:, t2], ALU.add).then_inc(*did())
                    dve.wait_ge(*did.latest())
                    for t in range(2 * f, 2 * f + 2):
                        dve.bn_stats(stats[:, t], y_tok[:, t]).then_inc(*did())
                    dve.wait_ge(*did.latest())
                    for t in range(2 * f, 2 * f + 2):
                        dve.bn_aggr(aggr[:, t], stats[:, t]).then_inc(*did("l1f_var" if t % 2 else None))
                for f in HALVES:
                    dve.wait_ge(S["l1f_rstd"], f + 1)
                    for t in range(2 * f, 2 * f + 2):
                        ts(y_tok[:, t], y_tok[:, t], aggr[:, t, 0:1], trs[:, t:t + 1], ALU.subtract, ALU.mult)\
                            .then_inc(*did("h4_tok" if t % 2 else None))
                for f in HALVES:
                    dve.wait_ge(*filled(("h4", f)))
                    o = result(("h4", f))
                    copy(half(h[0], f), two(o)).then_inc(*did("h4_copied"))

            def attention2():
                for f in HALVES:
                    for j in range(QT2 // 2):
                        dve.wait_ge(*filled(("k2", f, j)))
                        o = result(("k2", f, j))
                        copy(half(k2, f)[:, 2 * j:2 * j + 2], two(o)).then_inc(*did("k2_copied"))

                def shifted(t):
                    for g in range(4):
                        dve.wait_ge(*filled(("s2", t, g)))
                        o = result(("s2", t, g))
                        tt(s2[:, t, 4 * g:4 * g + 4], o[0:TN, 0:4 * TN].rearrange("p (h k) -> p h k", h=4),
                           over(sm("attmask", rows=TN), 4), ALU.add)\
                            .then_inc(*did("s2_masked"))
                    dve.wait_ge(*did.latest())
                    reduce(s2m[:, t], s2[:, t], ALU.max).then_inc(*did())
                    dve.wait_ge(*did.latest())
                    tt(s2[:, t], s2[:, t], last(s2m[:, t], TN), ALU.subtract).then_inc(*did("s2_shift"))

                def weights(t):
                    dve.wait_ge(S["s2_exp"], t + 1)
                    reduce(s2s[:, t], s2[:, t], ALU.add).then_inc(*did())
                    dve.wait_ge(*did.latest())
                    dve.reciprocal(s2r[:, t], s2s[:, t]).then_inc(*did())
                    dve.wait_ge(*did.latest())
                    tt(s2[:, t], s2[:, t], last(s2r[:, t], TN), ALU.mult).then_inc(*did("s2_prob"))

                def heads_out(t):
                    for g in range(2):
                        dve.wait_ge(*filled(("o2", t, g)))
                        o = result(("o2", t, g))
                        copy(o2[:, 4 * g:4 * g + 4, t * TN:(t + 1) * TN],
                             o[:, 0:4 * TN].rearrange("p (m q) -> p m q", m=4))\
                            .then_inc(*did("o2_copied"))

                shifted(0)
                shifted(1)
                for t in range(TT):
                    weights(t)
                    if t + 2 < TT:
                        shifted(t + 2)
                    if t == 3:
                        residual("r2", h[0], 0, "z_attn2")
                        centre(3, 0)
                    heads_out(t)
                scale(3, 0, h[1])
                residual("r2", h[0], 1, "z_attn2")
                centre(3, 1)
                scale(3, 1, h[1])

            def coupling():
                dve.wait_ge(*did.latest())
                ts(r2[:, 0:1], sm("gc_b3"), 0.5, None, ALU.mult).then_inc(*did())
                ts(r2[:, 1:2], sm("cn_b4"), 0.5, None, ALU.mult).then_inc(*did())
                for f in HALVES:
                    for m in range(CT):
                        reduce(gmn[f][:, m], tokens(half(h[1], f)[:, m]), ALU.add).then_inc(*did())
                    dve.wait_ge(*did.latest())
                    ts(gmn[f], gmn[f], 1.0 / L, None, ALU.mult).then_inc(*did("gmean"))
                for f in HALVES:
                    dve.wait_ge(S["gc_act"], 4 + f + 1)
                    ts(gf[f], gf[f], 0.7, None, ALU.mult).then_inc(*did())
                dve.wait_ge(*did.latest())
                for cyc in range(3):
                    for f in HALVES:
                        x = half(h[1], f) if cyc == 0 else cout[(cyc - 1) % 2][f]
                        y = cout[cyc % 2][f]
                        c = coup[f]
                        dve.wait_ge(S["c4_act"], CT * cyc + f + 1)
                        stt(tokens(c), tokens(cn_t[f]), 0.3, last(gf[f], L), ALU.mult, ALU.add).then_inc(*did())
                        dve.wait_ge(*did.latest())
                        ts(c, c, sm("range"), 0.1, ALU.mult, ALU.add).then_inc(*did())
                        dve.wait_ge(*did.latest())
                        ts(c, c, sm("sign"), None, ALU.mult).then_inc(*did())
                        dve.wait_ge(*did.latest())
                        tt(ctmp[f][:, 0], c, x[:, 1], ALU.mult).then_inc(*did())
                        tt(ctmp[f][:, 1], c, x[:, 0], ALU.mult).then_inc(*did())
                        dve.wait_ge(*did.latest())
                        tt(y[:, 0], x[:, 0], ctmp[f][:, 0], ALU.add).then_inc(*did())
                        tt(y[:, 1], x[:, 1], ctmp[f][:, 1], ALU.subtract).then_inc(*did("c_out"))
                dve.wait_ge(*did.latest())
                for f in HALVES:
                    tt(half(z, f), half(h[1], f), cout[0][f], ALU.add).then_inc(*did("z_ffn2"))
                norm_half(4, h[0])

            def attention3():
                flat = "p m n -> p (m n)"
                for f in HALVES:
                    dve.wait_ge(*filled(("gk2", f)))
                    o = result(("gk2", f))
                    for m in range(CT):
                        c = two(o)[:, m]
                        ts(gmin[f][:, m], c, sm("bgk2", m), 0.0, ALU.add, ALU.min).then_inc(*did())
                        ts(gaz[f][:, m], c, sm("bgk2", m), None, ALU.add)\
                            .then_inc(*did("gk_min" if m == CT - 1 else None))
                    dve.wait_ge(*did.latest())
                    stt(gaz[f], gmin[f], -2.0, gaz[f], ALU.mult, ALU.add).then_inc(*did("gk_abs"))
                dve.wait_ge(S["keep_set"], 1)
                for f in HALVES:
                    dve.wait_ge(S["gk_log"], f + 1)
                    tt(gmin[f], gmin[f], gaz[f], ALU.subtract).then_inc(*did())
                    dve.wait_ge(*did.latest())
                    ts(gmin[f], gmin[f], 1.0 / 16.0, None, ALU.mult).then_inc(*did())
                    dve.wait_ge(*did.latest())
                    dve.tensor_tensor_scan(gcum[f].rearrange(flat), keep, gmin[f].rearrange(flat),
                                               0.0, ALU.mult, ALU.add).then_inc(*did())
                    dve.wait_ge(*did.latest())
                    gt = tokens(gcum[f])
                    for d in range(1, L):
                        tt(gdf_d[f][d].rearrange("p m (b l) -> p m b l", l=L - d), gt[:, :, :, d:],
                           gt[:, :, :, :L - d], ALU.subtract)\
                            .then_inc(*did("g_diff" if d == L - 1 else None))
                for f in HALVES:
                    dve.wait_ge(S["qkv3_copied"], 2 * f + 2)
                    qt, kt = tokens(q3[f]), tokens(k3[f])
                    for d in LAGS:
                        tt(pr3_d[f][d].rearrange("p m (b l) -> p m b l", l=L - d), qt[:, :, :, d:],
                           kt[:, :, :, :L - d], ALU.mult)\
                            .then_inc(*did("s3_prod" if d == 0 else None))
                    dve.wait_ge(*did.latest())
                    dve.wait_ge(S["g_exp"], f + 1)
                    for d in range(1, L):
                        tt(pr3_d[f][d], pr3_d[f][d], gdf_d[f][d], ALU.mult).then_inc(*did("s3_prod"))
                i = 0
                for f in HALVES:
                    dve.wait_ge(S["qkv3_copied"], 4 + 2 * (f + 1))
                    adds = []
                    for d in LAGS:
                        for odd in range(2):
                            dve.wait_ge(*filled(("s3", f, d, odd)))
                            o = result(("s3", f, d, odd))
                            src = two(o)[:, :, 0:BH * (L - d)].rearrange("p m (b l) -> p m b l", l=L - d)
                            dst = tokens(o3[f][:, odd::2])[:, :, :, d:]
                            tmp = dst if d == 0 else tokens(t3[i % 4])[:, :, :, d:]
                            tt(tmp, src, tokens(v3[f][:, odd::2])[:, :, :, :L - d], ALU.mult).then_inc(*did("s3_mul"))
                            i += 1
                            if adds:
                                a_dst, a_tmp, a_i = adds.pop()
                                dve.wait_ge(S["s3_mul"], a_i)
                                tt(a_dst, a_dst, a_tmp, ALU.add).then_inc(*did())
                            if d:
                                adds.append((dst, tmp, i))
                    a_dst, a_tmp, a_i = adds.pop()
                    dve.wait_ge(S["s3_mul"], a_i)
                    tt(a_dst, a_dst, a_tmp, ALU.add).then_inc(*did("o3_sum"))
                    dve.wait_ge(S["o3_sum"], f + 1)
                for f in HALVES:
                    dve.wait_ge(S["o3_rstd"], f + 1)
                    stt(o3[f].rearrange(flat), o3[f].rearrange(flat), sm("gnorm"), rs3[f].rearrange(flat),
                        ALU.mult, ALU.mult).then_inc(*did())
                    dve.wait_ge(*did.latest())
                    dve.wait_ge(S["g3_silu"], 2 * (f + 1))
                    tt(o3[f], o3[f], sg3[f], ALU.mult).then_inc(*did("o3_out"))
                for f in HALVES:
                    residual("wo3", h[0], f, "z_attn3")
                norm_half(5, h[1])

            def last_ffn():
                i = 0
                for f in HALVES:
                    for m in range(HT3):
                        i += 1
                        dve.wait_ge(S["f1_silu"], i)
                        dve.wait_ge(*filled(("w2", f, m)))
                        o = result(("w2", f, m))
                        stt(half(fa, f)[:, m], o[:, 0:NH], sm("w2_s", m), fsil[i % 2], ALU.mult, ALU.mult)\
                            .then_inc(*did("f_gate"))
                for f in HALVES:
                    dve.wait_ge(*filled(("f3", f)))
                    o = result(("f3", f))
                    for m in range(CT):
                        stt(half(z, f)[:, m], two(o)[:, m], sm("w3_s", m), half(h[1], f)[:, m], ALU.mult, ALU.add)\
                            .then_inc(*did("z_ffn3" if m == CT - 1 else None))
                norm_half(6, h[0])
                for f in HALVES:
                    dve.wait_ge(*filled(("out", f)))
                    o = result(("out", f))
                    copy(otok[:, 2 * f:2 * f + 2], o[0:TN, :].rearrange("p (t c) -> p t c", t=2))\
                        .then_inc(*did("tok_out"))

            for f in [tokenizer, state_space, experts, attention1, ternary, attention2, coupling, attention3, last_ffn]:
                f()

        @block.scalar
        def _(act):
            did = Counts(S, "act_step")
            act_fn = act.activation

            ln_at = [0]

            def norm(key, n):
                i = ln_at[0] = ln_at[0] + 1
                act.wait_ge(S["ln_xc"], i)
                act_fn(sq[:, :, 0:n], xc[:, :, 0:n], ACT.Square).then_inc(*did("ln_sq"))
                act.wait_ge(*filled((key, "var")))
                var = result((key, "var"))[:, 0:n]
                act_fn(SQ[:, 0:n], var, ACT.Ln, bias=sm("eps")).then_inc(*did("ln_logvar"))
                act.wait_ge(*did.latest())
                act_fn(SQ[:, N:N + n], SQ[:, 0:n], ACT.Exp, scale=-0.5).then_inc(*did("ln_rstd"))

            def square(i, f):
                act.wait_ge(S["ln_xc"], norm_at(i, f))
                act_fn(sqh[f], half(xc, f), ACT.Square).then_inc(*did("ln_sq"))

            def rstd(i, f):
                act.wait_ge(*filled(("var", i, f)))
                o = result(("var", i, f))
                act_fn(sqh[f][:, 0], o[:, 0:NH], ACT.Ln, bias=sm("eps")).then_inc(*did("ln_logvar"))
                act.wait_ge(*did.latest())
                act_fn(sqh[f][:, 1], sqh[f][:, 0], ACT.Exp, scale=-0.5).then_inc(*did("ln_rstd"))

            def norm_half(i):
                for f in HALVES:
                    square(i, f)
                for f in HALVES:
                    rstd(i, f)

            def tokenizer():
                act.preload_act_table_set("natural_log_exp_and_others")
                act.wait_ge(S["small_in"], 16)
                norm("cls", 1)
                for j in range(NCH + 2):
                    if j < NCH:
                        n = min(CHUNK, NP - j * CHUNK)
                        act.wait_ge(*filled(("conv", j, 1)))
                        o = result(("conv", j, 1))
                        act_fn(pe_all[:, 1, j * CHUNK:j * CHUNK + n], o[:, 0:n], ACT.Copy)\
                            .then_inc(*did("pe1_copied"))
                    if 1 <= j <= NCH:
                        i = j - 1
                        n = min(CHUNK, NP - i * CHUNK)
                        c = slice(i * CHUNK, i * CHUNK + n)
                        act.wait_ge(S["w_xc"], i + 1)
                        act_fn(sq_all[:, :, c], xn_all[:, :, c], ACT.Square).then_inc(*did("w_sq"))
                    if j >= 2:
                        i = j - 2
                        n = min(CHUNK, NP - i * CHUNK)
                        act.wait_ge(*filled(("wvar", i)))
                        o = result(("wvar", i))
                        if i:
                            act.wait_ge(S["w_rstd"], i)
                        act_fn(w_log[:, 0:n], o[:, 0:n], ACT.Ln, bias=sm("eps")).then_inc(*did("w_logvar"))
                        act.wait_ge(*did.latest())
                        if i:
                            act.wait_ge(S["w_xn"], i)
                        act_fn(w_rs[:, 0:n], w_log[:, 0:n], ACT.Exp, scale=-0.5).then_inc(*did("w_rstd"))
                norm("red", NW)
                for t in range(2):
                    act.wait_ge(*filled(("q", t)))
                    o = result(("q", t))
                    act_fn(q_w[:, t], o[:, 0:C], ACT.Copy, scale=float(C) ** -0.5).then_inc(*did("q_copied"))
                i = 0
                for t in range(2):
                    for k in range(TAPS):
                        i += 1
                        act.wait_ge(S["kq_done"], i)
                        act.wait_ge(*filled(("kv", k, t)))
                        o = result(("kv", k, t))
                        act_fn(v_w[:, t, k], o[:, C:2 * C], ACT.Copy).then_inc(*did("v_copied"))
                    act.wait_ge(S["la_shift"], t + 1)
                    act_fn(sc_e[:, t], sc_e[:, t], ACT.Exp).then_inc(*did("la_exp"))
                norm("lo", NW)
                act.wait_ge(*filled("gk"))
                o = result("gk")
                act_fn(gkT.rearrange("p m w -> p (m w)"), o[:, :], ACT.Copy).then_inc(*did("gk_copied"))
                act.wait_ge(S["gs_shift"], 1)
                act_fn(gse, gs, ACT.Exp).then_inc(*did("gs_exp"))

            def state_space():
                act.wait_ge(S["a_clip"], 1)
                act_fn(negA, negA, ACT.Exp).then_inc(*did("a_exp"))
                act.wait_ge(S["u_conv"], DIT)
                act_fn(u, u_raw, ACT.Silu).then_inc(*did("u_silu"))
                for m in range(DIT):
                    act.wait_ge(*filled(("win", DIT + m)))
                    o = result(("win", DIT + m))
                    act_fn(sres[:, m], o[:, 0:N], ACT.Silu).then_inc(*did("res_silu"))
                act.preload_act_table_set("natural_log_exp_and_others")
                for m in range(DIT):
                    act.wait_ge(*filled(("wdt", m)))
                    o = result(("wdt", m))
                    act_fn(az[:, m], o[:, 0:N], ACT.Abs, bias=sm("b_dt", m)).then_inc(*did("dt_abs"))
                act.wait_ge(*did.latest())
                act_fn(e1, az, ACT.Exp, scale=-1.0).then_inc(*did("dt_exp"))
                act.wait_ge(S["dt_exp1"], 1)
                act_fn(az, w1, ACT.Ln).then_inc(*did("dt_log"))
                for n in range(NS):
                    act.wait_ge(S["arg"], n + 1)
                    a = arg[n % 2].rearrange("p m (b l) -> p (m b) l", l=L)[:, :, 1:]
                    act_fn(a, a, ACT.Exp).then_inc(*did("decay"))
                norm_half(0)

            def experts():
                act.wait_ge(S["gate_shift"], 1)
                act_fn(ex, ex, ACT.Exp).then_inc(*did("gate_exp"))
                for e in range(NE):
                    act.wait_ge(*filled(("comb", e)))
                    o = result(("comb", e))
                    if e >= 2:
                        act.wait_ge(S["moe_act"], HIDT * (e - 1))
                    act_fn(combb[e % 2], o[:, 0:N], ACT.Copy).then_inc(*did("combine_copied"))
                    for m in range(HIDT):
                        i = e * HIDT + m
                        act.wait_ge(*filled(("W1", e, m)))
                        o = result(("W1", e, m))
                        if i >= 2:
                            act.wait_ge(S["gated"], i - 1)
                        act_fn(sil[i % 2], o[:, 0:N], ACT.Silu).then_inc(*did("silu_h"))
                act.preload_act_table_set("natural_log_exp_and_others")
                norm_half(1)

            def attention1():
                for f in HALVES:
                    act.wait_ge(*filled(("v1", f)))
                    o = result(("v1", f))
                    act_fn(v1[f], o[:, 0:NH], ACT.Copy).then_inc(*did("v1_copied"))
                act.wait_ge(S["s1_clear"], 2)
                for f in HALVES:
                    by = s1[f].rearrange("p (m b l) d -> p m b l d", m=CT, l=L)
                    for d in LAGS:
                        act.wait_ge(*filled(("s1", f, d)))
                        o = result(("s1", f, d))
                        act_fn(by[:, :, :, d:, d],
                               two(o)[:, :, 0:BH * (L - d)].rearrange("p m (b l) -> p m b l", l=L - d), ACT.Copy)\
                            .then_inc(*did("s1_copied"))
                for f in HALVES:
                    act.wait_ge(S["s1_shift"], f + 1)
                    act_fn(s1e[f], s1[f], ACT.Exp).then_inc(*did("s1_exp"))
                norm_half(2)

            def ternary():
                for f in HALVES:
                    act.wait_ge(S["l1f_var"], f + 1)
                    act_fn(tmean[:, 2 * f:2 * f + 2], aggr[:, 2 * f:2 * f + 2, 1], ACT.Ln, bias=sm("eps", rows=TN))\
                        .then_inc(*did())
                    act.wait_ge(*did.latest())
                    act_fn(trs[:, 2 * f:2 * f + 2], tmean[:, 2 * f:2 * f + 2], ACT.Exp, scale=-0.5)\
                        .then_inc(*did("l1f_rstd"))

            def attention2():
                for f in HALVES:
                    for j in range(QT2 // 2):
                        act.wait_ge(*filled(("q2", f, j)))
                        o = result(("q2", f, j))
                        act_fn(half(q2, f)[:, 2 * j:2 * j + 2], two(o), ACT.Copy, scale=float(HD2) ** -0.5)\
                            .then_inc(*did("q2_copied"))

                def exps(t):
                    act.wait_ge(S["s2_shift"], t + 1)
                    act_fn(s2[:, t], s2[:, t], ACT.Exp).then_inc(*did("s2_exp"))

                exps(0)
                for t in range(TT):
                    for hf in range(2):
                        act.wait_ge(*filled(("v2", t, hf)))
                        o = result(("v2", t, hf))
                        act_fn(v2[:, t, hf * 512:(hf + 1) * 512], o[0:TN, :], ACT.Copy).then_inc(*did("v2_copied"))
                    if t + 1 < TT:
                        exps(t + 1)
                    for g in range(4):
                        act.wait_ge(*filled(("pT", t, g)))
                        o = result(("pT", t, g))
                        act_fn(pT[t % 2][:, 4 * g:4 * g + 4], o[0:TN, 0:4 * TN].rearrange("p (h q) -> p h q", h=4),
                               ACT.Copy).then_inc(*did("pT_copied"))
                square(3, 0)
                rstd(3, 0)
                square(3, 1)
                rstd(3, 1)

            def coupling():
                act.preload_act_table_set("gelu_and_others")

                def first(cyc, f):
                    act.wait_ge(*filled(("c1", cyc, f)))
                    o = result(("c1", cyc, f))
                    for m in range(CT):
                        act_fn(cn_a[f][:, m], two(o)[:, m], ACT.Gelu, bias=sm("cn_b1", m))\
                            .then_inc(*did("c1_act" if m == CT - 1 else None))

                for f in HALVES:
                    act.wait_ge(*filled(("gc1", f)))
                    o = result(("gc1", f))
                    act_fn(gc_a[f], o[:, 0:BH], ACT.Gelu, bias=sm("gc_b1")).then_inc(*did("gc_act"))
                    first(0, f)
                for f in HALVES:
                    act.wait_ge(*filled(("gc2", f)))
                    o = result(("gc2", f))
                    act_fn(gc_b[f], o[0:64, 0:BH], ACT.Gelu, bias=sm("gc_b2", rows=64)).then_inc(*did("gc_act"))
                for f in HALVES:
                    act.wait_ge(*filled(("gc3", f)))
                    o = result(("gc3", f))
                    act_fn(gf[f], o[:, 0:BH], ACT.Tanh, scale=0.5, bias=r2[:, 0:1]).then_inc(*did("gc_act"))
                for cyc in range(3):
                    if cyc:
                        for f in HALVES:
                            first(cyc, f)
                    for f in HALVES:
                        act.wait_ge(*filled(("c2", cyc, f)))
                        o = result(("c2", cyc, f))
                        act_fn(cn_b[f], o[:, 0:NH], ACT.Gelu, bias=sm("cn_b2")).then_inc(*did("c2_act"))
                    for f in HALVES:
                        act.wait_ge(*filled(("c3", cyc, f)))
                        o = result(("c3", cyc, f))
                        act_fn(cn_c[f], o[0:64, 0:NH], ACT.Gelu, bias=sm("cn_b3", rows=64)).then_inc(*did("c3_act"))
                    for f in HALVES:
                        act.wait_ge(*filled(("c4", cyc, f)))
                        o = result(("c4", cyc, f))
                        act_fn(cn_t[f], o[:, 0:NH], ACT.Tanh, scale=0.5, bias=r2[:, 1:2]).then_inc(*did("c4_act"))
                act.preload_act_table_set("natural_log_exp_and_others")
                norm_half(4)

            def attention3():
                for f in HALVES:
                    act.wait_ge(*filled(("gk1", f)))
                    o = result(("gk1", f))
                    act_fn(gk1[f], o[0:RANK, 0:NH], ACT.Copy).then_inc(*did("gk1_copied"))
                    act.wait_ge(*filled(("q3", f)))
                    o = result(("q3", f))
                    act_fn(q3[f], two(o), ACT.Copy, scale=0.125).then_inc(*did("qkv3_copied"))
                    act.wait_ge(*filled(("k3", f)))
                    o = result(("k3", f))
                    act_fn(k3[f], two(o), ACT.Copy).then_inc(*did("qkv3_copied"))
                for f in HALVES:
                    act.wait_ge(S["gk_abs"], f + 1)
                    act_fn(gaz[f], gaz[f], ACT.Exp, scale=-1.0).then_inc(*did("gk_exp"))
                    act.wait_ge(*did.latest())
                    act_fn(gaz[f], gaz[f], ACT.Ln, bias=sm("one")).then_inc(*did("gk_log"))
                for f in HALVES:
                    for j in range(2):
                        act.wait_ge(*filled(("v3", f, j)))
                        o = result(("v3", f, j))
                        act_fn(v3[f][:, 2 * j:2 * j + 2], two(o), ACT.Copy).then_inc(*did("qkv3_copied"))
                for f in HALVES:
                    act.wait_ge(S["g_diff"], f + 1)
                    late = view(PAT, D3 + CT * (PAIRS * f + PAIR_OFF[1]), CT * (PAIRS - PAIR_OFF[1]))
                    act_fn(late, late, ACT.Exp).then_inc(*did("g_exp"))
                for f in HALVES:
                    for j in range(2):
                        act.wait_ge(*filled(("g3", f, j)))
                        o = result(("g3", f, j))
                        act_fn(sg3[f][:, 2 * j:2 * j + 2], two(o), ACT.Silu).then_inc(*did("g3_silu"))
                act.preload_act_table_set("natural_log_exp_and_others")
                for f in HALVES:
                    act.wait_ge(S["o3_sum"], f + 1)
                    act_fn(osq[f], o3[f], ACT.Square).then_inc(*did("o3_sq"))
                for f in HALVES:
                    for j in range(2):
                        act.wait_ge(*filled(("ms3", f, j)))
                        o = result(("ms3", f, j))
                        act_fn(rs3[f][:, 2 * j:2 * j + 2], two(o), ACT.Ln, bias=sm("eps")).then_inc(*did("o3_logvar"))
                    act.wait_ge(*did.latest())
                    act_fn(rs3[f], rs3[f], ACT.Exp, scale=-0.5).then_inc(*did("o3_rstd"))
                norm_half(5)

            def last_ffn():
                act.preload_act_table_set("silu_and_others")
                i = 0
                for f in HALVES:
                    for m in range(HT3):
                        i += 1
                        act.wait_ge(*filled(("w1", f, m)))
                        o = result(("w1", f, m))
                        if i > 2:
                            act.wait_ge(S["f_gate"], i - 2)
                        act_fn(fsil[i % 2], o[:, 0:NH], ACT.Silu, scale=sm("w1_s", m)).then_inc(*did("f1_silu"))
                act.preload_act_table_set("gelu_and_others")
                for m in range(HT3):
                    act.wait_ge(*filled(("h1", m)))
                    o = result(("h1", m))
                    act_fn(fb[:, m], o[:, 0:N], ACT.Gelu, scale=sm("h1_s", m)).then_inc(*did("fh1_act"))
                for m in range(HT3):
                    act.wait_ge(*filled(("h2", m)))
                    o = result(("h2", m))
                    act_fn(fa[:, m], o[:, 0:N], ACT.Gelu, scale=sm("h2_s", m)).then_inc(*did("fh2_act"))
                act.preload_act_table_set("natural_log_exp_and_others")
                norm_half(6)

            for f in [tokenizer, state_space, experts, attention1, ternary, attention2, coupling, attention3, last_ffn]:
                f()

        @block.gpsimd
        def _(pool):
            did = Counts(S, "pool_step")

            def state_space():
                pool.wait_ge(S["cls_out"], 1)
                for i in range(2):
                    pool.memset(arg[i], 0.0).then_inc(*did("arg_zero"))

            def attention1():
                pool.wait_ge(S["z_moe"], CT)
                for f in HALVES:
                    pool.memset(s1[f], FAR).then_inc(*did("s1_clear"))

            def attention3():
                pool.wait_ge(S["z_attn2"], CT)
                pool.memset(keep, 1.0).then_inc(*did())
                pool.wait_ge(*did.latest())
                pool.memset(keep.rearrange("p (x l) -> p x l", l=L)[:, :, 0], 0.0).then_inc(*did("keep_set"))

            for f in (state_space, attention1, attention3):
                f()

        @block.sync
        def _(sync):
            def load(dst, src, signal):
                sync.dma_start(dst, src).then_inc(S[signal], 16)

            load(SM[:, :], small, "small_in")
            nconv = KCT * C
            load(WTOK[:, 0:nconv], w_tok[:, 0:nconv], "conv_w_in")
            for j in range(NCH):
                n = min(CHUNK, NP - j * CHUNK)
                for k in range(KCT):
                    r = min(P, KC - k * P)
                    load(PAT[0:r, k * NP + j * CHUNK:k * NP + j * CHUNK + n],
                         patches[k * P:k * P + r, j * CHUNK:j * CHUNK + n], f"patches_in_{j}")
            load(WTOK[:, nconv:N_TOK], w_tok[:, nconv:], "tok_w_in")
            load(WMAM[:, 0:N_MAM], w_mam, "mam_w_in")
            load(wint[:, :], packed, "packed_in")
            sync.wait_ge(S["cls_out"], 1)
            for i in range(NE // 2):
                c = slice(2 * i * N_EXP, 2 * (i + 1) * N_EXP)
                sync.dma_start(BIG[:, c], w_exp[:, c]).then_inc(expert_in[i], 16)
            sync.wait_ge(S["z_mam"], CT)
            load(PAT[:, N_L2:N_L2 + N_L1], w_l1, "l1_w_in")
            load(PAT[:, 0:N_L2], w_l2, "l2_w_in")
            load(WMAM[:, 0:N_F3], w_f3, "f3_w_in")
            load(WTOK[:, 0:N_F1], w_f1, "f1_w_in")
            sync.wait_ge(S["z_attn2"], CT)
            load(PAT[:, 0:N_L3], w_l3, "l3_w_in")
            half = N_FH // 2
            for i in range(2):
                load(BIG[:, i * half:(i + 1) * half], w_fh[:, i * half:(i + 1) * half], "fh_w_in")
            for f in HALVES:
                sync.wait_ge(S["tok_out"], f + 1)
                sync.dma_start(out[f * NH:(f + 1) * NH, :].rearrange("(t p) c -> p t c", t=2),
                               otok[:, 2 * f:2 * f + 2]).then_inc(S["stored"], 16)
            sync.wait_ge(S["stored"], 16 * len(HALVES))


def layout(x):
    def cols(v):
        return np.ascontiguousarray(v.reshape(-1, P).T)

    def wt(w):
        k = w.shape[0] // P
        return w.reshape(k, P, w.shape[1]).transpose(1, 0, 2).reshape(P, -1)

    def low(w):
        return np.concatenate([w, np.zeros((P - w.shape[0], w.shape[1]), w.dtype)])

    def rep(v):
        return np.broadcast_to(v.reshape(1, -1), (P, v.size))

    f = np.float32
    p = np.arange(P)
    pos = np.arange(L, dtype=np.float64)
    freq = 1.0 / 1000.0 ** (np.arange(0, HD1, 2) / HD1)
    ang = pos[None, :] * freq[p % 8][:, None]
    side = np.where(p % HD1 < 8, -1.0, 1.0)[:, None]
    tok = np.arange(TN)
    same = (tok[:, None] // L) == (tok[None, :] // L)
    mask = np.where(same, np.where(tok[None, :] > tok[:, None], -50.0, 0.0), FAR)
    e = np.arange(NE)
    g = {k: v for k, v in x.items()}
    parts = {
        "ident": np.eye(P), "same32": p[:, None] // 32 == p[None] // 32, "same16": p[:, None] // 16 == p[None] // 16,
        "inv256": np.full((P, 1), 1 / 256), "inv128": np.full((P, 1), 1 / 128), "one": np.ones((P, 1)),
        "eps": np.full((P, 1), EPS), "sign": np.where(p < 64, 1.0, -1.0)[:, None],
        "before": rep((e[None, :] < e[:, None]).astype(f)), "cosq": np.cos(ang) / 4, "sinq": side * np.sin(ang) / 4,
        "cosk": np.cos(ang), "sink": side * np.sin(ang), "attmask": low(mask),
        "W_conv": g["L0_attn_W_conv"].reshape(4, P, 3).transpose(1, 0, 2).reshape(P, 12),
        "b_dt": cols(g["L0_attn_b_dt"]), "A_log": g["L0_attn_A_log"].reshape(4, P, NS).transpose(1, 0, 2).reshape(P, 64),
        "D_param": cols(g["L0_attn_D_param"]), "Wr": wt(g["L0_ffn_Wr"]),
        "l1_bias": rep(g["L1_ffn_bias"]), "l1_scale": rep(g["L1_ffn_weight_scale"]),
        "cn_b1": cols(g["L2_ffn_cn_b1"]), "cn_b2": cols(g["L2_ffn_cn_b2"]), "cn_b3": low(g["L2_ffn_cn_b3"].reshape(-1, 1)),
        "cn_b4": rep(g["L2_ffn_cn_b4"]), "gc_b1": cols(g["L2_ffn_gc_b1"]), "gc_b2": low(g["L2_ffn_gc_b2"].reshape(-1, 1)),
        "gc_b3": rep(g["L2_ffn_gc_b3"]), "range": rep(g["L2_ffn_adaptive_range"]), "bgk2": cols(g["L3_attn_bgk2"]),
        "gnorm": g["L3_attn_g_norm_weight"].reshape(P, 1), "w1_s": cols(g["L3_ffn_w1_s"]), "w2_s": cols(g["L3_ffn_w2_s"]),
        "h1_s": cols(g["L3_ffn_h1_s"]), "h2_s": cols(g["L3_ffn_h2_s"]), "w3_s": cols(g["L3_ffn_w3_s"]),
    }
    for n in ("la_ln_q_g", "la_ln_q_b", "la_ln_kv_g", "la_ln_kv_b", "la_proj_b", "ga_ln_q_g", "ga_ln_q_b", "ga_ln_kv_g",
              "ga_ln_kv_b", "ga_proj_b", "mod_b", "class_emb"):
        parts[n] = cols(g["L0_tok_" + n])
    small = np.concatenate([np.asarray(parts[n]).astype(f) if parts[n].dtype != f else parts[n] for n in SMALL], axis=1)
    im = g["x"][:, :, :84, :84].reshape(B, 3, 2, 3, PATCH, 2, 3, PATCH)
    patches = im.transpose(1, 4, 7, 3, 6, 0, 2, 5).reshape(KC, NP)
    conv = g["L0_tok_conv_w"].reshape(C, KC).T
    conv = np.concatenate([conv, np.zeros((KCT * P - KC, C), f)])
    t = "L0_tok_"
    w_tok = [wt(conv)] + [wt(g[t + n]) for n in ("la_wq", "la_wkv", "la_proj_w", "ga_wq", "ga_wkv", "ga_proj_w", "mod_w")]
    a = "L0_attn_"
    w_mam = [wt(g[a + "W_in"]), wt(g[a + "W_x"]), low(g[a + "W_dt"]), wt(g[a + "W_out"])]
    w_exp = [wt(g["L0_ffn_" + n][i]) for i in range(NE) for n in ("W1", "W3", "W2")]
    w_l2 = [wt(g["L2_attn_" + n]) for n in ("Wq", "Wk", "Wv", "Wr")]
    straight = np.concatenate([np.arange(0, HD1, 2), np.arange(1, HD1, 2)])
    turned = np.concatenate([np.arange(1, HD1, 2), np.arange(0, HD1, 2)])
    heads = np.arange(H16)[:, None] * HD1
    wq, wk, wv = g["L1_attn_wq"].T, g["L1_attn_wk"], g["L1_attn_wv"]
    w_l1 = [wt(wq[:, (heads + straight).reshape(-1)]), wt(wq[:, (heads + turned).reshape(-1)]),
            wt(np.tile(wk[:, straight], (1, 8))), wt(np.tile(wk[:, turned], (1, 8))), wt(np.tile(wv, (1, 8))),
            wt(g["L1_attn_wo"].T)]
    w_f1 = [wt(g["L3_ffn_w1_w"].T), wt(g["L3_ffn_w2_w"].T)]
    n2 = "L2_ffn_"
    w_f3 = [wt(g["L3_ffn_w3_w"].T), wt(g[n2 + "cn_w1"]), wt(g[n2 + "cn_w2"]), g[n2 + "cn_w3"], low(g[n2 + "cn_w4"]),
            wt(g[n2 + "gc_w1"]), g[n2 + "gc_w2"], low(g[n2 + "gc_w3"])]
    b = "L3_attn_"
    w_l3 = [wt(g[b + "Wq"]), wt(g[b + "Wk"]), wt(g[b + "Wv"]), wt(g[b + "Wg"]), wt(g[b + "Wgk1"]), low(g[b + "Wgk2"]),
            wt(g[b + "Wo"])]
    w_fh = [wt(g["L3_ffn_h1_w"].T), wt(g["L3_ffn_h2_w"].T)]
    packed = wt(g["L1_ffn_packed_weight"].reshape(64, C).T)
    side_by_side = {"w_tok": w_tok, "w_mam": w_mam, "w_exp": w_exp, "w_l2": w_l2, "w_l1": w_l1, "w_f1": w_f1,
                    "w_f3": w_f3, "w_l3": w_l3, "w_fh": w_fh}
    arrays = {"small": small, "packed": packed, "patches": patches}
    arrays.update({k: np.concatenate(v, axis=1) for k, v in side_by_side.items()})
    return {k: np.ascontiguousarray(v) for k, v in arrays.items()}


def kernel(**inputs):
    import concourse.bacc as bacc
    from concourse.bass_utils import run_bass_kernel_spmd

    arrays = layout({k: np.asarray(v) for k, v in inputs.items()})
    nc = bacc.Bacc("TRN2", target_bir_lowering=False, num_devices=1)
    args = {k: nc.dram_tensor("in_" + k, v.shape, mybir.dt.from_np(v.dtype), kind="ExternalInput").ap()
            for k, v in arrays.items()}
    out = nc.dram_tensor("out_0", (N, C), F32, kind="ExternalOutput").ap()
    tower(nc, out=out, **args)
    r = run_bass_kernel_spmd(nc, [{"in_" + k: v for k, v in arrays.items()}], core_ids=[0])
    return r.results[0]["out_0"].reshape(B, L, C)
```

```python
from contextlib import ExitStack

import numpy as np

import concourse.bass as bass
from concourse import mybir

F32 = mybir.dt.float32
F32R = mybir.dt.float32r
BF16 = mybir.dt.bfloat16
I32 = mybir.dt.int32
ALU = mybir.AluOpType
ACT = mybir.ActivationFunctionType
AX = mybir.AxisListType

P = 128
C = 256
CT = C // P
B = 64
L = 5
N = B * L
TT = 4
TN = N // TT
HALVES = (0, 1)
BH = B // 2
NH = N // 2
PATCH = 14
TAPS = 9
WIN = 4
NW = B * WIN
NP = NW * TAPS
KC = 3 * PATCH * PATCH
KCT = -(-KC // P)
CHUNK = 512
NCH = -(-NP // CHUNK)
H8 = 8
DH = C // H8
DI = 512
DIT = DI // P
NS = 16
RANK = 16
NE = 8
HID = 384
HIDT = HID // P
H16 = 16
HD1 = 16
HD2 = 64
QT2 = H16 * HD2 // P
LAGS = range(L)
PAIR_OFF = [0]
for _d in LAGS:
    PAIR_OFF.append(PAIR_OFF[-1] + BH * (L - _d))
PAIRS = PAIR_OFF[-1]
DH3 = 1024
HT3 = DH3 // P
EPS = 1e-5
MAGIC = 12582912.0
A_LOG_TOP = 88.7
EXP_FLOOR = -200.0
FAR = -1e30

SMALL = {}
for _n, _w in [("ident", 128), ("same32", 128), ("same16", 128), ("inv256", 1), ("inv128", 1), ("one", 1), ("eps", 1),
               ("sign", 1), ("before", 64), ("cosq", 5), ("sinq", 5), ("cosk", 5), ("sink", 5), ("attmask", 80),
               ("la_ln_q_g", 2), ("la_ln_q_b", 2), ("la_ln_kv_g", 2), ("la_ln_kv_b", 2), ("la_proj_b", 2),
               ("ga_ln_q_g", 2), ("ga_ln_q_b", 2), ("ga_ln_kv_g", 2), ("ga_ln_kv_b", 2), ("ga_proj_b", 2),
               ("mod_b", 2), ("class_emb", 2), ("W_conv", 12), ("b_dt", 4), ("A_log", 64), ("D_param", 4),
               ("Wr", 16), ("l1_bias", 256), ("l1_scale", 1), ("cn_b1", 2), ("cn_b2", 1), ("cn_b3", 1), ("cn_b4", 1),
               ("gc_b1", 1), ("gc_b2", 1), ("gc_b3", 1), ("range", 1), ("bgk2", 2), ("gnorm", 1),
               ("w1_s", 8), ("w2_s", 8), ("h1_s", 8), ("h2_s", 8), ("w3_s", 2)]:
    SMALL[_n] = (sum(w for _, w in SMALL.values()), _w)
NSMALL = sum(w for _, w in SMALL.values())


def columns(parts):
    out, at = {}, 0
    for name, kt, width in parts:
        out[name] = (at, kt, width)
        at += kt * width
    return out, at


W_TOK, N_TOK = columns([("conv", KCT, C), ("la_wq", 2, C), ("la_wkv", 2, 2 * C), ("la_proj", 2, C), ("ga_wq", 2, C),
                        ("ga_wkv", 2, 2 * C), ("ga_proj", 2, C), ("mod", 2, C)])
W_MAM, N_MAM = columns([("W_in", 2, 2 * DI), ("W_x", 4, 48), ("W_dt", 1, DI), ("W_out", 4, C)])
W_EXP, N_EXP = columns([("W1", 2, HID), ("W3", 2, HID), ("W2", 3, C)])
W_L2, N_L2 = columns([("wq", 2, 1024), ("wk", 2, 1024), ("wv", 2, 1024), ("wr", 8, C)])
W_L1, N_L1 = columns([("wqp", 2, C), ("wqr", 2, C), ("wkp", 2, P), ("wkr", 2, P), ("wv", 2, P), ("wo", 2, C)])
W_F1, N_F1 = columns([("w1", 2, DH3), ("w2", 2, DH3)])
W_F3, N_F3 = columns([("w3", 8, C), ("cn1", 2, C), ("cn2", 2, P), ("cn3", 1, 64), ("cn4", 1, 1),
                      ("gc1", 2, P), ("gc2", 1, 64), ("gc3", 1, 1)])
W_L3, N_L3 = columns([("wq", 2, C), ("wk", 2, C), ("wv", 2, 512), ("wg", 2, 512), ("gk1", 2, 16), ("gk2", 1, C),
                      ("wo", 4, C)])
W_FH, N_FH = columns([("h1", 8, DH3), ("h2", 8, DH3)])
N_PAT = max(KCT * NP, N_L2 + N_L1, N_L3)
N_BIG = max(NE * N_EXP, 4 * CT * NP, N_FH)
N_WTOK = max(N_TOK, N_F1)
N_WMAM = max(N_MAM, N_F3)
SLOT = DIT * N
N_SCR = 6 * SLOT

SIGNALS = """
small_in packed_in patches_in_0 patches_in_1 patches_in_2 patches_in_3 patches_in_4 conv_w_in tok_w_in mam_w_in
l2_w_in l1_w_in f1_w_in f3_w_in l3_w_in fh_w_in dve_step act_step pool_step cls_in ln_xc ln_sq ln_logvar ln_rstd ln_out
gq_read pe0_copied pe1_copied w_xc w_sq w_logvar w_rstd w_xn red q_copied kq_done v_copied la_shift la_exp agg
aggT_copied lo gk_copied gs_shift gs_exp gv_used gagg cls_out patch_out
u_conv u_silu res_silu xdbl_copied a_clip a_exp dt_relu dt_abs dt_exp dt_exp1 dt_log arg_zero arg decay b_used
scanned hc hc_added y_skip y_out z_mam
gate_copied gate_shift gate_exp comb comb_copied combine_copied silu_h gated moe_act act_lo act_used up_used w_hi w_lo x_lo z_moe
rope1 v1_copied s1_clear s1_prod s1_copied s1_shift s1_exp s1_sum s1_recip a1_out z_attn1
x_tok_copied x_int xint_copied l1f_read l1f_var l1f_rstd h4_tok h4_copied
q2_copied k2_copied v2_copied s2_masked s2_shift s2_exp s2_prob pT_copied o2_copied z_attn2
gmean gc_act c1_act c2_act c3_act c4_act c_out z_ffn2
qkv3_copied g3_silu gk1_copied gk_min gk_abs gk_log keep_set g_diff g_exp s3_prod s3_mul o3_sum
o3_sq o3_logvar o3_rstd o3_out z_attn3
f1_silu f_gate fh1_act fh2_act z_ffn3 tok_out stored
""".split()


class Counts:

    def __init__(self, sems, step):
        self.sems, self.step, self.count, self.last = sems, step, {}, None

    def __call__(self, signal=None):
        name = signal or self.step
        self.count[name] = self.count.get(name, 0) + 1
        self.last = name
        return self.sems[name], 1

    def latest(self):
        return self.sems[self.last], self.count[self.last]


def tower(nc, small, packed, patches, w_tok, w_mam, w_exp, w_l2, w_l1, w_f1, w_f3, w_l3, w_fh, out):
    ctx = ExitStack()
    with ctx:
        def sb(name, cols, dt=F32):
            return ctx.enter_context(nc.sbuf_tensor(name, [P, cols], dt))

        def with_rounded(name, cols):
            at = (nc.sbuf_base + 31) // 32 * 32
            plain = sb(name, cols)
            return plain, nc.alloc_sbuf_tensor_at(name + "_R", [P, cols], F32R, offset=at)

        BIG, BIG_R = with_rounded("BIG", N_BIG)
        PAT, PAT_R = with_rounded("PAT", N_PAT)
        WTOK, WTOK_R = with_rounded("WTOK", N_WTOK)
        WMAM, WMAM_R = with_rounded("WMAM", N_WMAM)
        SCR, SCR_R = with_rounded("SCR", N_SCR)
        SM = sb("SM", NSMALL)
        H = [sb(f"H{i}", CT * N) for i in range(2)]
        Z = sb("Z", CT * N)
        XC = sb("XC", CT * N)
        SQ = sb("SQ", CT * N)
        BANK = [ctx.enter_context(nc.psum_tensor(f"bank{i}", [P, 512], F32)) for i in range(8)]
        S = {name: ctx.enter_context(nc.semaphore(name)) for name in SIGNALS}
        bank_full = [ctx.enter_context(nc.semaphore(f"bank_full_{i}")) for i in range(8)]
        expert_in = [ctx.enter_context(nc.semaphore(f"experts_in_{i}")) for i in range(NE // 4)]

        def sm(name, i=None, rows=P):
            at, w = SMALL[name]
            return SM[0:rows, at:at + w] if i is None else SM[0:rows, at + i:at + i + 1]

        def view(buf, at, *dims, rows=P):
            n = int(np.prod(dims))
            v = buf[0:rows, at:at + n]
            if len(dims) == 2:
                v = v.rearrange("p (a b) -> p a b", b=dims[1])
            elif len(dims) == 3:
                v = v.rearrange("p (a b c) -> p a b c", b=dims[1], c=dims[2])
            elif len(dims) == 4:
                v = v.rearrange("p (a b c d) -> p a b c d", b=dims[1], c=dims[2], d=dims[3])
            return v

        def weight(buf, table, name, base=0, rows=P):
            at, kt, width = table[name]
            return view(buf, base + at, kt, width, rows=rows)

        def exact(ap):
            return ap.bitcast(F32)

        def half(ap, f):
            c = slice(f * NH, (f + 1) * NH)
            return ap[:, c] if len(ap.shape) == 2 else ap[:, :, c]

        def norm_at(i, f):
            return 3 + CT * i + f + 1

        def tokens(ap):
            if len(ap.shape) == 2:
                return ap.rearrange("p (b l) -> p b l", l=L)
            return ap.rearrange("p m (b l) -> p m b l", l=L)

        def over(ap, n):
            return ap.unsqueeze(1).to_broadcast([ap.shape[0], n] + list(ap.shape[1:]))

        def last(ap, n):
            return ap.unsqueeze(len(ap.shape)).to_broadcast(list(ap.shape) + [n])

        h = [view(H[i], 0, CT, N) for i in range(2)]
        z, xc, sq = view(Z, 0, CT, N), view(XC, 0, CT, N), view(SQ, 0, CT, N)
        sqh = [view(SQ, CT * NH * f, CT, NH) for f in HALVES]
        ident = sm("ident")

        pe_all = view(BIG, 0, CT, NP)
        xn_all = view(BIG, CT * NP, CT, NP)
        prod_w = view(BIG, 2 * CT * NP, 2, TAPS, C)
        sq_all = view(BIG, 2 * CT * NP, CT, NP)
        v_w = view(BIG, 3 * CT * NP, 2, TAPS, C)
        cw_hi, cw_lo = (view(SCR_R, 1024 + i * KCT * C, KCT, C) for i in range(2))
        KFULL, KREST = KC // P, KC % P
        W0 = NCH

        def patch_part(buf, j):
            n = min(CHUNK, NP - j * CHUNK)
            v = view(buf, 0, KCT, NP)[:, :, j * CHUNK:j * CHUNK + n]
            return v[:, 0:KFULL], v[0:KREST, KFULL]

        def patch_hi(j):
            n = min(CHUNK, NP - j * CHUNK)
            if j % 2:
                v = view(BIG_R, 3 * CT * NP, KCT, CHUNK)
                return v[:, 0:KFULL, 0:n], v[0:KREST, KFULL, 0:n]
            return (view(BIG_R, 3 * CT * NP + KCT * CHUNK, KFULL, CHUNK)[:, :, 0:n],
                    view(SCR_R, 1024 + 2 * KCT * C, CHUNK)[0:KREST, 0:n])

        red = view(SCR, 0, CT, NW)
        redn = view(SCR, 512, CT, NW)
        q_w = view(SCR, 1024, 2, C)
        sc = view(SCR, 1536, 2, TAPS, H8)
        sc_e = view(SCR, 1680, 2, TAPS, H8)
        sc_m = view(SCR, 1824, 2, H8)
        sc_s = view(SCR, 1840, 2, H8)
        sc_r = view(SCR, 1856, 2, H8)
        agg = view(SCR, 1880, 2, C)
        aggT = view(SCR, 2392, CT, NW)
        lo = view(SCR, 2904, CT, NW)
        lon = view(SCR, 3416, CT, NW)
        gkT = view(SCR, 3928, CT, NW)
        gs = view(SCR, 4440, CT, NW)
        gse = view(SCR, 4952, CT, NW)
        gm = view(SCR, 5464, CT, B)
        gr = view(SCR, 5592, CT, B)
        gaggT = view(SCR, 5720, CT, B)
        clsn = view(SCR, 5848, CT, 1)
        gq = view(SCR, 5850, CT, 1)
        gqm = view(SCR, 5852, CT, P)
        w_log = view(SCR, 6108, CHUNK)
        w_rs = view(SCR, 6620, CHUNK)

        u_raw, u, sres, delta, du, e1, az, rz = (view(PAT, i * SLOT, DIT, N) for i in range(8))
        arg = [view(SCR, i * SLOT, DIT, N) for i in range(2)]
        dbu = [view(SCR, (2 + i) * SLOT, DIT, N) for i in range(2)]
        hs = [view(SCR, (4 + i) * SLOT, DIT, N) for i in range(2)]
        hc = [e1, az]
        w1, lost = delta, du
        xdbl = view(PAT, 8 * SLOT, N, rows=48)
        negA = view(PAT, 8 * SLOT + N, DIT, NS)

        lg, ex = (view(SCR, i * 32, TT, NE, rows=TN) for i in range(2))
        gmax, gsum, grec = (view(SCR, 96 + 4 * i, TT, rows=TN) for i in range(3))
        cmp1, cmp2 = (view(SCR, 128 + i * 256, TT, NE, NE, rows=TN) for i in range(2))
        rank = view(SCR, 640, TT, NE, rows=TN)
        combT = view(SCR, 700, N, rows=NE)
        combb = [view(SCR, 1100 + i * N, N) for i in range(2)]
        sil = [view(SCR, 1800 + i * N, N) for i in range(2)]
        gated = [view(SCR, 2500 + i * N, N) for i in range(2)]
        mixed = [view(SCR, 3200 + i * HIDT * N, HIDT, N) for i in range(2)]
        act_lo = [view(SCR_R, 3200 + i * HIDT * N, HIDT, N) for i in range(2)]
        act_hi = [view(SCR_R, 3200 + (2 + i) * HIDT * N, HIDT, N) for i in range(2)]
        exp_hi = [view(WTOK_R, i * N_EXP, N_EXP) for i in range(2)]
        x_hi, x_lo = (view(WTOK_R, 2 * N_EXP + i * CT * N, CT, N) for i in range(2))
        PART = CT * HID

        q1, t1a, t1b, o1, t1 = ([view(BIG, 640 * i + CT * NH * f, CT, NH) for f in HALVES] for i in range(5))
        k1, v1, kt1, kt2 = ([view(BIG, 3200 + 320 * i + NH * f, NH) for f in HALVES] for i in range(4))
        pr1 = [[view(BIG, 4480 + CT * (PAIRS * f + PAIR_OFF[d]), CT, BH * (L - d)) for d in LAGS] for f in HALVES]
        s1 = [view(BIG, 6400 + 1600 * f, CT * NH, L) for f in HALVES]
        s1e = [view(BIG, 9600 + 1600 * f, CT * NH, L) for f in HALVES]
        s1m, s1s, s1r = ([view(BIG, 12800 + 640 * i + 320 * f, CT * NH) for f in HALVES] for i in range(3))

        x_tok = view(SCR, 0, TT, C, rows=TN)
        xq = view(SCR, 1024, TT, C, rows=TN)
        y_tok = view(SCR, 2048, TT, C, rows=TN)
        amax, asc, ainv, tmean, trs = (view(SCR, 3072 + 8 * i, TT, rows=TN) for i in range(5))
        stats = view(SCR, 3120, TT, 6, rows=TN)
        aggr = view(SCR, 3150, TT, 2, rows=TN)
        xqT = sb("xqT", CT * N, BF16)
        wint = sb("wint", 2 * 64, I32)
        wenc = sb("wenc", 2 * C, I32)
        wT = sb("wT", 2 * C, BF16)
        xT = xqT[:, :].rearrange("p (m n) -> p m n", m=CT)

        q2, k2 = view(BIG, 0, QT2, N), view(BIG, 2560, QT2, N)
        v2 = view(BIG, 5120, TT, 1024, rows=TN)
        s2 = view(BIG, 9216, TT, H16, TN, rows=TN)
        o2 = view(BIG, 14336, QT2, N)
        s2m = view(SCR, 0, TT, H16, rows=TN)

        def slot2(hd):
            return 8 * (hd // 8) + 4 * (hd % 2) + hd % 8 // 2

        s2s = view(SCR, 64, TT, H16, rows=TN)
        s2r = view(SCR, 128, TT, H16, rows=TN)
        pT = [view(SCR, 256 + i * 1280, H16, TN, rows=TN) for i in range(2)]

        cn_a = [view(SCR, 320 * f, CT, NH) for f in HALVES]
        cn_b = [view(SCR, 640 + NH * f, NH) for f in HALVES]
        cn_c = [view(SCR, 960 + NH * f, NH, rows=64) for f in HALVES]
        cn_t = [view(SCR, 1280 + NH * f, NH) for f in HALVES]
        coup = [view(SCR, 1600 + NH * f, NH) for f in HALVES]
        ctmp = [view(SCR, 1920 + 320 * f, CT, NH) for f in HALVES]
        cout = [[view(SCR, 2560 + 640 * i + 320 * f, CT, NH) for f in HALVES] for i in range(2)]
        gmn = [view(SCR, 3840 + 64 * f, CT, BH) for f in HALVES]
        gc_a = [view(SCR, 3968 + BH * f, BH) for f in HALVES]
        gc_b = [view(SCR, 4032 + BH * f, BH, rows=64) for f in HALVES]
        gf = [view(SCR, 4096 + BH * f, BH) for f in HALVES]
        r2 = view(SCR, 4160, 2)

        A3 = 5000
        q3, k3, gaz, gmin, gcum = ([view(SCR, 640 * i + 320 * f, CT, NH) for f in HALVES] for i in range(5))
        sg3 = [view(SCR, 3200 + 640 * f, 4, NH) for f in HALVES]
        v3 = [view(SCR, 4480 + 640 * f, 4, NH) for f in HALVES]
        o3 = [view(SCR, 5760 + 640 * f, 4, NH) for f in HALVES]
        gk1 = [view(SCR, 7040 + NH * f, NH, rows=RANK) for f in HALVES]
        keep = view(PAT, A3, CT * NH)
        t3 = [view(PAT, A3 + 320 + i * 320, 2, NH) for i in range(4)]
        D3, P3 = A3 + 1600, A3 + 1600 + 2 * CT * PAIRS
        gdf_d = [[view(PAT, D3 + CT * (PAIRS * f + PAIR_OFF[d]), CT, BH * (L - d)) for d in LAGS] for f in HALVES]
        pr3_d = [[view(PAT, P3 + CT * (PAIRS * f + PAIR_OFF[d]), CT, BH * (L - d)) for d in LAGS] for f in HALVES]
        osq = [view(PAT, D3 + CT * PAIRS * f, 4, NH) for f in HALVES]
        rs3 = [view(PAT, P3 + CT * PAIRS * f, 4, NH) for f in HALVES]

        fa = view(PAT, 0, HT3, N)
        fb = view(PAT, 2560, HT3, N)
        fa_hi, fb_hi = view(PAT_R, 5120, HT3, N), view(PAT_R, 7680, HT3, N)
        fa_lo, fb_lo = view(PAT_R, 0, HT3, N), view(PAT_R, 2560, HT3, N)
        x3_hi, x3_lo = view(SCR_R, 6400, CT, N), view(SCR_R, 7040, CT, N)
        w1_hi = view(BIG_R, N_FH, CT, DH3)
        w2_hi = [view(WTOK_R, N_F1 + CT * P * m, CT, P) if N_F1 + CT * P * (m + 1) <= N_WTOK else view(WMAM_R, N_F3, CT, P)
                 for m in range(HT3)]
        w3_hi = view(WTOK_R, 0, HT3, C)
        fh_slots = ([view(SCR_R, 2048 + DH3 * i, HT3, P) for i in range(4)] + [view(PAT_R, 10240, HT3, P)]
                    + [view(BIG_R, N_FH + DH3 * i, HT3, P) for i in range(2)]
                    + [view(WTOK_R, 2048 + DH3 * i, HT3, P) for i in range(3)])
        EARLY = 5

        def fh_hi(c):
            return fh_slots[c % len(fh_slots)]

        def fh_tile(c, buf=BIG):
            return weight(buf, W_FH, "h1" if c < HT3 else "h2")[:, :, c % HT3 * P:(c % HT3 + 1) * P]

        fsil = [view(SCR, i * N, N) for i in range(2)]
        otok = view(SCR, 1024, TT, C, rows=TN)

        place = {}
        uses = [0] * 8
        reader = [(S["small_in"], 16)] * 8
        before = {}
        expected = {}

        block = ctx.enter_context(nc.Block())

        @block.tensor
        def _(pe):
            ring = {"banks": list(range(8)), "at": 0}

            def rotate(banks):
                ring["banks"], ring["at"] = list(banks), 0

            def take(key, signal, bank=None, count=None):
                if bank is None:
                    bank = ring["banks"][ring["at"] % len(ring["banks"])]
                    ring["at"] += 1
                if count is None:
                    expected[signal] = expected.get(signal, 0) + 1
                    count = expected[signal]
                before[key] = reader[bank]
                reader[bank] = (S[signal], count)
                uses[bank] += 1
                place[key] = (bank, uses[bank])
                return BANK[bank]

            def emptied(key):
                return before[key]

            def fills(key):
                return bank_full[place[key][0]], 1

            def product(out, w, m0, m1, x, tiles, xs=None):
                for k in range(tiles):
                    ins = pe.matmul(out, w[:, k, m0:m1], x[:, k] if xs is None else xs(k),
                                    start=(k == 0), stop=(k == tiles - 1))
                return ins

            ln_at = [0]

            def norm_mean(key, x, n, ready, count=1):
                pe.wait_ge(S[ready], count)
                o = take((key, "mean"), "ln_xc")
                pe.wait_ge(*emptied((key, "mean")))
                for k in range(CT):
                    ins = pe.matmul(o[:, 0:n], sm("inv256").to_broadcast([P, P]), x[:, k], start=(k == 0), stop=(k == CT - 1))
                ins.then_inc(*fills((key, "mean")))

            def norm_var(key, sq_x, n):
                i = ln_at[0] = ln_at[0] + 1
                pe.wait_ge(S["ln_sq"], i)
                o = take((key, "var"), "ln_logvar")
                pe.wait_ge(*emptied((key, "var")))
                for k in range(CT):
                    ins = pe.matmul(o[:, 0:n], sm("inv256").to_broadcast([P, P]), sq_x[:, k], start=(k == 0), stop=(k == CT - 1))
                ins.then_inc(*fills((key, "var")))

            def product3(out, w_hi, w_lo, m0, m1, hi, lo, first=True, last=True):
                for k, (x, y) in enumerate(zip(hi, lo)):
                    wh, wl = w_hi[:, k, m0:m1], w_lo[:, k, m0:m1]
                    pe.matmul(out, wl, x, start=(first and k == 0), stop=False)
                    pe.matmul(out, wh, y, start=False, stop=False)
                    ins = pe.matmul(out, wh, x, start=False, stop=(last and k == len(hi) - 1))
                return ins

            def mean_of(i, f, ready, count):
                pe.wait_ge(S[ready], count)
                o = take(("mean", i, f), "ln_xc")
                pe.wait_ge(*emptied(("mean", i, f)))
                product(o[:, 0:NH], inv, 0, P, half(z, f), CT).then_inc(*fills(("mean", i, f)))

            def var_of(i, f):
                pe.wait_ge(S["ln_sq"], norm_at(i, f))
                o = take(("var", i, f), "ln_logvar")
                pe.wait_ge(*emptied(("var", i, f)))
                product(o[:, 0:NH], inv, 0, P, sqh[f], CT).then_inc(*fills(("var", i, f)))

            def norm_half(i, ready, count=lambda f: f + 1):
                for f in HALVES:
                    mean_of(i, f, ready, count(f))
                for f in HALVES:
                    var_of(i, f)

            def pair(o, w, x, tiles, at=0):
                for m in range(CT):
                    ins = product(o[:, m * NH:(m + 1) * NH], w, at + m * P, at + (m + 1) * P, x, tiles)
                return ins

            inv = sm("inv256").unsqueeze(2).to_broadcast([P, CT, P])

            def tokenizer():
                w = {n: weight(WTOK, W_TOK, n) for n in W_TOK}
                pe.wait_ge(S["small_in"], 16)
                norm_mean("cls", z[:, :, 0:1], 1, "cls_in")
                norm_var("cls", sq[:, :, 0:1], 1)
                pe.wait_ge(S["conv_w_in"], 16)

                def conv(j):
                    n = min(CHUNK, NP - j * CHUNK)
                    if j == 0:
                        pe.wait_ge(S["patches_in_0"], 16 * KCT)
                    else:
                        pe.wait_ge(S["w_lo"], j + 1)
                        hi, lo = patch_hi(j), patch_part(PAT_R, j)
                    for m in range(CT):
                        o = take(("conv", j, m), f"pe{m}_copied")
                        pe.wait_ge(*emptied(("conv", j, m)))
                        for k in range(KCT):
                            r = min(P, KC - k * P)
                            if j:
                                c = slice(m * P, (m + 1) * P)
                                x, y = (v[0][:, k] if k < KFULL else v[1] for v in (hi, lo))
                                pe.matmul(o[:, 0:n], cw_lo[0:r, k, c], x, start=(k == 0), stop=False)
                                pe.matmul(o[:, 0:n], cw_hi[0:r, k, c], y, start=False, stop=False)
                                ins = pe.matmul(o[:, 0:n], cw_hi[0:r, k, c], x, start=False, stop=(k == KCT - 1))
                                continue
                            ins = pe.matmul(o[:, 0:n], w["conv"][0:r, k, m * P:(m + 1) * P],
                                            PAT[0:r, k * NP + j * CHUNK:k * NP + j * CHUNK + n],
                                            start=(k == 0), stop=(k == KCT - 1))
                        ins.then_inc(*fills(("conv", j, m)))

                def stat(kind, j, src, signal):
                    n = min(CHUNK, NP - j * CHUNK)
                    o = take((kind, j), signal)
                    pe.wait_ge(*emptied((kind, j)))
                    for k in range(CT):
                        ins = pe.matmul(o[:, 0:n], sm("inv256").to_broadcast([P, P]), src[:, k, j * CHUNK:j * CHUNK + n],
                                        start=(k == 0), stop=(k == CT - 1))
                    ins.then_inc(*fills((kind, j)))

                AHEAD = 4

                def window(k, t):
                    pe.wait_ge(S["w_xn"], k * NW // CHUNK + 1)
                    o = take(("kv", k, t), "v_copied")
                    pe.wait_ge(*emptied(("kv", k, t)))
                    at = k * NW + t * P
                    ins = product(o[:, :], xn_all[:, :, at:at + P], 0, P, w["la_wkv"], CT)
                    ins.then_inc(*fills(("kv", k, t)))

                for j in range(NCH + 2):
                    if j < NCH:
                        conv(j)
                    if 1 <= j <= NCH:
                        pe.wait_ge(S["pe0_copied"], j)
                        pe.wait_ge(S["pe1_copied"], j)
                        stat("wmean", j - 1, pe_all, "w_xc")
                    if j == NCH:
                        pe.wait_ge(S["tok_w_in"], 16)
                        pe.wait_ge(S["ln_out"], 1)
                        o = take("gq", "gq_read")
                        pe.wait_ge(*emptied("gq"))
                        for m in range(CT):
                            ins = product(o[:, m:m + 1], w["ga_wq"], m * P, (m + 1) * P, clsn, CT)
                        ins.then_inc(*fills("gq"))
                    if j == NCH + 1:
                        window(0, 0)
                        norm_mean("red", red, NW, "red")
                    if j >= 2:
                        pe.wait_ge(S["w_sq"], j - 1)
                        stat("wvar", j - 2, sq_all, "w_logvar")
                window(1, 0)
                window(2, 0)
                norm_var("red", sq[:, :, 0:NW], NW)
                window(3, 0)
                pe.wait_ge(S["ln_out"], 2)
                o = take("q", "q_copied")
                pe.wait_ge(*emptied("q"))
                for t in range(2):
                    ins = product(o[:, t * C:(t + 1) * C], redn[:, :, t * P:(t + 1) * P], 0, P, w["la_wq"], CT)
                ins.then_inc(*fills("q"))
                for k in range(AHEAD, TAPS):
                    window(k, 0)
                for k in range(TAPS):
                    window(k, 1)
                o = take("aggT", "aggT_copied")
                pe.wait_ge(*emptied("aggT"))
                for t in range(2):
                    pe.wait_ge(S["agg"], t + 1)
                    for m in range(CT):
                        ins = pe.transpose(o[:, m * NW + t * P:m * NW + (t + 1) * P], agg[:, t, m * P:(m + 1) * P], ident)
                ins.then_inc(*fills("aggT"))
                pe.wait_ge(S["aggT_copied"], 1)
                o = take("proj", "lo")
                pe.wait_ge(*emptied("proj"))
                for m in range(CT):
                    ins = product(o[:, m * NW:(m + 1) * NW], w["la_proj"], m * P, (m + 1) * P, aggT, CT)
                ins.then_inc(*fills("proj"))
                norm_mean("lo", lo, NW, "lo")
                o = take("mod", "patch_out")
                pe.wait_ge(*emptied("mod"))
                for m in range(CT):
                    ins = product(o[:, m * NW:(m + 1) * NW], w["mod"], m * P, (m + 1) * P, lo, CT)
                ins.then_inc(*fills("mod"))
                norm_var("lo", sq[:, :, 0:NW], NW)
                pe.wait_ge(S["ln_out"], 3)
                o = take("gk", "gk_copied")
                pe.wait_ge(*emptied("gk"))
                for m in range(CT):
                    ins = product(o[:, m * NW:(m + 1) * NW], w["ga_wkv"], m * P, (m + 1) * P, lon, CT)
                ins.then_inc(*fills("gk"))
                gv = take("gv", "gv_used")
                pe.wait_ge(*emptied("gv"))
                product(gv[:, 0:NW], w["ga_wkv"], C, C + P, lon, CT)
                pe.wait_ge(S["gk_copied"], 1)
                pe.wait_ge(S["gq_read"], 1)
                o = take("gs", "gs_shift")
                pe.wait_ge(*emptied("gs"))
                for m in range(CT):
                    ins = pe.matmul(o[:, m * NW:(m + 1) * NW], gqm[:, m, :], gkT[:, m, :], start=True, stop=True)
                ins.then_inc(*fills("gs"))
                product(gv[:, NW:2 * NW], w["ga_wkv"], C + P, C + 2 * P, lon, CT).then_inc(*fills("gv"))
                pe.wait_ge(S["gagg"], 1)
                o = take("gproj", "cls_out")
                pe.wait_ge(*emptied("gproj"))
                for m in range(CT):
                    ins = product(o[:, m * B:(m + 1) * B], w["ga_proj"], m * P, (m + 1) * P, gaggT, CT)
                ins.then_inc(*fills("gproj"))

            def state_space():
                w = {n: weight(WMAM, W_MAM, n) for n in W_MAM}
                pe.wait_ge(S["mam_w_in"], 16)
                pe.wait_ge(S["cls_out"], 1)
                pe.wait_ge(S["patch_out"], 1)
                for m in range(2 * DIT):
                    o = take(("win", m), "u_conv" if m < DIT else "res_silu")
                    pe.wait_ge(*emptied(("win", m)))
                    product(o[:, 0:N], w["W_in"], m * P, (m + 1) * P, h[0], CT).then_inc(*fills(("win", m)))
                pe.wait_ge(S["u_silu"], 1)
                o = take("xdbl", "xdbl_copied")
                pe.wait_ge(*emptied("xdbl"))
                product(o[0:48, 0:N], w["W_x"], 0, 48, u, DIT).then_inc(*fills("xdbl"))
                pe.wait_ge(S["xdbl_copied"], 1)
                for m in range(DIT):
                    o = take(("wdt", m), "dt_relu")
                    pe.wait_ge(*emptied(("wdt", m)))
                    pe.matmul(o[:, 0:N], w["W_dt"][0:RANK, 0, m * P:(m + 1) * P], xdbl[0:RANK, :],
                                               start=True, stop=True).then_inc(*fills(("wdt", m)))
                y = []
                for m in range(DIT):
                    o = take(("y", m), "y_skip", bank=4 + m)
                    pe.wait_ge(*emptied(("y", m)))
                    y.append(o)
                rotate(range(4))

                def add(n):
                    pe.wait_ge(S["hc"], n + 1)
                    for m in range(DIT):
                        ins = pe.matmul(y[m][:, 0:N], ident, hc[n % 2][:, m], start=(n == 0), stop=(n == NS - 1))
                        if n == NS - 1:
                            ins.then_inc(*fills(("y", m)))
                    if n < NS - 1:
                        ins.then_inc(S["hc_added"], 1)

                def spread(n):
                    for key, row, sig in (("B", RANK + n, "b_used"), ("C", RANK + NS + n, "hc")):
                        o = take((key, n), sig)
                        pe.wait_ge(*emptied((key, n)))
                        pe.matmul(o[:, 0:N], ident[0:48, row:row + 1].to_broadcast([48, P]), xdbl,
                                                 start=True, stop=True).then_inc(*fills((key, n)))

                spread(0)
                spread(1)
                for n in range(NS):
                    if n + 2 < NS:
                        spread(n + 2)
                    add(n)
                rotate(range(8))
                pe.wait_ge(S["y_out"], DIT)
                for f in HALVES:
                    o = take(("wout", f), "z_mam")
                    pe.wait_ge(*emptied(("wout", f)))
                    pair(o, w["W_out"], half(u_raw, f), DIT).then_inc(*fills(("wout", f)))
                norm_half(0, "z_mam")

            def experts():
                pe.wait_ge(S["ln_out"], norm_at(0, 1))
                o = take("gate", "gate_copied")
                pe.wait_ge(*emptied("gate"))
                wr = view(SM, SMALL["Wr"][0], 2, NE)
                for t in range(TT):
                    ins = product(o[0:TN, t * NE:(t + 1) * NE], h[1][:, :, t * TN:(t + 1) * TN], 0, TN, wr, CT)
                ins.then_inc(*fills("gate"))
                rotate(range(6))

                tiles = range(CT)

                def up(e):
                    for i, (name, sig) in enumerate((("W1", "silu_h"), ("W3", "gated"))):
                        pe.wait_ge(S["w_lo"], W0 + 3 * e + i + 1)
                    for m in range(HIDT):
                        for name, sig in (("W1", "silu_h"), ("W3", "gated")):
                            w_hi = weight(WTOK_R, W_EXP, name, base=(e % 2) * N_EXP)
                            w_lo = weight(BIG_R, W_EXP, name, base=e * N_EXP)
                            o = take((name, e, m), sig)
                            pe.wait_ge(*emptied((name, e, m)))
                            ins = product3(o[:, 0:N], w_hi, w_lo, m * P, (m + 1) * P, [x_hi[:, k] for k in tiles],
                                           [x_lo[:, k] for k in tiles])
                            ins.then_inc(*fills((name, e, m)))
                    pe.nop().then_inc(S["up_used"], 1)

                acc = []
                for m in range(CT):
                    o = take(("moe", m), "z_moe", bank=6 + m, count=2)
                    pe.wait_ge(*emptied(("moe", m)))
                    acc.append(o)

                def combine(e):
                    o = take(("comb", e), "combine_copied")
                    pe.wait_ge(*emptied(("comb", e)))
                    pe.matmul(o[:, 0:N], ident[0:NE, e:e + 1].to_broadcast([NE, P]), combT,
                                                start=True, stop=True).then_inc(*fills(("comb", e)))

                def down(e):
                    w_hi = weight(WTOK_R, W_EXP, "W2", base=(e % 2) * N_EXP)
                    w_lo = weight(BIG_R, W_EXP, "W2", base=e * N_EXP)
                    pe.wait_ge(S["w_lo"], W0 + 3 * e + 3)
                    for k in range(HIDT):
                        pe.wait_ge(S["act_lo"], e * HIDT + k + 1)
                        for m in range(CT):
                            ins = product3(acc[m][:, 0:N], w_hi[:, k:k + 1], w_lo[:, k:k + 1], m * P, (m + 1) * P,
                                           [act_hi[e % 2][:, k]], [act_lo[e % 2][:, k]], first=(e == 0 and k == 0),
                                           last=(e == NE - 1 and k == HIDT - 1))
                            if e == NE - 1 and k == HIDT - 1:
                                ins.then_inc(*fills(("moe", m)))
                    if e < NE - 1:
                        ins.then_inc(S["act_used"], 1)

                pe.wait_ge(S["x_lo"], 1)
                up(0)
                pe.wait_ge(S["comb"], 1)
                o = take("combT", "comb_copied")
                pe.wait_ge(*emptied("combT"))
                for t in range(TT):
                    ins = pe.transpose(o[0:NE, t * TN:(t + 1) * TN], ex[:, t, :], ident[0:TN, 0:TN])
                ins.then_inc(*fills("combT"))
                pe.wait_ge(S["comb_copied"], 1)
                combine(0)
                for e in range(1, NE + 1):
                    if e < NE:
                        combine(e)
                        up(e)
                    down(e - 1)
                rotate(range(8))
                norm_half(1, "z_moe")

            def attention1():
                base = N_L2
                w = {n: weight(PAT, W_L1, n, base=base) for n in W_L1}
                pe.wait_ge(S["l1_w_in"], 16)
                for f in HALVES:
                    pe.wait_ge(S["ln_out"], norm_at(1, f))
                    x = half(h[0], f)
                    o = take(("q1", f), "rope1")
                    pe.wait_ge(*emptied(("q1", f)))
                    pair(o, w["wqp"], x, CT).then_inc(*fills(("q1", f)))
                    o = take(("q1r", f), "rope1")
                    pe.wait_ge(*emptied(("q1r", f)))
                    pair(o, w["wqr"], x, CT).then_inc(*fills(("q1r", f)))
                    o = take(("k1", f), "rope1")
                    pe.wait_ge(*emptied(("k1", f)))
                    product(o[:, 0:NH], w["wkp"], 0, P, x, CT)
                    product(o[:, NH:2 * NH], w["wkr"], 0, P, x, CT).then_inc(*fills(("k1", f)))
                    o = take(("v1", f), "v1_copied")
                    pe.wait_ge(*emptied(("v1", f)))
                    product(o[:, 0:NH], w["wv"], 0, P, x, CT).then_inc(*fills(("v1", f)))
                for f in HALVES:
                    for d in LAGS:
                        pe.wait_ge(S["s1_prod"], L * f + d + 1)
                        o = take(("s1", f, d), "s1_copied")
                        pe.wait_ge(*emptied(("s1", f, d)))
                        for m in range(CT):
                            ins = pe.matmul(o[:, m * NH:m * NH + BH * (L - d)], sm("same16"), pr1[f][d][:, m],
                                            start=True, stop=True)
                        ins.then_inc(*fills(("s1", f, d)))
                for f in HALVES:
                    pe.wait_ge(S["a1_out"], f + 1)
                    o = take(("wo1", f), "z_attn1")
                    pe.wait_ge(*emptied(("wo1", f)))
                    pair(o, w["wo"], o1[f], CT).then_inc(*fills(("wo1", f)))
                norm_half(2, "z_attn1")

            def ternary():
                for f in HALVES:
                    pe.wait_ge(S["ln_out"], norm_at(2, f))
                    o = take(("xtok", f), "x_tok_copied")
                    pe.wait_ge(*emptied(("xtok", f)))
                    for i in range(2):
                        for m in range(CT):
                            c = (2 * f + i) * TN
                            ins = pe.transpose(o[0:TN, i * C + m * P:i * C + (m + 1) * P], h[1][:, m, c:c + TN], ident)
                    ins.then_inc(*fills(("xtok", f)))
                for f in HALVES:
                    pe.wait_ge(S["x_int"], f + 1)
                    o = take(("xint", f), "xint_copied")
                    pe.wait_ge(*emptied(("xint", f)))
                    for m in range(CT):
                        for i in range(2):
                            ins = pe.transpose(o[:, m * NH + i * TN:m * NH + (i + 1) * TN],
                                               xq[:, 2 * f + i, m * P:(m + 1) * P], ident[0:TN, 0:TN])
                    ins.then_inc(*fills(("xint", f)))
                wv = wT[:, :].rearrange("p (c o) -> p c o", c=2)
                for f in HALVES:
                    pe.wait_ge(S["xint_copied"], f + 1)
                    o = take(("l1f", f), "l1f_read")
                    pe.wait_ge(*emptied(("l1f", f)))
                    for i in range(2):
                        ins = product(o[0:TN, i * C:(i + 1) * C], xT[:, :, (2 * f + i) * TN:(2 * f + i + 1) * TN], 0, TN, wv, CT)
                    ins.then_inc(*fills(("l1f", f)))
                for f in HALVES:
                    pe.wait_ge(S["h4_tok"], f + 1)
                    o = take(("h4", f), "h4_copied")
                    pe.wait_ge(*emptied(("h4", f)))
                    for m in range(CT):
                        for i in range(2):
                            ins = pe.transpose(o[:, m * NH + i * TN:m * NH + (i + 1) * TN],
                                               y_tok[:, 2 * f + i, m * P:(m + 1) * P], ident[0:TN, 0:TN])
                    ins.then_inc(*fills(("h4", f)))

            def attention2():
                w = {n: weight(PAT, W_L2, n) for n in W_L2}
                pe.wait_ge(S["l2_w_in"], 16)
                for f in HALVES:
                    pe.wait_ge(S["h4_copied"], f + 1)
                    for j in range(QT2 // 2):
                        for name, key in (("wq", "q2"), ("wk", "k2")):
                            o = take((key, f, j), f"{key}_copied")
                            pe.wait_ge(*emptied((key, f, j)))
                            pair(o, w[name], half(h[0], f), CT, at=2 * j * P).then_inc(*fills((key, f, j)))

                def values(t):
                    for hf in range(2):
                        o = take(("v2", t, hf), "v2_copied")
                        pe.wait_ge(*emptied(("v2", t, hf)))
                        product(o[0:TN, :], h[0][:, :, t * TN:(t + 1) * TN], 0, TN,
                                                    w["wv"][:, :, hf * 512:(hf + 1) * 512], CT).then_inc(*fills(("v2", t, hf)))

                def scores(t):
                    for q in range(2):
                        pe.wait_ge(S["q2_copied"], 4 * (t // 2) + 2 * q + 2)
                        pe.wait_ge(S["k2_copied"], 4 * (t // 2) + 2 * q + 2)
                        banks = []
                        for odd in range(2):
                            o = take(("s2", t, 2 * q + odd), "s2_masked")
                            pe.wait_ge(*emptied(("s2", t, 2 * q + odd)))
                            banks.append(o)
                        for i in range(4):
                            for odd in range(2):
                                r = slice(HD2 * odd, HD2 * odd + HD2)
                                m = 4 * q + i
                                ins = pe.matmul(banks[odd][0:TN, i * TN:(i + 1) * TN], q2[r, m, t * TN:(t + 1) * TN],
                                                k2[r, m, t * TN:(t + 1) * TN], start=True, stop=True)
                                if i == 3:
                                    ins.then_inc(*fills(("s2", t, 2 * q + odd)))

                def mix(t):
                    pe.wait_ge(S["s2_prob"], t + 1)
                    for g in range(4):
                        o = take(("pT", t, g), "pT_copied")
                        pe.wait_ge(*emptied(("pT", t, g)))
                        for i in range(4):
                            ins = pe.transpose(o[0:TN, i * TN:(i + 1) * TN], s2[:, t, 4 * g + i, :], ident[0:TN, 0:TN])
                        ins.then_inc(*fills(("pT", t, g)))
                    pe.wait_ge(S["v2_copied"], 2 * t + 2)
                    for g in range(2):
                        pe.wait_ge(S["pT_copied"], 4 * t + 2 * g + 2)
                        o = take(("o2", t, g), "o2_copied")
                        pe.wait_ge(*emptied(("o2", t, g)))
                        for i in range(8):
                            hd = 8 * g + i
                            r = slice(HD2 * (hd % 2), HD2 * (hd % 2) + HD2)
                            ins = pe.matmul(o[r, (i // 2) * TN:(i // 2 + 1) * TN], v2[:, t, hd * HD2:(hd + 1) * HD2],
                                            pT[t % 2][:, slot2(hd), :], start=True, stop=True)
                        ins.then_inc(*fills(("o2", t, g)))

                def output(f):
                    pe.wait_ge(S["o2_copied"], 4 * f + 4)
                    o = take(("r2", f), "z_attn2")
                    pe.wait_ge(*emptied(("r2", f)))
                    pair(o, w["wr"], half(o2, f), QT2).then_inc(*fills(("r2", f)))

                scores(0)
                scores(1)
                for t in range(TT):
                    values(t)
                    if t + 2 < TT:
                        scores(t + 2)
                    mix(t)
                    if t == 2:
                        output(0)
                        mean_of(3, 0, "z_attn2", 1)
                var_of(3, 0)
                output(1)
                mean_of(3, 1, "z_attn2", 2)
                var_of(3, 1)

            def coupling():
                w = {n: weight(WMAM, W_F3, n) for n in W_F3}
                pe.wait_ge(S["f3_w_in"], 16)

                def first(cyc, f):
                    if cyc:
                        pe.wait_ge(S["c_out"], CT * (cyc - 1) + f + 1)
                    o = take(("c1", cyc, f), "c1_act")
                    pe.wait_ge(*emptied(("c1", cyc, f)))
                    pair(o, w["cn1"], half(h[1], f) if cyc == 0 else cout[(cyc - 1) % 2][f], CT).then_inc(*fills(("c1", cyc, f)))

                for f in HALVES:
                    pe.wait_ge(S["gmean"], f + 1)
                    o = take(("gc1", f), "gc_act")
                    pe.wait_ge(*emptied(("gc1", f)))
                    product(o[:, 0:BH], w["gc1"], 0, P, gmn[f], CT).then_inc(*fills(("gc1", f)))
                    first(0, f)
                for f in HALVES:
                    pe.wait_ge(S["gc_act"], f + 1)
                    o = take(("gc2", f), "gc_act")
                    pe.wait_ge(*emptied(("gc2", f)))
                    pe.matmul(o[0:64, 0:BH], w["gc2"][:, 0, :], gc_a[f], start=True, stop=True).then_inc(*fills(("gc2", f)))
                for f in HALVES:
                    pe.wait_ge(S["gc_act"], 2 + f + 1)
                    o = take(("gc3", f), "gc_act")
                    pe.wait_ge(*emptied(("gc3", f)))
                    pe.matmul(o[:, 0:BH], w["gc3"][0:64, 0, :].to_broadcast([64, P]), gc_b[f],
                                               start=True, stop=True).then_inc(*fills(("gc3", f)))
                for cyc in range(3):
                    n = CT * cyc + 1
                    if cyc:
                        for f in HALVES:
                            first(cyc, f)
                    for f in HALVES:
                        pe.wait_ge(S["c1_act"], n + f)
                        o = take(("c2", cyc, f), "c2_act")
                        pe.wait_ge(*emptied(("c2", cyc, f)))
                        product(o[:, 0:NH], w["cn2"], 0, P, cn_a[f], CT).then_inc(*fills(("c2", cyc, f)))
                    for f in HALVES:
                        pe.wait_ge(S["c2_act"], n + f)
                        o = take(("c3", cyc, f), "c3_act")
                        pe.wait_ge(*emptied(("c3", cyc, f)))
                        pe.matmul(o[0:64, 0:NH], w["cn3"][:, 0, :], cn_b[f], start=True, stop=True).then_inc(*fills(("c3", cyc, f)))
                    for f in HALVES:
                        pe.wait_ge(S["c3_act"], n + f)
                        o = take(("c4", cyc, f), "c4_act")
                        pe.wait_ge(*emptied(("c4", cyc, f)))
                        pe.matmul(o[:, 0:NH], w["cn4"][0:64, 0, :].to_broadcast([64, P]), cn_c[f],
                                                       start=True, stop=True).then_inc(*fills(("c4", cyc, f)))
                norm_half(4, "z_ffn2")

            def attention3():
                w = {n: weight(PAT, W_L3, n) for n in W_L3}
                pe.wait_ge(S["l3_w_in"], 16)
                for f in HALVES:
                    pe.wait_ge(S["ln_out"], norm_at(4, f))
                    x = half(h[0], f)
                    o = take(("gk1", f), "gk1_copied")
                    pe.wait_ge(*emptied(("gk1", f)))
                    product(o[0:RANK, 0:NH], w["gk1"], 0, RANK, x, CT).then_inc(*fills(("gk1", f)))
                    for key, name in (("q3", "wq"), ("k3", "wk")):
                        o = take((key, f), "qkv3_copied")
                        pe.wait_ge(*emptied((key, f)))
                        pair(o, w[name], x, CT).then_inc(*fills((key, f)))
                for f in HALVES:
                    pe.wait_ge(S["gk1_copied"], f + 1)
                    o = take(("gk2", f), "gk_min")
                    pe.wait_ge(*emptied(("gk2", f)))
                    for m in range(CT):
                        ins = pe.matmul(o[:, m * NH:(m + 1) * NH], w["gk2"][0:RANK, 0, m * P:(m + 1) * P], gk1[f],
                                        start=True, stop=True)
                    ins.then_inc(*fills(("gk2", f)))
                for key, name, sig in (("v3", "wv", "qkv3_copied"), ("g3", "wg", "g3_silu")):
                    for f in HALVES:
                        for j in range(2):
                            o = take((key, f, j), sig)
                            pe.wait_ge(*emptied((key, f, j)))
                            pair(o, w[name], half(h[0], f), CT, at=2 * j * P).then_inc(*fills((key, f, j)))
                for f in HALVES:
                    for d in LAGS:
                        pe.wait_ge(S["s3_prod"], L * f + d + 1)
                        for odd in range(2):
                            o = take(("s3", f, d, odd), "s3_mul")
                            pe.wait_ge(*emptied(("s3", f, d, odd)))
                            r = slice(64 * odd, 64 * odd + 64)
                            for m in range(CT):
                                ins = pe.matmul(o[:, m * NH:m * NH + BH * (L - d)], sm("one")[r, :].to_broadcast([64, P]),
                                                pr3_d[f][d][r, m], start=True, stop=True)
                            ins.then_inc(*fills(("s3", f, d, odd)))
                for f in HALVES:
                    pe.wait_ge(S["o3_sq"], f + 1)
                    for j in range(2):
                        o = take(("ms3", f, j), "o3_logvar")
                        pe.wait_ge(*emptied(("ms3", f, j)))
                        for i in range(2):
                            ins = pe.matmul(o[:, i * NH:(i + 1) * NH], sm("inv128").to_broadcast([P, P]),
                                            osq[f][:, 2 * j + i], start=True, stop=True)
                        ins.then_inc(*fills(("ms3", f, j)))
                for f in HALVES:
                    pe.wait_ge(S["o3_out"], f + 1)
                    o = take(("wo3", f), "z_attn3")
                    pe.wait_ge(*emptied(("wo3", f)))
                    pair(o, w["wo"], o3[f], 4).then_inc(*fills(("wo3", f)))
                norm_half(5, "z_attn3")

            def last_ffn():
                w12 = {n: weight(WTOK_R, W_F1, n) for n in W_F1}
                w3_lo = weight(WMAM_R, W_F3, "w3")
                pe.wait_ge(S["w_lo"], W0 + 3 * NE + 2)
                pe.wait_ge(S["x_lo"], 3)
                x = [[v[:, k] for k in range(CT)] for v in (x3_hi, x3_lo)]
                for m in range(HT3):
                    o = take(("w1", m), "f1_silu")
                    pe.wait_ge(*emptied(("w1", m)))
                    ins = product3(o[:, 0:N], w1_hi, w12["w1"], m * P, (m + 1) * P, *x)
                    ins.then_inc(*fills(("w1", m)))
                    o = take(("w2", m), "f_gate")
                    pe.wait_ge(*emptied(("w2", m)))
                    ins = product3(o[:, 0:N], w2_hi[m], w12["w2"][:, :, m * P:(m + 1) * P], 0, P, *x)
                    ins.then_inc(*fills(("w2", m)))
                acts = HIDT * NE
                for name, x, n0, sig in (("h1", (fa_hi, fa_lo), acts, "fh1_act"),
                                         ("h2", (fb_hi, fb_lo), acts + HT3, "fh2_act")):
                    for m in range(HT3):
                        c = m + (HT3 if name == "h2" else 0)
                        pe.wait_ge(S["w_lo"], W0 + 3 * NE + 2 + c + 1)
                        o = take((name, m), sig)
                        pe.wait_ge(*emptied((name, m)))
                        for k in range(HT3):
                            if m == 0:
                                pe.wait_ge(S["act_lo"], n0 + k + 1)
                            ins = product3(o[:, 0:N], fh_hi(c)[:, k:k + 1], fh_tile(c, BIG_R)[:, k:k + 1], 0, P,
                                           [x[0][:, k]], [x[1][:, k]], first=(k == 0), last=(k == HT3 - 1))
                        ins.then_inc(*fills((name, m)))
                pe.wait_ge(S["w_lo"], W0 + 3 * NE + 2 + 2 * HT3 + 1)
                sums = []
                for m in range(CT):
                    o = take(("f3", m), "z_ffn3", count=2)
                    pe.wait_ge(*emptied(("f3", m)))
                    sums.append(o)
                for k in range(HT3):
                    pe.wait_ge(S["act_lo"], acts + 2 * HT3 + k + 1)
                    for m in range(CT):
                        ins = product3(sums[m][:, 0:N], w3_hi[:, k:k + 1], w3_lo[:, k:k + 1], m * P, (m + 1) * P,
                                       [fa_hi[:, k]], [fa_lo[:, k]], first=(k == 0), last=(k == HT3 - 1))
                        if k == HT3 - 1:
                            ins.then_inc(*fills(("f3", m)))
                norm_half(6, "z_ffn3")
                for f in HALVES:
                    pe.wait_ge(S["ln_out"], norm_at(6, f))
                    o = take(("out", f), "tok_out")
                    pe.wait_ge(*emptied(("out", f)))
                    for i in range(2):
                        for m in range(CT):
                            c = (2 * f + i) * TN
                            ins = pe.transpose(o[0:TN, i * C + m * P:i * C + (m + 1) * P], h[0][:, m, c:c + TN], ident)
                    ins.then_inc(*fills(("out", f)))

            for f in [tokenizer, state_space, experts, attention1, ternary, attention2, coupling, attention3, last_ffn]:
                f()

        def two(bank, rows=P):
            return bank[0:rows, 0:2 * NH].rearrange("p (m n) -> p m n", m=2)

        def filled(key):
            return bank_full[place[key][0]], place[key][1]

        def result(key):
            return BANK[place[key][0]]

        @block.vector
        def _(dve):
            did = Counts(S, "dve_step")
            tt, ts, copy = dve.tensor_tensor, dve.tensor_scalar, dve.tensor_copy

            def stt(out, a, s, b, op0, op1):
                return dve.scalar_tensor_tensor(out=out, in0=a, scalar=s, in1=b, op0=op0, op1=op1)

            def reduce(out, a, op):
                return dve.tensor_reduce(out, a, AX.X, op)

            ln_at = [0]

            def norm(key, x, n, out, gain=None, shift=None):
                i = ln_at[0] = ln_at[0] + 1
                c = xc[:, :, 0:n]
                dve.wait_ge(*filled((key, "mean")))
                mean = result((key, "mean"))[:, 0:n]
                tt(c, x, over(mean, CT), ALU.subtract).then_inc(*did("ln_xc"))
                dve.wait_ge(S["ln_rstd"], i)
                rstd = SQ[:, N:N + n]
                if gain is None:
                    tt(out, c, over(rstd, CT), ALU.mult).then_inc(*did("ln_out"))
                    return
                for m in range(CT):
                    stt(out[:, m], c[:, m], sm(gain, m), rstd, ALU.mult, ALU.mult).then_inc(*did())
                dve.wait_ge(*did.latest())
                for m in range(CT):
                    ts(out[:, m], out[:, m], sm(shift, m), None, ALU.add)\
                        .then_inc(*did("ln_out" if m == CT - 1 else None))

            def residual(key, h_in, f, signal):
                dve.wait_ge(*filled((key, f)))
                o = result((key, f))
                tt(half(z, f), two(o), half(h_in, f), ALU.add).then_inc(*did(signal))

            def centre(i, f):
                dve.wait_ge(*filled(("mean", i, f)))
                o = result(("mean", i, f))
                tt(half(xc, f), half(z, f), over(o[:, 0:NH], CT), ALU.subtract).then_inc(*did("ln_xc"))

            def scale(i, f, out):
                dve.wait_ge(S["ln_rstd"], norm_at(i, f))
                tt(half(out, f), half(xc, f), over(sqh[f][:, 1], CT), ALU.mult).then_inc(*did("ln_out"))

            def norm_half(i, out):
                for f in HALVES:
                    centre(i, f)
                for f in HALVES:
                    scale(i, f, out)

            def tokenizer():
                dve.wait_ge(S["small_in"], 16)
                copy(z[:, :, 0:1], view(SM, SMALL["class_emb"][0], CT, 1)).then_inc(*did("cls_in"))
                norm("cls", z[:, :, 0:1], 1, clsn, "ga_ln_q_g", "ga_ln_q_b")
                dve.wait_ge(S["w_hi"], 1)
                tt(cw_lo, view(WTOK, 0, KCT, C), exact(cw_hi), ALU.subtract).then_inc(*did("w_lo"))
                dve.wait_ge(S["w_hi"], 2)
                x, hi, low = patch_part(PAT, 1), patch_hi(1), patch_part(PAT_R, 1)
                tt(low[0], x[0], exact(hi[0]), ALU.subtract).then_inc(*did())
                tt(low[1], x[1], exact(hi[1]), ALU.subtract).then_inc(*did("w_lo"))
                for j in range(NCH + 2):
                    if j < NCH:
                        n = min(CHUNK, NP - j * CHUNK)
                        dve.wait_ge(*filled(("conv", j, 0)))
                        o = result(("conv", j, 0))
                        copy(pe_all[:, 0, j * CHUNK:j * CHUNK + n], o[:, 0:n]).then_inc(*did("pe0_copied"))
                    if 1 <= j <= NCH:
                        i = j - 1
                        n = min(CHUNK, NP - i * CHUNK)
                        c = slice(i * CHUNK, i * CHUNK + n)
                        dve.wait_ge(*filled(("wmean", i)))
                        o = result(("wmean", i))
                        tt(xn_all[:, :, c], pe_all[:, :, c], over(o[:, 0:n], CT), ALU.subtract).then_inc(*did("w_xc"))
                    if 1 <= j <= NCH:
                        dve.wait_ge(S["pe0_copied"], j)
                        dve.wait_ge(S["pe1_copied"], j)
                        for k in range((j - 1) * CHUNK // NW, min(j * CHUNK, NP) // NW):
                            tap = pe_all[:, :, k * NW:(k + 1) * NW]
                            if k == 0:
                                copy(red, tap).then_inc(*did())
                            else:
                                dve.wait_ge(*did.latest())
                                tt(red, red, tap, ALU.add).then_inc(*did())
                    if j == NCH:
                        dve.wait_ge(*filled("gq"))
                        o = result("gq")
                        for m in range(CT):
                            ts(gqm[:, m, :], sm("same32"), o[:, m:m + 1], float(C) ** -0.5, ALU.mult, ALU.mult)\
                                .then_inc(*did("gq_read" if m == CT - 1 else None))
                        dve.wait_ge(*did.latest())
                        ts(red, red, 1.0 / TAPS, None, ALU.mult).then_inc(*did("red"))
                    if j >= 2:
                        i = j - 2
                        n = min(CHUNK, NP - i * CHUNK)
                        c = slice(i * CHUNK, i * CHUNK + n)
                        dve.wait_ge(S["w_rstd"], i + 1)
                        dve.wait_ge(S["w_sq"], i + 1)
                        for m in range(CT):
                            stt(xn_all[:, m, c], xn_all[:, m, c], sm("la_ln_kv_g", m), w_rs[:, 0:n], ALU.mult,
                                ALU.mult).then_inc(*did())
                        dve.wait_ge(*did.latest())
                        for m in range(CT):
                            ts(xn_all[:, m, c], xn_all[:, m, c], sm("la_ln_kv_b", m), None, ALU.add)\
                                .then_inc(*did("w_xn" if m == CT - 1 else None))
                norm("red", red, NW, redn, "la_ln_q_g", "la_ln_q_b")
                dve.wait_ge(S["q_copied"], 1)

                def products(t):
                    for k in range(TAPS):
                        dve.wait_ge(*filled(("kv", k, t)))
                        o = result(("kv", k, t))
                        tt(prod_w[:, t, k], o[:, 0:C], q_w[:, t], ALU.mult).then_inc(*did("kq_done"))
                        dve.wait_ge(S["kq_done"], TAPS * t + k + 1)
                        reduce(sc[:, t, k], prod_w[:, t, k].rearrange("p (h d) -> p h d", d=DH), ALU.add)\
                            .then_inc(*did())

                def shifted(t):
                    dve.wait_ge(*did.latest())
                    reduce(sc_m[:, t], sc[:, t].rearrange("p k h -> p h k"), ALU.max).then_inc(*did())
                    dve.wait_ge(*did.latest())
                    tt(sc_e[:, t], sc[:, t], over(sc_m[:, t], TAPS), ALU.subtract).then_inc(*did("la_shift"))

                def weighted(t):
                    dve.wait_ge(S["la_exp"], t + 1)
                    reduce(sc_s[:, t], sc_e[:, t].rearrange("p k h -> p h k"), ALU.add).then_inc(*did())
                    dve.wait_ge(*did.latest())
                    dve.reciprocal(sc_r[:, t], sc_s[:, t]).then_inc(*did())
                    dve.wait_ge(*did.latest())
                    tt(sc[:, t], sc_e[:, t], over(sc_r[:, t], TAPS), ALU.mult).then_inc(*did())
                    dve.wait_ge(*did.latest())
                    dve.wait_ge(S["v_copied"], TAPS * (t + 1))
                    tt(prod_w[:, t].rearrange("p k (h d) -> p (k h) d", d=DH),
                       v_w[:, t].rearrange("p k (h d) -> p (k h) d", d=DH),
                       last(sc[:, t].rearrange("p k h -> p (k h)"), DH), ALU.mult)\
                        .then_inc(*did())
                    dve.wait_ge(*did.latest())
                    reduce(agg[:, t], prod_w[:, t].rearrange("p k c -> p c k"), ALU.add).then_inc(*did("agg"))

                products(0)
                shifted(0)
                weighted(0)
                products(1)
                shifted(1)
                weighted(1)
                dve.wait_ge(*filled("aggT"))
                o = result("aggT")
                copy(aggT.rearrange("p m w -> p (m w)"), o[:, :]).then_inc(*did("aggT_copied"))
                dve.wait_ge(*filled("proj"))
                o = result("proj")
                for m in range(CT):
                    stt(lo[:, m], o[:, m * NW:(m + 1) * NW], sm("la_proj_b", m), red[:, m], ALU.add, ALU.add)\
                        .then_inc(*did("lo" if m == CT - 1 else None))
                norm("lo", lo, NW, lon, "ga_ln_kv_g", "ga_ln_kv_b")
                dve.wait_ge(*filled("mod"))
                o = result("mod")
                for m in range(CT):
                    ts(tokens(h[0])[:, m, :, 0:WIN],
                       o[:, m * NW:(m + 1) * NW].rearrange("p (b n) -> p b n", n=WIN), sm("mod_b", m), None,
                       ALU.add).then_inc(*did("patch_out" if m == CT - 1 else None))
                dve.wait_ge(*filled("gs"))
                o = result("gs")
                four = o[:, :].rearrange("p (x n) -> p x n", n=WIN)
                gm_ = gm.rearrange("p m b -> p (m b)")
                gr_ = gr.rearrange("p m b -> p (m b)")
                gs_ = gs.rearrange("p m (b n) -> p (m b) n", n=WIN)
                gse_ = gse.rearrange("p m (b n) -> p (m b) n", n=WIN)
                reduce(gm_, four, ALU.max).then_inc(*did())
                dve.wait_ge(*did.latest())
                tt(gs_, four, last(gm_, WIN), ALU.subtract).then_inc(*did("gs_shift"))
                dve.wait_ge(S["gs_exp"], 1)
                reduce(gr_, gse_, ALU.add).then_inc(*did())
                dve.wait_ge(*did.latest())
                dve.reciprocal(gr_, gr_).then_inc(*did())
                dve.wait_ge(*did.latest())
                tt(gse_, gse_, last(gr_, WIN), ALU.mult).then_inc(*did())
                dve.wait_ge(*did.latest())
                dve.wait_ge(*filled("gv"))
                o = result("gv")
                tt(gs_, gse_, o[:, :].rearrange("p (x n) -> p x n", n=WIN), ALU.mult).then_inc(*did("gv_used"))
                dve.wait_ge(*did.latest())
                reduce(gaggT.rearrange("p m b -> p (m b)"), gs_, ALU.add).then_inc(*did("gagg"))
                dve.wait_ge(*filled("gproj"))
                o = result("gproj")
                for m in range(CT):
                    ts(tokens(h[0])[:, m, :, WIN], o[:, m * B:(m + 1) * B], sm("ga_proj_b", m), sm("class_emb", m),
                       ALU.add, ALU.add).then_inc(*did("cls_out" if m == CT - 1 else None))

            def state_space():
                flat = "p m n -> p (m n)"
                ts(negA, view(SM, SMALL["A_log"][0], DIT, NS), A_LOG_TOP, None, ALU.min).then_inc(*did("a_clip"))
                dve.wait_ge(S["a_exp"], 1)
                ts(negA, negA, -1.0, None, ALU.mult).then_inc(*did())
                for m in range(DIT):
                    dve.wait_ge(*filled(("win", m)))
                    o = result(("win", m))
                    src, dst = tokens(o[:, 0:N]), tokens(u_raw[:, m])
                    ts(u_raw[:, m], o[:, 0:N], sm("W_conv", 3 * m + 2), None, ALU.mult).then_inc(*did())
                    dve.wait_ge(*did.latest())
                    stt(dst[:, :, 1:], src[:, :, :L - 1], sm("W_conv", 3 * m + 1), dst[:, :, 1:], ALU.mult, ALU.add)\
                        .then_inc(*did())
                    dve.wait_ge(*did.latest())
                    stt(dst[:, :, 2:], src[:, :, :L - 2], sm("W_conv", 3 * m), dst[:, :, 2:], ALU.mult, ALU.add)\
                        .then_inc(*did("u_conv"))
                dve.wait_ge(*filled("xdbl"))
                o = result("xdbl")
                copy(xdbl, o[0:48, 0:N]).then_inc(*did("xdbl_copied"))
                for m in range(DIT):
                    dve.wait_ge(S["dt_abs"], m + 1)
                    dve.wait_ge(*filled(("wdt", m)))
                    o = result(("wdt", m))
                    ts(rz[:, m], o[:, 0:N], sm("b_dt", m), 0.0, ALU.add, ALU.max).then_inc(*did("dt_relu"))
                dve.wait_ge(S["dt_exp"], 1)
                ts(w1, e1, 1.0, None, ALU.add).then_inc(*did("dt_exp1"))
                dve.wait_ge(*did.latest())
                stt(lost.rearrange(flat), w1.rearrange(flat), -1.0, e1.rearrange(flat), ALU.add, ALU.subtract)\
                    .then_inc(*did())
                dve.wait_ge(*did.latest())
                tt(rz, rz, lost, ALU.subtract).then_inc(*did())
                dve.wait_ge(*did.latest())
                dve.wait_ge(S["dt_log"], 1)
                tt(delta, az, rz, ALU.add).then_inc(*did())
                dve.wait_ge(*did.latest())
                dve.wait_ge(S["u_silu"], 1)
                tt(du, delta, u, ALU.mult).then_inc(*did())
                dve.wait_ge(*did.latest())

                def dbu_of(n):
                    dve.wait_ge(*filled(("B", n)))
                    o = result(("B", n))
                    tt(dbu[n % 2], du, over(o[:, 0:N], DIT), ALU.mult).then_inc(*did("b_used"))

                def arg_of(n):
                    if n >= 2:
                        dve.wait_ge(S["scanned"], n - 1)
                    for m in range(DIT):
                        ts(tokens(arg[n % 2][:, m])[:, :, 1:], tokens(delta[:, m])[:, :, 1:], negA[:, m, n:n + 1],
                           EXP_FLOOR, ALU.mult, ALU.max)\
                            .then_inc(*did("arg" if m == DIT - 1 else None))

                dve.wait_ge(S["arg_zero"], 2)
                arg_of(0)
                dbu_of(0)
                arg_of(1)
                for n in range(NS):
                    dve.wait_ge(S["b_used"], n + 1)
                    dve.wait_ge(S["decay"], n + 1)
                    dve.tensor_tensor_scan(hs[n % 2].rearrange(flat), arg[n % 2].rearrange(flat),
                                               dbu[n % 2].rearrange(flat), 0.0, ALU.mult, ALU.add).then_inc(*did("scanned"))
                    if n + 1 < NS:
                        dbu_of(n + 1)
                    dve.wait_ge(*filled(("C", n)))
                    o = result(("C", n))
                    dve.wait_ge(S["scanned"], n + 1)
                    if n >= 2:
                        dve.wait_ge(S["hc_added"], n - 1)
                    tt(hc[n % 2], hs[n % 2], over(o[:, 0:N], DIT), ALU.mult).then_inc(*did("hc"))
                    if n + 2 < NS:
                        arg_of(n + 2)
                for m in range(DIT):
                    dve.wait_ge(*filled(("y", m)))
                    o = result(("y", m))
                    stt(u_raw[:, m], u[:, m], sm("D_param", m), o[:, 0:N], ALU.mult, ALU.add).then_inc(*did("y_skip"))
                dve.wait_ge(S["res_silu"], DIT)
                for m in range(DIT):
                    dve.wait_ge(S["y_skip"], m + 1)
                    tt(u_raw[:, m], u_raw[:, m], sres[:, m], ALU.mult).then_inc(*did("y_out"))
                for f in HALVES:
                    residual("wout", h[0], f, "z_mam")
                norm_half(0, h[1])

            def experts():
                dve.wait_ge(*did.latest())
                copy(x_hi, h[1]).then_inc(*did())
                dve.wait_ge(*did.latest())
                tt(x_lo, h[1], exact(x_hi), ALU.subtract).then_inc(*did("x_lo"))
                dve.wait_ge(*filled("gate"))
                o = result("gate")
                copy(lg.rearrange("p t e -> p (t e)"), o[0:TN, 0:TT * NE]).then_inc(*did("gate_copied"))
                dve.wait_ge(*did.latest())
                reduce(gmax, lg, ALU.max).then_inc(*did())
                dve.wait_ge(*did.latest())
                tt(ex, lg, last(gmax, NE), ALU.subtract).then_inc(*did("gate_shift"))
                other, own = lg.unsqueeze(2).to_broadcast([TN, TT, NE, NE]), last(lg, NE)
                tt(cmp1, other, own, ALU.is_gt).then_inc(*did())
                tt(cmp2, other, own, ALU.is_equal).then_inc(*did())
                dve.wait_ge(*did.latest())
                c2 = cmp2.rearrange("p t e f -> p t (e f)")
                tt(c2, c2, over(sm("before", rows=TN), TT), ALU.mult).then_inc(*did())
                dve.wait_ge(*did.latest())
                tt(cmp1, cmp1, cmp2, ALU.add).then_inc(*did())
                dve.wait_ge(*did.latest())
                reduce(rank, cmp1, ALU.add).then_inc(*did())
                dve.wait_ge(*did.latest())
                dve.wait_ge(S["gate_exp"], 1)
                stt(ex, rank, 1.5, ex, ALU.is_lt, ALU.mult).then_inc(*did())
                dve.wait_ge(*did.latest())
                reduce(gsum, ex, ALU.add).then_inc(*did())
                dve.wait_ge(*did.latest())
                dve.reciprocal(grec, gsum).then_inc(*did())
                dve.wait_ge(*did.latest())
                tt(ex, ex, last(grec, NE), ALU.mult).then_inc(*did("comb"))
                dve.wait_ge(*filled("combT"))
                o = result("combT")
                copy(combT, o[0:NE, 0:N]).then_inc(*did("comb_copied"))
                for e in range(NE):
                    if e >= 2:
                        dve.wait_ge(S["act_used"], e - 1)
                    for m in range(HIDT):
                        i = e * HIDT + m
                        x, hi, lo = mixed[e % 2][:, m], act_hi[e % 2][:, m], act_lo[e % 2][:, m]
                        dve.wait_ge(S["silu_h"], i + 1)
                        dve.wait_ge(*filled(("W3", e, m)))
                        o = result(("W3", e, m))
                        tt(gated[i % 2], sil[i % 2], o[:, 0:N], ALU.mult).then_inc(*did("gated"))
                        dve.wait_ge(S["gated"], i + 1)
                        dve.wait_ge(S["combine_copied"], e + 1)
                        tt(x, gated[i % 2], combb[e % 2], ALU.mult).then_inc(*did("moe_act"))
                        dve.wait_ge(S["moe_act"], i + 1)
                        copy(hi, x).then_inc(*did())
                        dve.wait_ge(*did.latest())
                        tt(lo, x, exact(hi), ALU.subtract).then_inc(*did("act_lo"))
                for f in HALVES:
                    for m in range(CT):
                        dve.wait_ge(*filled(("moe", m)))
                        o = result(("moe", m))
                        tt(half(z, f)[:, m], half(o, f), half(h[1], f)[:, m], ALU.add)\
                            .then_inc(*did("z_moe" if m == CT - 1 else None))
                norm_half(1, h[0])

            def attention1():
                def rows(ap):
                    return ap.rearrange("p m (b l) -> p (m b) l", l=L)

                def table(name, n):
                    return sm(name).unsqueeze(1).to_broadcast([P, n, L])

                dve.wait_ge(S["packed_in"], 16)
                wi = wint[:, :].rearrange("p (c r) -> p c r", c=2)
                we = wenc[:, :].rearrange("p (c o) -> p c o", c=2)
                for k in range(4):
                    ts(we[:, :, k * 64:(k + 1) * 64], wi, 2 * k, 3, ALU.logical_shift_right, ALU.bitwise_and)\
                        .then_inc(*did())
                dve.wait_ge(*did.latest())
                ts(wT[:, :], wenc[:, :], -1.0, None, ALU.add).then_inc(*did())
                for f in HALVES:
                    dve.wait_ge(*filled(("q1", f)))
                    o = result(("q1", f))
                    tt(rows(t1a[f]), rows(two(o)), table("cosq", 2 * BH), ALU.mult).then_inc(*did("rope1"))
                    dve.wait_ge(*filled(("q1r", f)))
                    o = result(("q1r", f))
                    tt(rows(t1b[f]), rows(two(o)), table("sinq", 2 * BH), ALU.mult).then_inc(*did("rope1"))
                    dve.wait_ge(*filled(("k1", f)))
                    o = result(("k1", f))
                    tt(tokens(kt1[f]), tokens(o[:, 0:NH]), table("cosk", BH), ALU.mult).then_inc(*did())
                    tt(tokens(kt2[f]), tokens(o[:, NH:2 * NH]), table("sink", BH), ALU.mult).then_inc(*did("rope1"))
                    dve.wait_ge(*did.latest())
                    tt(q1[f], t1a[f], t1b[f], ALU.add).then_inc(*did())
                    tt(k1[f], kt1[f], kt2[f], ALU.add).then_inc(*did())
                    dve.wait_ge(*did.latest())
                    for d in LAGS:
                        tt(pr1[f][d].rearrange("p m (b l) -> p m b l", l=L - d), tokens(q1[f])[:, :, :, d:],
                           over(tokens(k1[f])[:, :, :L - d], CT), ALU.mult)\
                            .then_inc(*did("s1_prod"))
                for f in HALVES:
                    dve.wait_ge(S["s1_copied"], L * (f + 1))
                    reduce(s1m[f], s1[f], ALU.max).then_inc(*did())
                    dve.wait_ge(*did.latest())
                    tt(s1[f], s1[f], last(s1m[f], L), ALU.subtract).then_inc(*did("s1_shift"))
                for f in HALVES:
                    dve.wait_ge(S["s1_exp"], f + 1)
                    reduce(s1s[f], s1e[f], ALU.add).then_inc(*did("s1_sum"))
                by = [s1e[f].rearrange("p (m b l) d -> p m b l d", m=CT, l=L) for f in HALVES]
                ov, tv = [tokens(o1[f]) for f in HALVES], [tokens(t1[f]) for f in HALVES]
                for f in HALVES:
                    dve.wait_ge(S["v1_copied"], f + 1)
                    tt(ov[f], by[f][:, :, :, :, 0], over(tokens(v1[f]), CT), ALU.mult).then_inc(*did())
                for d in range(1, L):
                    for f in HALVES:
                        tt(tv[f][:, :, :, d:], by[f][:, :, :, d:, d], over(tokens(v1[f])[:, :, :L - d], CT), ALU.mult)\
                            .then_inc(*did())
                    dve.wait_ge(*did.latest())
                    for f in HALVES:
                        tt(ov[f][:, :, :, d:], ov[f][:, :, :, d:], tv[f][:, :, :, d:], ALU.add).then_inc(*did())
                    dve.wait_ge(*did.latest())
                for f in HALVES:
                    dve.wait_ge(S["s1_recip"], f + 1)
                    tt(o1[f], o1[f], s1r[f].rearrange("p (m n) -> p m n", m=CT), ALU.mult).then_inc(*did("a1_out"))
                for f in HALVES:
                    residual("wo1", h[0], f, "z_attn1")
                norm_half(2, h[1])

            def ternary():
                for f in HALVES:
                    t2 = slice(2 * f, 2 * f + 2)
                    dve.wait_ge(*filled(("xtok", f)))
                    o = result(("xtok", f))
                    copy(x_tok[:, t2], o[0:TN, :].rearrange("p (t c) -> p t c", t=2)).then_inc(*did("x_tok_copied"))
                    dve.wait_ge(*did.latest())
                    dve.tensor_reduce(amax[:, t2], x_tok[:, t2], AX.X, ALU.max, apply_absolute_value=True).then_inc(*did())
                    dve.wait_ge(*did.latest())
                    ts(amax[:, t2], amax[:, t2], 1e-5, None, ALU.max).then_inc(*did())
                    dve.wait_ge(*did.latest())
                    dve.reciprocal(asc[:, t2], amax[:, t2]).then_inc(*did())
                    dve.wait_ge(*did.latest())
                    ts(asc[:, t2], asc[:, t2], 127.0, None, ALU.mult).then_inc(*did())
                    ts(ainv[:, t2], amax[:, t2], 1.0 / 127.0, sm("l1_scale", 0, TN), ALU.mult, ALU.mult)\
                        .then_inc(*did())
                    dve.wait_ge(*did.latest())
                    for t in range(2 * f, 2 * f + 2):
                        ts(xq[:, t], x_tok[:, t], asc[:, t:t + 1], MAGIC, ALU.mult, ALU.add).then_inc(*did())
                    dve.wait_ge(*did.latest())
                    ts(xq[:, t2], xq[:, t2], -MAGIC, 127.0, ALU.add, ALU.min).then_inc(*did())
                    dve.wait_ge(*did.latest())
                    ts(xq[:, t2], xq[:, t2], -128.0, None, ALU.max).then_inc(*did("x_int"))
                for f in HALVES:
                    dve.wait_ge(*filled(("xint", f)))
                    o = result(("xint", f))
                    copy(half(xT, f), two(o)).then_inc(*did("xint_copied"))
                for f in HALVES:
                    t2 = slice(2 * f, 2 * f + 2)
                    dve.wait_ge(*filled(("l1f", f)))
                    o = result(("l1f", f))
                    for i in range(2):
                        stt(y_tok[:, 2 * f + i], o[0:TN, i * C:(i + 1) * C], ainv[:, 2 * f + i:2 * f + i + 1],
                            sm("l1_bias", rows=TN), ALU.mult, ALU.add)\
                            .then_inc(*did("l1f_read" if i else None))
                    dve.wait_ge(*did.latest())
                    tt(y_tok[:, t2], y_tok[:, t2], x_tok[:, t2], ALU.add).then_inc(*did())
                    dve.wait_ge(*did.latest())
                    for t in range(2 * f, 2 * f + 2):
                        dve.bn_stats(stats[:, t], y_tok[:, t]).then_inc(*did())
                    dve.wait_ge(*did.latest())
                    for t in range(2 * f, 2 * f + 2):
                        dve.bn_aggr(aggr[:, t], stats[:, t]).then_inc(*did("l1f_var" if t % 2 else None))
                for f in HALVES:
                    dve.wait_ge(S["l1f_rstd"], f + 1)
                    for t in range(2 * f, 2 * f + 2):
                        ts(y_tok[:, t], y_tok[:, t], aggr[:, t, 0:1], trs[:, t:t + 1], ALU.subtract, ALU.mult)\
                            .then_inc(*did("h4_tok" if t % 2 else None))
                for f in HALVES:
                    dve.wait_ge(*filled(("h4", f)))
                    o = result(("h4", f))
                    copy(half(h[0], f), two(o)).then_inc(*did("h4_copied"))

            def attention2():
                for f in HALVES:
                    for j in range(QT2 // 2):
                        dve.wait_ge(*filled(("k2", f, j)))
                        o = result(("k2", f, j))
                        copy(half(k2, f)[:, 2 * j:2 * j + 2], two(o)).then_inc(*did("k2_copied"))

                def masked(t):
                    for g in range(4):
                        dve.wait_ge(*filled(("s2", t, g)))
                        o = result(("s2", t, g))
                        tt(s2[:, t, 4 * g:4 * g + 4], o[0:TN, 0:4 * TN].rearrange("p (h k) -> p h k", h=4),
                           over(sm("attmask", rows=TN), 4), ALU.add)\
                            .then_inc(*did("s2_masked"))

                def shifted(t):
                    dve.wait_ge(S["s2_masked"], 4 * (t + 1))
                    reduce(s2m[:, t], s2[:, t], ALU.max).then_inc(*did())
                    dve.wait_ge(*did.latest())
                    tt(s2[:, t], s2[:, t], last(s2m[:, t], TN), ALU.subtract).then_inc(*did("s2_shift"))

                def weights(t):
                    dve.wait_ge(S["s2_exp"], t + 1)
                    reduce(s2s[:, t], s2[:, t], ALU.add).then_inc(*did())
                    dve.wait_ge(*did.latest())
                    dve.reciprocal(s2r[:, t], s2s[:, t]).then_inc(*did())
                    dve.wait_ge(*did.latest())
                    tt(s2[:, t], s2[:, t], last(s2r[:, t], TN), ALU.mult).then_inc(*did("s2_prob"))

                def heads_out(t):
                    for g in range(2):
                        dve.wait_ge(*filled(("o2", t, g)))
                        o = result(("o2", t, g))
                        copy(o2[:, 4 * g:4 * g + 4, t * TN:(t + 1) * TN],
                             o[:, 0:4 * TN].rearrange("p (m q) -> p m q", m=4))\
                            .then_inc(*did("o2_copied"))

                masked(0)
                shifted(0)
                masked(1)
                for t in range(TT):
                    weights(t)
                    if t == 0:
                        shifted(1)
                    if t + 2 < TT:
                        masked(t + 2)
                        shifted(t + 2)
                    if t == 3:
                        residual("r2", h[0], 0, "z_attn2")
                        centre(3, 0)
                    heads_out(t)
                scale(3, 0, h[1])
                residual("r2", h[0], 1, "z_attn2")
                centre(3, 1)
                scale(3, 1, h[1])

            def coupling():
                dve.wait_ge(*did.latest())
                ts(r2[:, 0:1], sm("gc_b3"), 0.5, None, ALU.mult).then_inc(*did())
                ts(r2[:, 1:2], sm("cn_b4"), 0.5, None, ALU.mult).then_inc(*did())
                for f in HALVES:
                    for m in range(CT):
                        reduce(gmn[f][:, m], tokens(half(h[1], f)[:, m]), ALU.add).then_inc(*did())
                    dve.wait_ge(*did.latest())
                    ts(gmn[f], gmn[f], 1.0 / L, None, ALU.mult).then_inc(*did("gmean"))
                for f in HALVES:
                    dve.wait_ge(S["gc_act"], 4 + f + 1)
                    ts(gf[f], gf[f], 0.7, None, ALU.mult).then_inc(*did())
                dve.wait_ge(*did.latest())
                for cyc in range(3):
                    for f in HALVES:
                        x = half(h[1], f) if cyc == 0 else cout[(cyc - 1) % 2][f]
                        y = cout[cyc % 2][f]
                        c = coup[f]
                        dve.wait_ge(S["c4_act"], CT * cyc + f + 1)
                        stt(tokens(c), tokens(cn_t[f]), 0.3, last(gf[f], L), ALU.mult, ALU.add).then_inc(*did())
                        dve.wait_ge(*did.latest())
                        ts(c, c, sm("range"), 0.1, ALU.mult, ALU.add).then_inc(*did())
                        dve.wait_ge(*did.latest())
                        ts(c, c, sm("sign"), None, ALU.mult).then_inc(*did())
                        dve.wait_ge(*did.latest())
                        tt(ctmp[f][:, 0], c, x[:, 1], ALU.mult).then_inc(*did())
                        tt(ctmp[f][:, 1], c, x[:, 0], ALU.mult).then_inc(*did())
                        dve.wait_ge(*did.latest())
                        tt(y[:, 0], x[:, 0], ctmp[f][:, 0], ALU.add).then_inc(*did())
                        tt(y[:, 1], x[:, 1], ctmp[f][:, 1], ALU.subtract).then_inc(*did("c_out"))
                dve.wait_ge(*did.latest())
                for f in HALVES:
                    tt(half(z, f), half(h[1], f), cout[0][f], ALU.add).then_inc(*did("z_ffn2"))
                norm_half(4, h[0])

            def attention3():
                flat = "p m n -> p (m n)"
                for f in HALVES:
                    dve.wait_ge(*filled(("gk2", f)))
                    o = result(("gk2", f))
                    for m in range(CT):
                        c = two(o)[:, m]
                        ts(gmin[f][:, m], c, sm("bgk2", m), 0.0, ALU.add, ALU.min).then_inc(*did())
                        ts(gaz[f][:, m], c, sm("bgk2", m), None, ALU.add)\
                            .then_inc(*did("gk_min" if m == CT - 1 else None))
                    dve.wait_ge(*did.latest())
                    stt(gaz[f], gmin[f], -2.0, gaz[f], ALU.mult, ALU.add).then_inc(*did("gk_abs"))
                dve.wait_ge(S["keep_set"], 1)
                for f in HALVES:
                    dve.wait_ge(S["gk_log"], f + 1)
                    tt(gmin[f], gmin[f], gaz[f], ALU.subtract).then_inc(*did())
                    dve.wait_ge(*did.latest())
                    ts(gmin[f], gmin[f], 1.0 / 16.0, None, ALU.mult).then_inc(*did())
                    dve.wait_ge(*did.latest())
                    dve.tensor_tensor_scan(gcum[f].rearrange(flat), keep, gmin[f].rearrange(flat),
                                               0.0, ALU.mult, ALU.add).then_inc(*did())
                    dve.wait_ge(*did.latest())
                    gt = tokens(gcum[f])
                    for d in range(1, L):
                        tt(gdf_d[f][d].rearrange("p m (b l) -> p m b l", l=L - d), gt[:, :, :, d:],
                           gt[:, :, :, :L - d], ALU.subtract)\
                            .then_inc(*did("g_diff" if d == L - 1 else None))
                for f in HALVES:
                    dve.wait_ge(S["qkv3_copied"], 2 * f + 2)
                    qt, kt = tokens(q3[f]), tokens(k3[f])
                    for d in LAGS:
                        tt(pr3_d[f][d].rearrange("p m (b l) -> p m b l", l=L - d), qt[:, :, :, d:],
                           kt[:, :, :, :L - d], ALU.mult)\
                            .then_inc(*did("s3_prod" if d == 0 else None))
                    dve.wait_ge(*did.latest())
                    dve.wait_ge(S["g_exp"], f + 1)
                    for d in range(1, L):
                        tt(pr3_d[f][d], pr3_d[f][d], gdf_d[f][d], ALU.mult).then_inc(*did("s3_prod"))
                i = 0
                for f in HALVES:
                    dve.wait_ge(S["qkv3_copied"], 4 + 2 * (f + 1))
                    adds = []
                    for d in LAGS:
                        for odd in range(2):
                            dve.wait_ge(*filled(("s3", f, d, odd)))
                            o = result(("s3", f, d, odd))
                            src = two(o)[:, :, 0:BH * (L - d)].rearrange("p m (b l) -> p m b l", l=L - d)
                            dst = tokens(o3[f][:, odd::2])[:, :, :, d:]
                            tmp = dst if d == 0 else tokens(t3[i % 4])[:, :, :, d:]
                            tt(tmp, src, tokens(v3[f][:, odd::2])[:, :, :, :L - d], ALU.mult).then_inc(*did("s3_mul"))
                            i += 1
                            if adds:
                                a_dst, a_tmp, a_i = adds.pop()
                                dve.wait_ge(S["s3_mul"], a_i)
                                tt(a_dst, a_dst, a_tmp, ALU.add).then_inc(*did())
                            if d:
                                adds.append((dst, tmp, i))
                    a_dst, a_tmp, a_i = adds.pop()
                    dve.wait_ge(S["s3_mul"], a_i)
                    tt(a_dst, a_dst, a_tmp, ALU.add).then_inc(*did("o3_sum"))
                    dve.wait_ge(S["o3_sum"], f + 1)
                for f in HALVES:
                    dve.wait_ge(S["o3_rstd"], f + 1)
                    stt(o3[f].rearrange(flat), o3[f].rearrange(flat), sm("gnorm"), rs3[f].rearrange(flat),
                        ALU.mult, ALU.mult).then_inc(*did())
                    dve.wait_ge(*did.latest())
                    dve.wait_ge(S["g3_silu"], 2 * (f + 1))
                    tt(o3[f], o3[f], sg3[f], ALU.mult).then_inc(*did("o3_out"))
                for f in HALVES:
                    residual("wo3", h[0], f, "z_attn3")
                norm_half(5, h[1])

            def last_ffn():
                for f in HALVES:
                    dve.wait_ge(S["ln_out"], norm_at(5, f))
                    copy(half(x3_hi, f), half(h[1], f)).then_inc(*did())
                    dve.wait_ge(*did.latest())
                    tt(half(x3_lo, f), half(h[1], f), exact(half(x3_hi, f)), ALU.subtract).then_inc(*did("x_lo"))

                def parts(x, hi, lo):
                    copy(hi, x).then_inc(*did())
                    dve.wait_ge(*did.latest())
                    tt(lo, x, exact(hi), ALU.subtract).then_inc(*did("act_lo"))

                def tile_low(c):
                    dve.wait_ge(S["w_hi"], W0 + 3 * NE + c + 1)
                    if c < 2 * HT3:
                        tt(fh_tile(c, BIG_R), fh_tile(c), exact(fh_hi(c)), ALU.subtract).then_inc(*did("w_lo"))
                    elif c == 2 * HT3:
                        tt(weight(WMAM_R, W_F3, "w3"), weight(WMAM, W_F3, "w3"), exact(w3_hi), ALU.subtract)\
                            .then_inc(*did("w_lo"))

                for m in range(HT3):
                    dve.wait_ge(S["f1_silu"], m + 1)
                    dve.wait_ge(*filled(("w2", m)))
                    o = result(("w2", m))
                    stt(fa[:, m], o[:, 0:N], sm("w2_s", m), fsil[m % 2], ALU.mult, ALU.mult).then_inc(*did("f_gate"))
                    dve.wait_ge(S["f_gate"], m + 1)
                    parts(fa[:, m], fa_hi[:, m], fa_lo[:, m])
                    if m in (3, 6):
                        tile_low(m // 3 - 1)
                for m in range(HT3):
                    dve.wait_ge(S["fh1_act"], m + 1)
                    parts(fb[:, m], fb_hi[:, m], fb_lo[:, m])
                    tile_low(m + 2)
                for m in range(HT3):
                    dve.wait_ge(S["fh2_act"], m + 1)
                    parts(fa[:, m], fa_hi[:, m], fa_lo[:, m])
                    if m < HT3 - 1:
                        tile_low(HT3 + m + 2)
                for f in HALVES:
                    for m in range(CT):
                        dve.wait_ge(*filled(("f3", m)))
                        o = result(("f3", m))
                        stt(half(z, f)[:, m], half(o, f), sm("w3_s", m), half(h[1], f)[:, m], ALU.mult, ALU.add)\
                            .then_inc(*did("z_ffn3" if m == CT - 1 else None))
                norm_half(6, h[0])
                for f in HALVES:
                    dve.wait_ge(*filled(("out", f)))
                    o = result(("out", f))
                    copy(otok[:, 2 * f:2 * f + 2], o[0:TN, :].rearrange("p (t c) -> p t c", t=2))\
                        .then_inc(*did("tok_out"))

            for f in [tokenizer, state_space, experts, attention1, ternary, attention2, coupling, attention3, last_ffn]:
                f()

        @block.scalar
        def _(act):
            did = Counts(S, "act_step")
            act_fn = act.activation

            ln_at = [0]

            def norm(key, n):
                i = ln_at[0] = ln_at[0] + 1
                act.wait_ge(S["ln_xc"], i)
                act_fn(sq[:, :, 0:n], xc[:, :, 0:n], ACT.Square).then_inc(*did("ln_sq"))
                act.wait_ge(*filled((key, "var")))
                var = result((key, "var"))[:, 0:n]
                act_fn(SQ[:, 0:n], var, ACT.Ln, bias=sm("eps")).then_inc(*did("ln_logvar"))
                act.wait_ge(*did.latest())
                act_fn(SQ[:, N:N + n], SQ[:, 0:n], ACT.Exp, scale=-0.5).then_inc(*did("ln_rstd"))

            def square(i, f):
                act.wait_ge(S["ln_xc"], norm_at(i, f))
                act_fn(sqh[f], half(xc, f), ACT.Square).then_inc(*did("ln_sq"))

            def rstd(i, f):
                act.wait_ge(*filled(("var", i, f)))
                o = result(("var", i, f))
                act_fn(sqh[f][:, 0], o[:, 0:NH], ACT.Ln, bias=sm("eps")).then_inc(*did("ln_logvar"))
                act.wait_ge(*did.latest())
                act_fn(sqh[f][:, 1], sqh[f][:, 0], ACT.Exp, scale=-0.5).then_inc(*did("ln_rstd"))

            def norm_half(i):
                for f in HALVES:
                    square(i, f)
                for f in HALVES:
                    rstd(i, f)

            def tokenizer():
                act.preload_act_table_set("natural_log_exp_and_others")
                act.wait_ge(S["small_in"], 16)
                norm("cls", 1)

                def high(j):
                    act.wait_ge(S[f"patches_in_{j}"], 16 * KCT)
                    if j >= 3:
                        act.wait_ge(S["pe0_copied"], j - 1)
                    x, hi = patch_part(PAT, j), patch_hi(j)
                    act_fn(hi[0], x[0], ACT.Copy).then_inc(*did())
                    act_fn(hi[1], x[1], ACT.Copy).then_inc(*did("w_hi"))

                act.wait_ge(S["conv_w_in"], 16)
                act_fn(cw_hi, view(WTOK, 0, KCT, C), ACT.Copy).then_inc(*did("w_hi"))
                high(1)
                for j in range(NCH + 2):
                    if j < NCH:
                        n = min(CHUNK, NP - j * CHUNK)
                        act.wait_ge(*filled(("conv", j, 1)))
                        o = result(("conv", j, 1))
                        act_fn(pe_all[:, 1, j * CHUNK:j * CHUNK + n], o[:, 0:n], ACT.Copy)\
                            .then_inc(*did("pe1_copied"))
                        if j + 2 < NCH:
                            high(j + 2)
                    if 1 <= j <= NCH:
                        i = j - 1
                        n = min(CHUNK, NP - i * CHUNK)
                        c = slice(i * CHUNK, i * CHUNK + n)
                        act.wait_ge(S["w_xc"], i + 1)
                        act_fn(sq_all[:, :, c], xn_all[:, :, c], ACT.Square).then_inc(*did("w_sq"))
                    if j >= 2:
                        i = j - 2
                        n = min(CHUNK, NP - i * CHUNK)
                        act.wait_ge(*filled(("wvar", i)))
                        o = result(("wvar", i))
                        if i:
                            act.wait_ge(S["w_rstd"], i)
                        act_fn(w_log[:, 0:n], o[:, 0:n], ACT.Ln, bias=sm("eps")).then_inc(*did("w_logvar"))
                        act.wait_ge(*did.latest())
                        if i:
                            act.wait_ge(S["w_xn"], i)
                        act_fn(w_rs[:, 0:n], w_log[:, 0:n], ACT.Exp, scale=-0.5).then_inc(*did("w_rstd"))
                norm("red", NW)
                act.wait_ge(*filled("q"))
                o = result("q")
                act_fn(q_w.rearrange("p t c -> p (t c)"), o[:, :], ACT.Copy, scale=float(C) ** -0.5)\
                    .then_inc(*did("q_copied"))
                i = 0
                for t in range(2):
                    for k in range(TAPS):
                        i += 1
                        act.wait_ge(S["kq_done"], i)
                        act.wait_ge(*filled(("kv", k, t)))
                        o = result(("kv", k, t))
                        act_fn(v_w[:, t, k], o[:, C:2 * C], ACT.Copy).then_inc(*did("v_copied"))
                    act.wait_ge(S["la_shift"], t + 1)
                    act_fn(sc_e[:, t], sc_e[:, t], ACT.Exp).then_inc(*did("la_exp"))
                norm("lo", NW)
                act.wait_ge(*filled("gk"))
                o = result("gk")
                act_fn(gkT.rearrange("p m w -> p (m w)"), o[:, :], ACT.Copy).then_inc(*did("gk_copied"))
                act.wait_ge(S["gs_shift"], 1)
                act_fn(gse, gs, ACT.Exp).then_inc(*did("gs_exp"))

            def split_part(e, i):
                if e >= 2:
                    act.wait_ge(S["up_used" if i < 2 else "act_used"], e - 1)
                at = i * PART
                act_fn(exp_hi[e % 2][:, at:at + PART], BIG[:, e * N_EXP + at:e * N_EXP + at + PART], ACT.Copy)\
                    .then_inc(*did("w_hi"))

            def split(e):
                act.wait_ge(expert_in[e // 4], 16)
                for i in range(3):
                    split_part(e, i)

            def state_space():
                act.wait_ge(S["a_clip"], 1)
                act_fn(negA, negA, ACT.Exp).then_inc(*did("a_exp"))
                act.wait_ge(S["u_conv"], DIT)
                act_fn(u, u_raw, ACT.Silu).then_inc(*did("u_silu"))
                for m in range(DIT):
                    act.wait_ge(*filled(("win", DIT + m)))
                    o = result(("win", DIT + m))
                    act_fn(sres[:, m], o[:, 0:N], ACT.Silu).then_inc(*did("res_silu"))
                act.preload_act_table_set("natural_log_exp_and_others")
                for m in range(DIT):
                    act.wait_ge(*filled(("wdt", m)))
                    o = result(("wdt", m))
                    act_fn(az[:, m], o[:, 0:N], ACT.Abs, bias=sm("b_dt", m)).then_inc(*did("dt_abs"))
                act.wait_ge(*did.latest())
                act_fn(e1, az, ACT.Exp, scale=-1.0).then_inc(*did("dt_exp"))
                act.wait_ge(S["dt_exp1"], 1)
                act_fn(az, w1, ACT.Ln).then_inc(*did("dt_log"))
                for n in range(NS):
                    act.wait_ge(S["arg"], n + 1)
                    a = arg[n % 2].rearrange("p m (b l) -> p (m b) l", l=L)[:, :, 1:]
                    act_fn(a, a, ACT.Exp).then_inc(*did("decay"))
                act.wait_ge(S["cls_out"], 1)
                act.wait_ge(S["patch_out"], 1)
                split(0)
                split(1)
                norm_half(0)

            def experts():
                act.wait_ge(S["gate_shift"], 1)
                act_fn(ex, ex, ACT.Exp).then_inc(*did("gate_exp"))
                act.preload_act_table_set("silu_and_others")
                for e in range(NE):
                    for m in range(HIDT):
                        i = e * HIDT + m
                        act.wait_ge(*filled(("W1", e, m)))
                        o = result(("W1", e, m))
                        if i >= 2:
                            act.wait_ge(S["gated"], i - 1)
                        act_fn(sil[i % 2], o[:, 0:N], ACT.Silu).then_inc(*did("silu_h"))
                        if m == 0:
                            act.wait_ge(*filled(("comb", e)))
                            o = result(("comb", e))
                            if e >= 2:
                                act.wait_ge(S["moe_act"], HIDT * (e - 1))
                            act_fn(combb[e % 2], o[:, 0:N], ACT.Copy).then_inc(*did("combine_copied"))
                        if 1 <= e < NE - 1:
                            act.wait_ge(expert_in[(e + 1) // 4], 16)
                            split_part(e + 1, m)
                act.preload_act_table_set("natural_log_exp_and_others")
                norm_half(1)

            def attention1():
                for f in HALVES:
                    act.wait_ge(*filled(("v1", f)))
                    o = result(("v1", f))
                    act_fn(v1[f], o[:, 0:NH], ACT.Copy).then_inc(*did("v1_copied"))
                act.wait_ge(S["s1_clear"], 2)
                for f in HALVES:
                    by = s1[f].rearrange("p (m b l) d -> p m b l d", m=CT, l=L)
                    for d in LAGS:
                        act.wait_ge(*filled(("s1", f, d)))
                        o = result(("s1", f, d))
                        act_fn(by[:, :, :, d:, d],
                               two(o)[:, :, 0:BH * (L - d)].rearrange("p m (b l) -> p m b l", l=L - d), ACT.Copy)\
                            .then_inc(*did("s1_copied"))
                for f in HALVES:
                    act.wait_ge(S["s1_shift"], f + 1)
                    act_fn(s1e[f], s1[f], ACT.Exp).then_inc(*did("s1_exp"))
                for f in HALVES:
                    act.wait_ge(S["s1_sum"], f + 1)
                    act_fn(s1r[f], s1s[f], ACT.Ln).then_inc(*did())
                    act.wait_ge(*did.latest())
                    act_fn(s1r[f], s1r[f], ACT.Exp, scale=-1.0).then_inc(*did("s1_recip"))
                norm_half(2)

            def ternary():
                for f in HALVES:
                    act.wait_ge(S["l1f_var"], f + 1)
                    act_fn(tmean[:, 2 * f:2 * f + 2], aggr[:, 2 * f:2 * f + 2, 1], ACT.Ln, bias=sm("eps", rows=TN))\
                        .then_inc(*did())
                    act.wait_ge(*did.latest())
                    act_fn(trs[:, 2 * f:2 * f + 2], tmean[:, 2 * f:2 * f + 2], ACT.Exp, scale=-0.5)\
                        .then_inc(*did("l1f_rstd"))

            def attention2():
                for f in HALVES:
                    for j in range(QT2 // 2):
                        act.wait_ge(*filled(("q2", f, j)))
                        o = result(("q2", f, j))
                        act_fn(half(q2, f)[:, 2 * j:2 * j + 2], two(o), ACT.Copy, scale=float(HD2) ** -0.5)\
                            .then_inc(*did("q2_copied"))

                def exps(t):
                    act.wait_ge(S["s2_shift"], t + 1)
                    act_fn(s2[:, t], s2[:, t], ACT.Exp).then_inc(*did("s2_exp"))

                exps(0)
                for t in range(TT):
                    for hf in range(2):
                        act.wait_ge(*filled(("v2", t, hf)))
                        o = result(("v2", t, hf))
                        act_fn(v2[:, t, hf * 512:(hf + 1) * 512], o[0:TN, :], ACT.Copy).then_inc(*did("v2_copied"))
                    if t + 1 < TT:
                        exps(t + 1)
                    for g in range(4):
                        act.wait_ge(*filled(("pT", t, g)))
                        o = result(("pT", t, g))
                        act_fn(pT[t % 2][:, 4 * g:4 * g + 4], o[0:TN, 0:4 * TN].rearrange("p (h q) -> p h q", h=4),
                               ACT.Copy).then_inc(*did("pT_copied"))
                square(3, 0)
                rstd(3, 0)
                square(3, 1)
                rstd(3, 1)

            def coupling():
                act.preload_act_table_set("gelu_and_others")

                def first(cyc, f):
                    act.wait_ge(*filled(("c1", cyc, f)))
                    o = result(("c1", cyc, f))
                    for m in range(CT):
                        act_fn(cn_a[f][:, m], two(o)[:, m], ACT.Gelu, bias=sm("cn_b1", m))\
                            .then_inc(*did("c1_act" if m == CT - 1 else None))

                for f in HALVES:
                    act.wait_ge(*filled(("gc1", f)))
                    o = result(("gc1", f))
                    act_fn(gc_a[f], o[:, 0:BH], ACT.Gelu, bias=sm("gc_b1")).then_inc(*did("gc_act"))
                    first(0, f)
                for f in HALVES:
                    act.wait_ge(*filled(("gc2", f)))
                    o = result(("gc2", f))
                    act_fn(gc_b[f], o[0:64, 0:BH], ACT.Gelu, bias=sm("gc_b2", rows=64)).then_inc(*did("gc_act"))
                for f in HALVES:
                    act.wait_ge(*filled(("gc3", f)))
                    o = result(("gc3", f))
                    act_fn(gf[f], o[:, 0:BH], ACT.Tanh, scale=0.5, bias=r2[:, 0:1]).then_inc(*did("gc_act"))
                for cyc in range(3):
                    if cyc:
                        for f in HALVES:
                            first(cyc, f)
                    for f in HALVES:
                        act.wait_ge(*filled(("c2", cyc, f)))
                        o = result(("c2", cyc, f))
                        act_fn(cn_b[f], o[:, 0:NH], ACT.Gelu, bias=sm("cn_b2")).then_inc(*did("c2_act"))
                    for f in HALVES:
                        act.wait_ge(*filled(("c3", cyc, f)))
                        o = result(("c3", cyc, f))
                        act_fn(cn_c[f], o[0:64, 0:NH], ACT.Gelu, bias=sm("cn_b3", rows=64)).then_inc(*did("c3_act"))
                    for f in HALVES:
                        act.wait_ge(*filled(("c4", cyc, f)))
                        o = result(("c4", cyc, f))
                        act_fn(cn_t[f], o[:, 0:NH], ACT.Tanh, scale=0.5, bias=r2[:, 1:2]).then_inc(*did("c4_act"))
                act.preload_act_table_set("natural_log_exp_and_others")
                norm_half(4)

            def attention3():
                for f in HALVES:
                    act.wait_ge(*filled(("gk1", f)))
                    o = result(("gk1", f))
                    act_fn(gk1[f], o[0:RANK, 0:NH], ACT.Copy).then_inc(*did("gk1_copied"))
                    act.wait_ge(*filled(("q3", f)))
                    o = result(("q3", f))
                    act_fn(q3[f], two(o), ACT.Copy, scale=0.125).then_inc(*did("qkv3_copied"))
                    act.wait_ge(*filled(("k3", f)))
                    o = result(("k3", f))
                    act_fn(k3[f], two(o), ACT.Copy).then_inc(*did("qkv3_copied"))
                for f in HALVES:
                    act.wait_ge(S["gk_abs"], f + 1)
                    act_fn(gaz[f], gaz[f], ACT.Exp, scale=-1.0).then_inc(*did())
                    act.wait_ge(*did.latest())
                    act_fn(gaz[f], gaz[f], ACT.Ln, bias=sm("one")).then_inc(*did("gk_log"))
                for f in HALVES:
                    for j in range(2):
                        act.wait_ge(*filled(("v3", f, j)))
                        o = result(("v3", f, j))
                        act_fn(v3[f][:, 2 * j:2 * j + 2], two(o), ACT.Copy).then_inc(*did("qkv3_copied"))
                for f in HALVES:
                    act.wait_ge(S["g_diff"], f + 1)
                    late = view(PAT, D3 + CT * (PAIRS * f + PAIR_OFF[1]), CT * (PAIRS - PAIR_OFF[1]))
                    act_fn(late, late, ACT.Exp).then_inc(*did("g_exp"))
                for f in HALVES:
                    for j in range(2):
                        act.wait_ge(*filled(("g3", f, j)))
                        o = result(("g3", f, j))
                        act_fn(sg3[f][:, 2 * j:2 * j + 2], two(o), ACT.Silu).then_inc(*did("g3_silu"))
                act.preload_act_table_set("natural_log_exp_and_others")
                for f in HALVES:
                    act.wait_ge(S["o3_sum"], f + 1)
                    act_fn(osq[f], o3[f], ACT.Square).then_inc(*did("o3_sq"))
                for f in HALVES:
                    for j in range(2):
                        act.wait_ge(*filled(("ms3", f, j)))
                        o = result(("ms3", f, j))
                        act_fn(rs3[f][:, 2 * j:2 * j + 2], two(o), ACT.Ln, bias=sm("eps")).then_inc(*did("o3_logvar"))
                    act.wait_ge(*did.latest())
                    act_fn(rs3[f], rs3[f], ACT.Exp, scale=-0.5).then_inc(*did("o3_rstd"))
                norm_half(5)

            def last_ffn():
                act.preload_act_table_set("silu_and_others")
                act.wait_ge(S["z_attn3"], 2)
                pieces = [0]

                def high():
                    c = pieces[0]
                    pieces[0] = c + 1
                    if c == EARLY:
                        act.wait_ge(S["f_gate"], HT3)
                    if c < 2 * HT3:
                        if c >= len(fh_slots):
                            act.wait_ge(S["fh1_act"], c - len(fh_slots) + 1)
                        act_fn(fh_hi(c), fh_tile(c), ACT.Copy).then_inc(*did("w_hi"))
                    elif c == 2 * HT3:
                        act_fn(w3_hi, weight(WMAM, W_F3, "w3"), ACT.Copy).then_inc(*did("w_hi"))

                act.wait_ge(S["fh_w_in"], 32)
                for m in range(HT3):
                    act.wait_ge(*filled(("w1", m)))
                    o = result(("w1", m))
                    if m >= 2:
                        act.wait_ge(S["f_gate"], m - 1)
                    act_fn(fsil[m % 2], o[:, 0:N], ACT.Silu, scale=sm("w1_s", m)).then_inc(*did("f1_silu"))
                    if m < EARLY:
                        high()
                act.preload_act_table_set("gelu_and_others")
                for m in range(HT3):
                    act.wait_ge(*filled(("h1", m)))
                    o = result(("h1", m))
                    act_fn(fb[:, m], o[:, 0:N], ACT.Gelu, scale=sm("h1_s", m)).then_inc(*did("fh1_act"))
                    high()
                for m in range(HT3):
                    act.wait_ge(*filled(("h2", m)))
                    o = result(("h2", m))
                    act_fn(fa[:, m], o[:, 0:N], ACT.Gelu, scale=sm("h2_s", m)).then_inc(*did("fh2_act"))
                    high()
                act.preload_act_table_set("natural_log_exp_and_others")
                norm_half(6)

            for f in [tokenizer, state_space, experts, attention1, ternary, attention2, coupling, attention3, last_ffn]:
                f()

        @block.gpsimd
        def _(pool):
            did = Counts(S, "pool_step")

            def tokenizer():
                pool.wait_ge(S["w_lo"], 2)
                for j in range(2, NCH):
                    x, hi, lo = patch_part(PAT, j), patch_hi(j), patch_part(PAT_R, j)
                    pool.wait_ge(S["w_hi"], j + 1)
                    pool.tensor_tensor(lo[0], x[0], exact(hi[0]), ALU.subtract).then_inc(*did())
                    pool.tensor_tensor(lo[1], x[1], exact(hi[1]), ALU.subtract).then_inc(*did("w_lo"))

            def state_space():
                pool.wait_ge(S["cls_out"], 1)
                for i in range(2):
                    pool.memset(arg[i], 0.0).then_inc(*did("arg_zero"))

            def experts():
                for e in range(NE):
                    for i in range(3):
                        at = i * PART
                        c = slice(e * N_EXP + at, e * N_EXP + at + PART)
                        pool.wait_ge(S["w_hi"], W0 + 3 * e + i + 1)
                        pool.tensor_tensor(BIG_R[:, c], BIG[:, c], exact(exp_hi[e % 2][:, at:at + PART]), ALU.subtract).then_inc(*did("w_lo"))

            def attention1():
                pool.wait_ge(S["z_moe"], CT)
                for f in HALVES:
                    pool.memset(s1[f], FAR).then_inc(*did("s1_clear"))

            def attention3():
                pool.wait_ge(S["z_attn2"], CT)
                pool.memset(keep, 1.0).then_inc(*did())
                pool.wait_ge(*did.latest())
                pool.memset(keep.rearrange("p (x l) -> p x l", l=L)[:, :, 0], 0.0).then_inc(*did("keep_set"))

            def split_first():
                pool.wait_ge(S["f1_w_in"], 16)
                for k in range(CT):
                    pool.tensor_copy(w1_hi[:, k], weight(WTOK, W_F1, "w1")[:, k]).then_inc(*did())
                for m in range(HT3):
                    pool.tensor_copy(w2_hi[m], weight(WTOK, W_F1, "w2")[:, :, m * P:(m + 1) * P]).then_inc(*did())
                pool.wait_ge(*did.latest())
                w = weight(WTOK, W_F1, "w1")
                pool.tensor_tensor(weight(WTOK_R, W_F1, "w1"), w, exact(w1_hi), ALU.subtract).then_inc(*did("w_lo"))
                for m in range(HT3):
                    w, w_lo = (weight(buf, W_F1, "w2")[:, :, m * P:(m + 1) * P] for buf in (WTOK, WTOK_R))
                    pool.tensor_tensor(w_lo, w, exact(w2_hi[m]), ALU.subtract).then_inc(*did("w_lo" if m == HT3 - 1 else "pool_step"))

            for f in (tokenizer, state_space, experts, attention1, attention3, split_first):
                f()

        @block.sync
        def _(sync):
            def load(dst, src, signal):
                sync.dma_start(dst, src).then_inc(S[signal], 16)

            load(SM[:, :], small, "small_in")
            nconv = KCT * C
            load(WTOK[:, 0:nconv], w_tok[:, 0:nconv], "conv_w_in")
            for j in range(NCH):
                n = min(CHUNK, NP - j * CHUNK)
                for k in range(KCT):
                    r = min(P, KC - k * P)
                    load(PAT[0:r, k * NP + j * CHUNK:k * NP + j * CHUNK + n],
                         patches[k * P:k * P + r, j * CHUNK:j * CHUNK + n], f"patches_in_{j}")
            load(WTOK[:, nconv:N_TOK], w_tok[:, nconv:], "tok_w_in")
            load(WMAM[:, 0:N_MAM], w_mam, "mam_w_in")
            load(wint[:, :], packed, "packed_in")
            sync.wait_ge(S["cls_out"], 1)
            for i in range(NE // 4):
                c = slice(4 * i * N_EXP, 4 * (i + 1) * N_EXP)
                sync.dma_start(BIG[:, c], w_exp[:, c]).then_inc(expert_in[i], 16)
            sync.wait_ge(S["z_mam"], CT)
            load(PAT[:, N_L2:N_L2 + N_L1], w_l1, "l1_w_in")
            load(PAT[:, 0:N_L2], w_l2, "l2_w_in")
            load(WMAM[:, 0:N_F3], w_f3, "f3_w_in")
            sync.wait_ge(S["z_moe"], 2)
            load(WTOK[:, 0:N_F1], w_f1, "f1_w_in")
            sync.wait_ge(S["z_attn2"], CT)
            load(PAT[:, 0:N_L3], w_l3, "l3_w_in")
            half = N_FH // 2
            for i in range(2):
                load(BIG[:, i * half:(i + 1) * half], w_fh[:, i * half:(i + 1) * half], "fh_w_in")
            for f in HALVES:
                sync.wait_ge(S["tok_out"], f + 1)
                sync.dma_start(out[f * NH:(f + 1) * NH, :].rearrange("(t p) c -> p t c", t=2),
                               otok[:, 2 * f:2 * f + 2]).then_inc(S["stored"], 16)
            sync.wait_ge(S["stored"], 16 * len(HALVES))


def layout(x):
    def cols(v):
        return np.ascontiguousarray(v.reshape(-1, P).T)

    def wt(w):
        k = w.shape[0] // P
        return w.reshape(k, P, w.shape[1]).transpose(1, 0, 2).reshape(P, -1)

    def low(w):
        return np.concatenate([w, np.zeros((P - w.shape[0], w.shape[1]), w.dtype)])

    def rep(v):
        return np.broadcast_to(v.reshape(1, -1), (P, v.size))

    f = np.float32
    p = np.arange(P)
    pos = np.arange(L, dtype=np.float64)
    freq = 1.0 / 1000.0 ** (np.arange(0, HD1, 2) / HD1)
    ang = pos[None, :] * freq[p % 8][:, None]
    side = np.where(p % HD1 < 8, -1.0, 1.0)[:, None]
    tok = np.arange(TN)
    same = (tok[:, None] // L) == (tok[None, :] // L)
    mask = np.where(same, np.where(tok[None, :] > tok[:, None], -50.0, 0.0), FAR)
    e = np.arange(NE)
    g = {k: v for k, v in x.items()}
    parts = {
        "ident": np.eye(P), "same32": p[:, None] // 32 == p[None] // 32, "same16": p[:, None] // 16 == p[None] // 16,
        "inv256": np.full((P, 1), 1 / 256), "inv128": np.full((P, 1), 1 / 128), "one": np.ones((P, 1)),
        "eps": np.full((P, 1), EPS), "sign": np.where(p < 64, 1.0, -1.0)[:, None],
        "before": rep((e[None, :] < e[:, None]).astype(f)), "cosq": np.cos(ang) / 4, "sinq": side * np.sin(ang) / 4,
        "cosk": np.cos(ang), "sink": side * np.sin(ang), "attmask": low(mask),
        "W_conv": g["L0_attn_W_conv"].reshape(4, P, 3).transpose(1, 0, 2).reshape(P, 12),
        "b_dt": cols(g["L0_attn_b_dt"]), "A_log": g["L0_attn_A_log"].reshape(4, P, NS).transpose(1, 0, 2).reshape(P, 64),
        "D_param": cols(g["L0_attn_D_param"]), "Wr": wt(g["L0_ffn_Wr"]),
        "l1_bias": rep(g["L1_ffn_bias"]), "l1_scale": rep(g["L1_ffn_weight_scale"]),
        "cn_b1": cols(g["L2_ffn_cn_b1"]), "cn_b2": cols(g["L2_ffn_cn_b2"]), "cn_b3": low(g["L2_ffn_cn_b3"].reshape(-1, 1)),
        "cn_b4": rep(g["L2_ffn_cn_b4"]), "gc_b1": cols(g["L2_ffn_gc_b1"]), "gc_b2": low(g["L2_ffn_gc_b2"].reshape(-1, 1)),
        "gc_b3": rep(g["L2_ffn_gc_b3"]), "range": rep(g["L2_ffn_adaptive_range"]), "bgk2": cols(g["L3_attn_bgk2"]),
        "gnorm": g["L3_attn_g_norm_weight"].reshape(P, 1), "w1_s": cols(g["L3_ffn_w1_s"]), "w2_s": cols(g["L3_ffn_w2_s"]),
        "h1_s": cols(g["L3_ffn_h1_s"]), "h2_s": cols(g["L3_ffn_h2_s"]), "w3_s": cols(g["L3_ffn_w3_s"]),
    }
    for n in ("la_ln_q_g", "la_ln_q_b", "la_ln_kv_g", "la_ln_kv_b", "la_proj_b", "ga_ln_q_g", "ga_ln_q_b", "ga_ln_kv_g",
              "ga_ln_kv_b", "ga_proj_b", "mod_b", "class_emb"):
        parts[n] = cols(g["L0_tok_" + n])
    small = np.concatenate([np.asarray(parts[n]).astype(f) if parts[n].dtype != f else parts[n] for n in SMALL], axis=1)
    im = g["x"][:, :, :84, :84].reshape(B, 3, 2, 3, PATCH, 2, 3, PATCH)
    patches = im.transpose(1, 4, 7, 3, 6, 0, 2, 5).reshape(KC, NP)
    conv = g["L0_tok_conv_w"].reshape(C, KC).T
    conv = np.concatenate([conv, np.zeros((KCT * P - KC, C), f)])
    t = "L0_tok_"
    w_tok = [wt(conv)] + [wt(g[t + n]) for n in ("la_wq", "la_wkv", "la_proj_w", "ga_wq", "ga_wkv", "ga_proj_w", "mod_w")]
    a = "L0_attn_"
    w_mam = [wt(g[a + "W_in"]), wt(g[a + "W_x"]), low(g[a + "W_dt"]), wt(g[a + "W_out"])]
    w_exp = [wt(g["L0_ffn_" + n][i]) for i in range(NE) for n in ("W1", "W3", "W2")]
    w_l2 = [wt(g["L2_attn_" + n]) for n in ("Wq", "Wk", "Wv", "Wr")]
    straight = np.concatenate([np.arange(0, HD1, 2), np.arange(1, HD1, 2)])
    turned = np.concatenate([np.arange(1, HD1, 2), np.arange(0, HD1, 2)])
    heads = np.arange(H16)[:, None] * HD1
    wq, wk, wv = g["L1_attn_wq"].T, g["L1_attn_wk"], g["L1_attn_wv"]
    w_l1 = [wt(wq[:, (heads + straight).reshape(-1)]), wt(wq[:, (heads + turned).reshape(-1)]),
            wt(np.tile(wk[:, straight], (1, 8))), wt(np.tile(wk[:, turned], (1, 8))), wt(np.tile(wv, (1, 8))),
            wt(g["L1_attn_wo"].T)]
    w_f1 = [wt(g["L3_ffn_w1_w"].T), wt(g["L3_ffn_w2_w"].T)]
    n2 = "L2_ffn_"
    w_f3 = [wt(g["L3_ffn_w3_w"].T), wt(g[n2 + "cn_w1"]), wt(g[n2 + "cn_w2"]), g[n2 + "cn_w3"], low(g[n2 + "cn_w4"]),
            wt(g[n2 + "gc_w1"]), g[n2 + "gc_w2"], low(g[n2 + "gc_w3"])]
    b = "L3_attn_"
    w_l3 = [wt(g[b + "Wq"]), wt(g[b + "Wk"]), wt(g[b + "Wv"]), wt(g[b + "Wg"]), wt(g[b + "Wgk1"]), low(g[b + "Wgk2"]),
            wt(g[b + "Wo"])]
    w_fh = [wt(g["L3_ffn_h1_w"].T), wt(g["L3_ffn_h2_w"].T)]
    packed = wt(g["L1_ffn_packed_weight"].reshape(64, C).T)
    side_by_side = {"w_tok": w_tok, "w_mam": w_mam, "w_exp": w_exp, "w_l2": w_l2, "w_l1": w_l1, "w_f1": w_f1,
                    "w_f3": w_f3, "w_l3": w_l3, "w_fh": w_fh}
    arrays = {"small": small, "packed": packed, "patches": patches}
    arrays.update({k: np.concatenate(v, axis=1) for k, v in side_by_side.items()})
    return {k: np.ascontiguousarray(v) for k, v in arrays.items()}


def kernel(**inputs):
    import concourse.bacc as bacc
    from concourse.bass_utils import run_bass_kernel_spmd

    arrays = layout({k: np.asarray(v) for k, v in inputs.items()})
    nc = bacc.Bacc("TRN2", target_bir_lowering=False, num_devices=1)
    args = {k: nc.dram_tensor("in_" + k, v.shape, mybir.dt.from_np(v.dtype), kind="ExternalInput").ap()
            for k, v in arrays.items()}
    out = nc.dram_tensor("out_0", (N, C), F32, kind="ExternalOutput").ap()
    tower(nc, out=out, **args)
    r = run_bass_kernel_spmd(nc, [{"in_" + k: v for k, v in arrays.items()}], core_ids=[0])
    return r.results[0]["out_0"].reshape(B, L, C)
```
